# Optimizing a Trainium2 kernel written in Bass

```python
import numpy as np
import jax
import jax.numpy as jnp

def _softmax(x, axis=-1):
    return jax.nn.softmax(x, axis=axis)

def _gelu(x):
    return jax.nn.gelu(x, approximate=True)

def _silu(x):
    return jax.nn.silu(x)

def _sigmoid(x):
    return jax.nn.sigmoid(x)

def _layernorm(x, axis=-1, eps=1e-05):
    m = jnp.mean(x, axis=axis, keepdims=True)
    v = jnp.var(x, axis=axis, keepdims=True)
    return (x - m) / jnp.sqrt(v + eps)

def _scatter_add(tgt, idx, src, axis=0):
    return tgt.at[idx].add(src)

def _segment_sum(src, seg, n):
    return jax.ops.segment_sum(src, seg, n)
kernel_name = 'mk_adaln_d1_jaxref_r4_e1bc7a'

def setup_inputs(seed: int=0):
    np.random.seed(seed)
    _w = jnp.asarray

    def _L0_attn_setup():
        import jax, jax.numpy as jnp
        import numpy as np
        B, S, HID = (4, 256, 256)
        H, D = (16, 64)
        NEG_INF = -10000000000.0

        def rope_alternate(inputs, position, min_timescale=1.0, max_timescale=10000.0):
            d = inputs.shape[-1]
            half = d // 2
            fraction = 2.0 * jnp.arange(half, dtype=jnp.float32) / d
            timescale = min_timescale * (max_timescale / min_timescale) ** fraction
            sinusoid = position[:, :, None, None] / timescale
            sin, cos = (jnp.sin(sinusoid), jnp.cos(sinusoid))
            first, second = jnp.split(inputs, 2, axis=-1)
            return jnp.concatenate([(first * cos - second * sin).astype(inputs.dtype), (second * cos + first * sin).astype(inputs.dtype)], axis=-1)
        key = jax.random.key(seed)
        k1, k2, k3 = jax.random.split(key, 3)
        x = jax.random.normal(k1, (B, S, HID), dtype=jnp.float32)
        wqkv = jax.random.normal(k2, (HID, 3 * H * D), dtype=jnp.float32) * (1.0 / np.sqrt(HID))
        wo = jax.random.normal(k3, (H * D, HID), dtype=jnp.float32) * (1.0 / np.sqrt(H * D))
        return {'x': x, 'wqkv': wqkv, 'wo': wo}
    _L0_attn_in = _L0_attn_setup()

    def _L0_ffn_setup():
        import jax, jax.numpy as jnp
        import numpy as np
        NUM_EXPERTS = 8
        HIDDEN = 256
        FFN = 1024
        BATCH = 2
        SEQ = 512
        key = jax.random.key(seed)
        k_x, k_g, k_u, k_d = jax.random.split(key, 4)
        scale_in = 1.0 / np.sqrt(HIDDEN)
        scale_mid = 1.0 / np.sqrt(FFN)
        return {'hidden_states': jax.random.normal(k_x, (BATCH, SEQ, HIDDEN), dtype=jnp.float32), 'Wg': jax.random.normal(k_g, (NUM_EXPERTS, HIDDEN, FFN), dtype=jnp.float32) * scale_in, 'Wu': jax.random.normal(k_u, (NUM_EXPERTS, HIDDEN, FFN), dtype=jnp.float32) * scale_in, 'Wd': jax.random.normal(k_d, (NUM_EXPERTS, FFN, HIDDEN), dtype=jnp.float32) * scale_mid}
    _L0_ffn_in = _L0_ffn_setup()
    _L0_c = _w((lambda *s: np.random.randn(*s).astype(np.float32) * 0.05)(8, 256))
    _L0_wmod = _w((lambda *s: np.random.randn(*s).astype(np.float32) * 0.05)(256, 6 * 256) * 256 ** (-0.5))
    _d = {'L0_attn_x': _L0_attn_in['x'], 'L0_attn_wqkv': _L0_attn_in['wqkv'], 'L0_attn_wo': _L0_attn_in['wo'], 'L0_ffn_Wg': _L0_ffn_in['Wg'], 'L0_ffn_Wu': _L0_ffn_in['Wu'], 'L0_ffn_Wd': _L0_ffn_in['Wd'], 'L0_c': _L0_c, 'L0_wmod': _L0_wmod}
    _x0 = _d['L0_attn_x']
    _d['L0_attn_x'] = jax.random.normal(jax.random.fold_in(jax.random.key(seed), 1), (8, 512, 256), dtype=_x0.dtype)
    del _x0
    return _d

def reference(L0_attn_x, L0_attn_wqkv, L0_attn_wo, L0_ffn_Wg, L0_ffn_Wu, L0_ffn_Wd, L0_c, L0_wmod):

    def _L0_attn_ref(x, wqkv, wo):
        import jax, jax.numpy as jnp
        import numpy as np
        B, S, HID = (4, 256, 256)
        H, D = (16, 64)
        NEG_INF = -10000000000.0

        def rope_alternate(inputs, position, min_timescale=1.0, max_timescale=10000.0):
            d = inputs.shape[-1]
            half = d // 2
            fraction = 2.0 * jnp.arange(half, dtype=jnp.float32) / d
            timescale = min_timescale * (max_timescale / min_timescale) ** fraction
            sinusoid = position[:, :, None, None] / timescale
            sin, cos = (jnp.sin(sinusoid), jnp.cos(sinusoid))
            first, second = jnp.split(inputs, 2, axis=-1)
            return jnp.concatenate([(first * cos - second * sin).astype(inputs.dtype), (second * cos + first * sin).astype(inputs.dtype)], axis=-1)
        b, s, _ = x.shape
        qkv = jnp.einsum('bsh,hf->bsf', x, wqkv).reshape(b, s, 3, H, D)
        q, k, v = (qkv[:, :, 0], qkv[:, :, 1], qkv[:, :, 2])
        pos = jnp.broadcast_to(jnp.arange(s, dtype=jnp.float32)[None, :], (b, s))
        q = rope_alternate(q, pos)
        k = rope_alternate(k, pos)
        q = q / jnp.sqrt(jnp.float32(D)).astype(q.dtype)
        logits = jnp.einsum('bqhd,bkhd->bhqk', q, k)
        causal = jnp.where(jnp.tril(jnp.ones((s, s), dtype=bool))[None, None], 0.0, NEG_INF).astype(logits.dtype)
        probs = jax.nn.softmax(logits + causal, axis=-1)
        ctx = jnp.einsum('bhqk,bkhd->bqhd', probs, v).reshape(b, s, H * D)
        return jnp.einsum('bsf,fh->bsh', ctx, wo)

    def _L0_ffn_ref(hidden_states, Wg, Wu, Wd):
        import jax, jax.numpy as jnp
        import numpy as np
        NUM_EXPERTS = 8
        HIDDEN = 256
        FFN = 1024
        BATCH = 2
        SEQ = 512
        B, S, H = hidden_states.shape
        x = hidden_states.reshape(-1, H)

        def expert_step(acc, w):
            wg, wu, wd = w
            h = jax.nn.silu(x @ wg) * (x @ wu)
            return (acc + h @ wd, None)
        acc, _ = jax.lax.scan(expert_step, jnp.zeros_like(x), (Wg, Wu, Wd))
        return acc.reshape(B, S, H)
    x = L0_attn_x
    mod = (_silu(L0_c) @ L0_wmod).reshape(L0_c.shape[0], 6, 1, -1)
    sa, ca, ga, sb, cb, gb = (mod[:, 0], mod[:, 1], mod[:, 2], mod[:, 3], mod[:, 4], mod[:, 5])
    ga = (2 * (ga >= 0) - 1) * jnp.maximum(jnp.abs(ga), 0.25)
    gb = (2 * (gb >= 0) - 1) * jnp.maximum(jnp.abs(gb), 0.25)
    h = _layernorm(x, axis=-1) * (1 + ca) + sa
    x = x + ga * _L0_attn_ref(h, L0_attn_wqkv, L0_attn_wo)
    h = _layernorm(x, axis=-1) * (1 + cb) + sb
    x = x + gb * _L0_ffn_ref(h, L0_ffn_Wg, L0_ffn_Wu, L0_ffn_Wd)
    return x

_drawn_inputs = setup_inputs


def setup_inputs(seed=0):
    import zlib

    import numpy as np

    out = dict(_drawn_inputs(seed))
    spreads = {}
    factors = {}
    for name, (base, spread) in spreads.items():
        noise = np.random.default_rng([zlib.crc32(name.encode()), seed]).standard_normal(out[name].shape)
        drawn = base * np.exp(spread * noise) if base else spread * noise
        out[name] = jnp.asarray(drawn.astype(out[name].dtype))
    for name, factor in factors.items():
        out[name] = (out[name] * factor).astype(out[name].dtype)
    return out
```

```python
import concourse.bass as bass
from concourse import mybir
from contextlib import ExitStack

F32 = mybir.dt.float32
F16 = mybir.dt.float16
I32 = mybir.dt.int32
ACT = mybir.ActivationFunctionType
ALU = mybir.AluOpType
AX = mybir.AxisListType

P = 128
B = 8
S = 512
C = 256
H = 16
D = 64
E = 8
F = 1024
KC = C // P
TT = S // P
G = 4
HG = H // G
CC = H * D // P
FC = F // P
EPS = 1e-5

TINY = 1e-30
EXPONENT = 0x7F800000
H_SCALE = 2.0 ** 13
W_SCALE = 2.0 ** 9
O_SCALE = 2.0 ** 14
QK_SHIFT = 2.0 ** -17
V_SHIFT = 2.0 ** -13
MAX_UNIT = 2.0 ** 15
LOGIT_SCALE = (1.0 / 8.0) / (H_SCALE * W_SCALE * QK_SHIFT) ** 2
ATTN_UNSCALE = 1.0 / (H_SCALE * W_SCALE * V_SHIFT * O_SCALE)
SILU_UNSCALE = 1.0 / (H_SCALE * W_SCALE)
MID_SHIFT = 2.0 ** -19
DOWN_UNSCALE = 1.0 / (H_SCALE * W_SCALE * MID_SHIFT * O_SCALE)

WOFF = [0, 512, 896, 1152]
PW = 1280
MASKED = -2.0 ** 15


def flat(ap):
    return ap.rearrange("p a n -> p (a n)")


def three_passes(nc, out, stationary, moving, first, last):
    s, m = stationary, moving
    nc.tensor.matmul(out, s[0], m[0], start=first, stop=False)
    nc.tensor.matmul(out, s[0], m[1], start=False, stop=False)
    return nc.tensor.matmul(out, s[1], m[0], start=False, stop=last)


def normalise_chunk(nc, dve, tiles, ps, which, b, k, n, h32_done, hhi_done, hlo_done):
    hT_hi, hT_lo, h32, ln_mul, ln_add = tiles
    hi = flat(hT_hi[:, bass.ds(b, 1), k, :])
    lo = flat(hT_lo[:, bass.ds(b, 1), k, :])
    nc.vector.tensor_scalar(h32[:, k], ps, ln_mul[:, which, k, bass.ds(b, 1)], ln_add[:, which, k, bass.ds(b, 1)],
                            ALU.mult, ALU.add).then_inc(h32_done, 1)
    dve.wait_ge(h32_done, n + 1)
    nc.vector.tensor_copy(hi, h32[:, k]).then_inc(hhi_done, 1)
    dve.wait_ge(hhi_done, n + 1)
    nc.vector.tensor_tensor(lo, h32[:, k], hi, ALU.subtract).then_inc(hlo_done, 1)


def adaln_block_kernel(nc, x, wqkv, wo, wg, wu, wd, cT, wmod, cosT, sinT, out, x1_dram, rows_dram):
    ctx = ExitStack()
    with ctx:
        def sb(stack, name, shape, dt=F32):
            return stack.enter_context(nc.sbuf_tensor(name, shape, dt))

        def sem(stack, name):
            return stack.enter_context(nc.semaphore(name))

        bank = [ctx.enter_context(nc.psum_tensor(f"bank{i}", [P, 512], F32)) for i in range(8)]

        hT_hi = sb(ctx, "hT_hi", [P, B + 1, KC, S], F16)
        hT_lo = sb(ctx, "hT_lo", [P, B + 1, KC, S], F16)
        modT = sb(ctx, "modT", [P, 12, B])
        ln_mul = sb(ctx, "ln_mul", [P, 2, KC, B])
        ln_add = sb(ctx, "ln_add", [P, 2, KC, B])
        gate = sb(ctx, "gate", [P, 2, KC, B])
        pow2 = sb(ctx, "pow2", [P, 4])
        ipow2 = sb(ctx, "ipow2", [P, 4])
        logit_scale = sb(ctx, "logit_scale", [P, 1])
        ph2sq = sb(ctx, "ph2sq", [P, 1])
        ident32 = sb(ctx, "ident32", [P, P])
        neg_half = sb(ctx, "neg_half", [P, 4 * B])
        h32 = sb(ctx, "h32", [P, 2, S])
        xhat = sb(ctx, "xhat", [P, TT, C])
        mean_var = sb(ctx, "mean_var", [P, TT * B, 2])
        var_eps = sb(ctx, "var_eps", [P, TT * B])
        rstd = sb(ctx, "rstd", [P, TT * B])

        norm_tiles = (hT_hi, hT_lo, h32, ln_mul, ln_add)
        attn = ctx.enter_context(ExitStack())
        wqkv_hi = sb(attn, "wqkv_hi", [P, KC, G, 6 * P], F16)
        wqkv_lo = sb(attn, "wqkv_lo", [P, KC, G, 6 * P], F16)
        wo_hi = sb(attn, "wo_hi", [P, CC, C], F16)
        wo_lo = sb(attn, "wo_lo", [P, CC, C], F16)
        cos_t = sb(attn, "cos_t", [P, S])
        sin_t = sb(attn, "sin_t", [P, S])
        max_mask = sb(attn, "max_mask", [P, P], F16)
        ident_unit = sb(attn, "ident_unit", [P, P], F16)
        ident16 = sb(attn, "ident16", [P, P], F16)
        ones15 = sb(attn, "ones15", [P, P], F16)

        with ExitStack() as st:
            x_all = sb(st, "x_all", [P, B * TT, C])
            wqkv_f = sb(st, "wqkv_f", [P, KC * G * 6 * P])
            wo_f = sb(st, "wo_f", [P, CC * C])
            wmod_f = sb(st, "wmod_f", [P, KC, 6 * C])
            c_f = sb(st, "c_f", [P, KC, B])
            c_silu = sb(st, "c_silu", [P, KC, B])
            stats = sb(st, "stats", [P, B * TT, 6])
            one_c = sb(st, "one_c", [P, 2, KC, B])
            amax = sb(st, "amax", [P, 6])
            amax_all = sb(st, "amax_all", [P, 6])
            bound = sb(st, "bound", [P, 4])
            alpha = sb(st, "alpha", [P, 4])
            tmp = sb(st, "tmp", [P, 2, KC, B])
            tmp1 = sb(st, "tmp1", [P, 1])

            x_in, w_in, wo_in, c_in, table_in = (sem(st, n) for n in ("x_in", "w_in", "wo_in", "c_in", "table_in"))
            silu_done, mod_full, amax_done, amax_reduced, chain, bn_done = (
                sem(st, n) for n in ("silu_done", "mod_full", "amax_done", "amax_reduced", "chain", "bn_done"))
            var_done, rstd_done, alpha_done, wq_hi_done, wo_hi_done = (
                sem(st, n) for n in ("var_done", "rstd_done", "alpha_done", "wq_hi_done", "wo_hi_done"))
            const_pool, xhat_done, tr_full, h32_done, hhi_done, hlo_done = (
                sem(st, n) for n in ("const_pool", "xhat_done", "tr_full", "h32_done", "hhi_done", "hlo_done"))

            with nc.Block() as block:
                @block.sync
                def _(sp):
                    sp.dma_start(c_f[:], cT).then_inc(c_in, 16)
                    sp.dma_start(wmod_f[:], wmod.rearrange("(k p) n -> p k n", p=P)).then_inc(c_in, 16)
                    for b in range(B):
                        sp.dma_start(x_all[:, b * TT:(b + 1) * TT, :],
                                     x.rearrange("(n p) c -> p n c", p=P)[:, b * TT:(b + 1) * TT, :]).then_inc(x_in, 16)
                    sp.dma_start(wqkv_f[:], wqkv).then_inc(w_in, 16)
                    sp.dma_start(wo_f[:].rearrange("p (c n) -> p c n", n=C),
                                 wo.rearrange("(c p) n -> p c n", p=P)).then_inc(wo_in, 16)
                    sp.dma_start(cos_t[:], cosT).then_inc(table_in, 16)
                    sp.dma_start(sin_t[:], sinT).then_inc(table_in, 16)
                    sp.wait_ge(table_in, 32)

                @block.gpsimd
                def _(pool):
                    step = [0]

                    def link(ins):
                        step[0] += 1
                        ins.then_inc(const_pool, 1)
                        pool.wait_ge(const_pool, step[0])

                    link(nc.gpsimd.memset(ident32[:], 0.0))
                    link(nc.gpsimd.affine_select(out=ident32[:], in_=ident32[:], pattern=[[-1, P]],
                                                 compare_op=ALU.not_equal, fill=1.0, base=0, channel_multiplier=1))
                    link(nc.gpsimd.memset(ident16[:], 0.0))
                    link(nc.gpsimd.affine_select(out=ident16[:], in_=ident16[:], pattern=[[-1, P]],
                                                 compare_op=ALU.not_equal, fill=1.0, base=0, channel_multiplier=1))
                    link(nc.gpsimd.memset(ident_unit[:], 0.0))
                    link(nc.gpsimd.affine_select(out=ident_unit[:], in_=ident_unit[:], pattern=[[-1, P]],
                                                 compare_op=ALU.not_equal, fill=MAX_UNIT, base=0, channel_multiplier=1))
                    link(nc.gpsimd.memset(max_mask[:], 0.0))
                    link(nc.gpsimd.affine_select(out=max_mask[:], in_=max_mask[:],
                                                 pattern=[[-1, P]], compare_op=ALU.is_ge, fill=MASKED,
                                                 base=0, channel_multiplier=1))
                    link(nc.gpsimd.memset(ones15[:], MAX_UNIT))
                    link(nc.gpsimd.memset(neg_half[:], -0.5))
                    link(nc.gpsimd.memset(hT_hi[:, B, :, :], 0.0))
                    link(nc.gpsimd.memset(hT_lo[:, B, :, :], 0.0))
                    pool.wait_ge(var_done, 1)
                    nc.gpsimd.tensor_tensor(rstd[:], var_eps[:], neg_half[:], ALU.pow).then_inc(rstd_done, 1)
                    pool.wait_ge(amax_done, 6)
                    nc.gpsimd.partition_all_reduce(amax_all[:], amax[:], P, bass.bass_isa.ReduceOp.max).then_inc(amax_reduced, 1)

                @block.scalar
                def _(act):
                    act.wait_ge(c_in, 32)
                    nc.scalar.activation(c_silu[:], c_f[:], ACT.Silu).then_inc(silu_done, 1)
                    act.wait_ge(alpha_done, 1)
                    act.wait_ge(w_in, 16)
                    nc.scalar.activation(flat(wqkv_hi[:].rearrange("p k g n -> p k (g n)")), wqkv_f[:], ACT.Copy,
                                         scale=alpha[:, 2:3]).then_inc(wq_hi_done, 1)
                    act.wait_ge(wo_in, 16)
                    nc.scalar.activation(flat(wo_hi[:]), wo_f[:], ACT.Copy, scale=alpha[:, 3:4]).then_inc(wo_hi_done, 1)

                @block.tensor
                def _(pe):
                    pe.wait_ge(silu_done, 1)
                    for m in range(12):
                        for k in range(KC):
                            last = nc.tensor.matmul(bank[0][:, m * B:(m + 1) * B], wmod_f[:, k, m * P:(m + 1) * P],
                                                    c_silu[:, k, :], start=(k == 0), stop=(k == KC - 1))
                    last.then_inc(mod_full, 1)
                    pe.wait_ge(const_pool, 2)
                    with pe.Fori(0, B) as b:
                        pe.wait_ge(xhat_done, b + 1)
                        for k in range(KC):
                            for t in range(TT):
                                last = nc.tensor.transpose(bank[6 + k][:, t * P:(t + 1) * P],
                                                           xhat[:, t, k * P:(k + 1) * P], ident32[:])
                            last.then_inc(tr_full, 1)

                @block.vector
                def _(dve):
                    step = [0]

                    def link(ins):
                        step[0] += 1
                        ins.then_inc(chain, 1)
                        dve.wait_ge(chain, step[0])

                    dve.wait_ge(mod_full, 1)
                    link(nc.vector.tensor_copy(modT[:].rearrange("p m b -> p (m b)"), bank[0][:, 0:12 * B]))
                    m = modT[:].rearrange("p (l r k) b -> p l r k b", l=2, r=3)
                    link(nc.vector.tensor_scalar(one_c[:], m[:, :, 1], 1.0, None, ALU.add))
                    for i in range(2):
                        nc.vector.tensor_reduce(amax[:, 2 + 2 * i:3 + 2 * i], one_c[:, i], AX.XY, ALU.max,
                                                apply_absolute_value=True).then_inc(amax_done, 1)
                        nc.vector.tensor_reduce(amax[:, 3 + 2 * i:4 + 2 * i], m[:, i, 0], AX.XY, ALU.max,
                                                apply_absolute_value=True).then_inc(amax_done, 1)
                    dve.wait_ge(x_in, 16 * B)
                    with dve.Fori(0, B * TT) as t:
                        nc.vector.bn_stats(flat(stats[:, bass.ds(t, 1), :]), flat(x_all[:, bass.ds(t, 1), :])).then_inc(bn_done, 1)
                    dve.wait_ge(bn_done, B * TT)
                    for t in range(B * TT):
                        nc.vector.bn_aggr(mean_var[:, t, :], stats[:, t, :]).then_inc(bn_done, 1)
                    dve.wait_ge(bn_done, 2 * B * TT)
                    nc.vector.tensor_scalar(var_eps[:], mean_var[:, :, 1], EPS, None, ALU.add).then_inc(var_done, 1)
                    dve.wait_ge(w_in, 16)
                    nc.vector.tensor_reduce(amax[:, 0:1], wqkv_f[:], AX.X, ALU.max,
                                            apply_absolute_value=True).then_inc(amax_done, 1)
                    dve.wait_ge(wo_in, 16)
                    nc.vector.tensor_reduce(amax[:, 1:2], wo_f[:], AX.X, ALU.max,
                                            apply_absolute_value=True).then_inc(amax_done, 1)
                    dve.wait_ge(amax_reduced, 1)
                    for i in range(2):
                        link(nc.vector.tensor_scalar(bound[:, i:i + 1], amax_all[:, 2 + 2 * i:3 + 2 * i],
                                                     amax_all[:, 3 + 2 * i:4 + 2 * i], 16.0, ALU.add, ALU.mult))
                    link(nc.vector.tensor_copy(bound[:, 2:4], amax_all[:, 0:2]))
                    link(nc.vector.tensor_scalar(bound[:], bound[:], TINY, None, ALU.max))
                    link(nc.vector.tensor_scalar(pow2[:].bitcast(I32), bound[:].bitcast(I32), EXPONENT, None, ALU.bitwise_and))
                    link(nc.vector.reciprocal(ipow2[:], pow2[:]))
                    for i, s in enumerate((H_SCALE, H_SCALE, W_SCALE, O_SCALE)):
                        ins = nc.vector.tensor_scalar(alpha[:, i:i + 1], ipow2[:, i:i + 1], s, None, ALU.mult)
                        link(ins)
                    nc.vector.tensor_scalar(tmp1[:], pow2[:, 0:1], pow2[:, 2:3], None, ALU.mult).then_inc(alpha_done, 1)
                    dve.wait_ge(alpha_done, 1)
                    link(nc.vector.tensor_scalar(logit_scale[:], tmp1[:], tmp1[:], LOGIT_SCALE, ALU.mult, ALU.mult))
                    link(nc.vector.tensor_scalar(ph2sq[:], pow2[:, 1:2], pow2[:, 1:2], None, ALU.mult))
                    for i in range(2):
                        link(nc.vector.tensor_scalar(ln_mul[:, i], one_c[:, i], alpha[:, i:i + 1], None, ALU.mult))
                        link(nc.vector.tensor_scalar(ln_add[:, i], m[:, i, 0], alpha[:, i:i + 1], None, ALU.mult))
                    g = m[:, :, 2]
                    link(nc.vector.tensor_scalar(tmp[:], g, 0.0, 2.0, ALU.is_ge, ALU.mult))
                    link(nc.vector.tensor_scalar(tmp[:], tmp[:], -1.0, None, ALU.add))
                    link(nc.vector.scalar_tensor_tensor(gate[:].rearrange("p l k b -> p l (k b)"),
                                                        g.rearrange("p l k b -> p l (k b)"), -1.0,
                                                        g.rearrange("p l k b -> p l (k b)"), ALU.mult, ALU.max))
                    link(nc.vector.tensor_scalar(gate[:], gate[:], 0.25, None, ALU.max))
                    link(nc.vector.tensor_tensor(gate[:], gate[:], tmp[:], ALU.mult))
                    link(nc.vector.tensor_scalar(tmp1[:], tmp1[:], pow2[:, 3:4], ATTN_UNSCALE, ALU.mult, ALU.mult))
                    link(nc.vector.tensor_scalar(gate[:, 0], gate[:, 0], tmp1[:], None, ALU.mult))
                    dve.wait_ge(wq_hi_done, 1)
                    nc.vector.scalar_tensor_tensor(flat(wqkv_lo[:].rearrange("p k g n -> p k (g n)")), wqkv_f[:],
                                                   alpha[:, 2:3], flat(wqkv_hi[:].rearrange("p k g n -> p k (g n)")),
                                                   ALU.mult, ALU.subtract)
                    dve.wait_ge(wo_hi_done, 1)
                    nc.vector.scalar_tensor_tensor(flat(wo_lo[:]), wo_f[:], alpha[:, 3:4], flat(wo_hi[:]),
                                                   ALU.mult, ALU.subtract)
                    dve.wait_ge(rstd_done, 1)
                    with dve.Fori(0, B) as b:
                        for t in range(TT):
                            n = b * TT + t
                            last = nc.vector.tensor_scalar(
                                xhat[:, t, :], flat(x_all[:, bass.ds(n, 1), :]), flat(mean_var[:, bass.ds(n, 1), 0:1]),
                                rstd[:, bass.ds(n, 1)], ALU.subtract, ALU.mult)
                        last.then_inc(xhat_done, 1)
                        for k in range(KC):
                            dve.wait_ge(tr_full, b * KC + k + 1)
                            normalise_chunk(nc, dve, norm_tiles, bank[6 + k][:], 0, b, k, b * KC + k, h32_done, hhi_done, hlo_done)

        with ExitStack() as st:
            k_stack = sb(st, "k_stack", [P, 2, HG, S], F16)
            q_stack = sb(st, "q_stack", [P, 2, HG, 2, S], F16)
            rot_part = sb(st, "rot_part", [P, 4, S])
            rot = sb(st, "rot", [P, 2, S])
            qk_split = sb(st, "qk_split", [P, 2, 2, 2, S], F16)
            v_hi = sb(st, "v_hi", [P, 2, TT * HG, P], F16)
            v_lo = sb(st, "v_lo", [P, 2, TT * HG, P], F16)
            spare = sb(st, "spare", [P, 4], F16)
            row_max = sb(st, "row_max", [P, 2, TT])
            neg_max = sb(st, "neg_max", [P, 2, S], F16)
            p32 = sb(st, "p32", [P, 2, PW])
            p_hi = sb(st, "p_hi", [P, 2, PW], F16)
            p_lo = sb(st, "p_lo", [P, 2, PW], F16)
            recip = sb(st, "recip", [P, S])
            ctx32 = sb(st, "ctx32", [P, S])
            ctx_hi = sb(st, "ctx_hi", [P, CC, S], F16)
            ctx_lo = sb(st, "ctx_lo", [P, CC, S], F16)
            attn_T = sb(st, "attn_T", [P, KC, S])
            x_t = sb(st, "x_t", [P, TT, C])
            x1_t = sb(st, "x1_t", [P, TT, C])
            stats = sb(st, "stats_b", [P, TT, 6])

            names = """pair_full pair_free rope_mul rope_sum rope_hi rope_lo q_stacked k_stacked v_ready v_hi_done v_lo_done
                s_full max_done diag_done st_full exp_done mask_done phi_done plo_done pv_full recip_done ctx_done
                ctx_part ctx_split attn_scaled x_loaded x1_done x1_stored bn_done2 agg_done var_done2 rstd_done2 xhat_done2
                h32_done2 hhi_done2 hlo_done2""".split()
            (pair_full, pair_free, rope_mul, rope_sum, rope_hi, rope_lo, q_stacked, k_stacked, v_ready, v_hi_done, v_lo_done,
             s_full, max_done, diag_done, st_full, exp_done, mask_done, phi_done, plo_done, pv_full, recip_done, ctx_done,
             ctx_part, ctx_split, attn_scaled, x_loaded, x1_done, x1_stored, bn_done, agg_done, var_done, rstd_done, xhat_done,
             h32_done, hhi_done, hlo_done) = (sem(st, n) for n in names)
            rows_out = (sem(st, "q_rows_out"), sem(st, "k_rows_out"))

            PAIR_FIRST, PAIR_USES = 3, 15
            Q, K, V = 0, 1, 2
            Q_DMAS, K_DMAS = 4, 4
            pair = (bank[6], bank[7])

            def value_part(v, par, half, eo):
                tiles = v[:, par, 2 * HG * half:2 * HG * (half + 1), :].rearrange("p (j two) n -> p j two n", two=2)
                return tiles[:, :, eo, eo * D:(eo + 1) * D]

            def value_source(half, eo):
                return pair[half][:].rearrange("p (j two n) -> p j two n", two=2, n=D)[:, :, eo, :]

            def turn(b, n, what):
                return PAIR_FIRST + PAIR_USES * b + 3 * (n - 1) + what

            def rope_turn(b, n, what):
                return 2 + 2 * G * b + 2 * (n - 1) + what

            with nc.Block() as block:
                @block.sync
                def _(sp):
                    x_v = x.rearrange("(n p) c -> p n c", p=P)
                    x1_v = x1_dram.rearrange("(n p) c -> p n c", p=P)

                    def stack(what, par, r, uses):
                        there = rows_dram[what].rearrange("h p l t -> p h l t")
                        sp.wait_ge(rope_lo, r + 1)
                        sp.dma_start(there, qk_split[:, what]).then_inc(rows_out[what], 16)
                        sp.wait_ge(rows_out[what], 16 * uses + 16)
                        for quad in range(4):
                            half = rows_dram[what, quad % 2].rearrange("(i d) l t -> d i l t", i=HG)
                            to = slice(32 * quad, 32 * quad + 32)
                            if what == Q:
                                sp.dma_start(q_stack[to, par], half).then_inc(q_stacked, 16)
                            else:
                                sp.dma_start(k_stack[to, par], half[:, :, quad // 2]).then_inc(k_stacked, 16)

                    stack(Q, 0, 0, 0)
                    stack(K, 0, 1, 0)
                    sp.dma_start(x_t[:], x_v[:, 0:TT, :]).then_inc(x_loaded, 16)
                    with sp.Fori(0, B) as b:
                        for n in range(1, G + 1):
                            stack(Q, n % 2, rope_turn(b, n, Q), G * b + n)
                            stack(K, n % 2, rope_turn(b, n, K), G * b + n)
                        sp.wait_ge(x1_done, b + 1)
                        sp.dma_start(x1_v[:, bass.ds(b * TT, TT), :], x1_t[:]).then_inc(x1_stored, 16)
                        sp.wait_ge(x1_stored, 16 * b + 16)
                        sp.dma_start(x_t[:], x_v[:, bass.ds((b + 1) % B * TT, TT), :]).then_inc(x_loaded, 16)
                    sp.wait_ge(x_loaded, 16 * (B + 1))

                @block.tensor
                def _(pe):
                    def proj(b, g, what, t):
                        if isinstance(t, int):
                            if t >= 1:
                                pe.wait_ge(pair_free, t)
                        else:
                            pe.wait_ge(pair_free, t)
                        if what in (Q, K):
                            for half in range(2):
                                for k in range(KC):
                                    h = (flat(hT_hi[:, bass.ds(b, 1), k, :]), flat(hT_lo[:, bass.ds(b, 1), k, :]))
                                    cols = slice((2 * what + half) * P, (2 * what + half + 1) * P)
                                    w = (wqkv_hi[:, k, g, cols], wqkv_lo[:, k, g, cols])
                                    last = three_passes(nc, pair[half][:], w, h, k == 0, k == KC - 1)
                        else:
                            for tt in range(TT):
                                for k in range(KC):
                                    rows = slice(tt * P, (tt + 1) * P)
                                    h = (flat(hT_hi[:, bass.ds(b, 1), k, rows]), flat(hT_lo[:, bass.ds(b, 1), k, rows]))
                                    w = (wqkv_hi[:, k, g, 4 * P:], wqkv_lo[:, k, g, 4 * P:])
                                    last = three_passes(nc, pair[tt // 2][:, (tt % 2) * C:(tt % 2 + 1) * C], h, w,
                                                        k == 0, k == KC - 1)
                        last.then_inc(pair_full, 1)

                    def scores_qk(b, h):
                        par, i, g = (h // HG) % 2, h % HG, h // HG
                        if i == 0:
                            pe.wait_ge(q_stacked, Q_DMAS * 16 * (1 + G * b + g))
                            pe.wait_ge(k_stacked, K_DMAS * 16 * (1 + G * b + g))
                        for qt in range(TT):
                            pe.wait_ge(max_done, TT * (H * b + h) + qt + 1)
                            nc.tensor.matmul(bank[qt % 2][:, 0:(qt + 1) * P], q_stack[:, par, i, 0, qt * P:(qt + 1) * P],
                                             k_stack[:, par, i, 0:(qt + 1) * P], start=True, stop=False)
                            nc.tensor.matmul(bank[qt % 2][:, qt * P:(qt + 1) * P], ident_unit[:], max_mask[:],
                                             start=False, stop=True).then_inc(s_full, 1)

                    def scores_kq(b, h):
                        par, i = (h // HG) % 2, h % HG
                        hh = H * b + h
                        for kt in range(TT):
                            to = bank[2 + min(kt, 2)][:, (2 * P if kt == 3 else 0):(2 * P if kt == 3 else 0) + S - kt * P]
                            rows = slice(kt * P, (kt + 1) * P)
                            if kt < 3:
                                pe.wait_ge(exp_done, 3 * hh + kt + 1)
                            if kt == 0:
                                pe.wait_ge(diag_done, hh + 1)
                            nc.tensor.matmul(to, k_stack[:, par, i, rows], q_stack[:, par, i, 0, kt * P:], start=True, stop=False)
                            nc.tensor.matmul(to, k_stack[:, par, i, rows], q_stack[:, par, i, 1, kt * P:], start=False, stop=False)
                            last = nc.tensor.matmul(to, ones15[:], neg_max[:, h % 2, kt * P:], start=False, stop=True)
                            if kt != 2:
                                last.then_inc(st_full, 1)

                    def context(b, h):
                        par, i = (h // HG) % 2, h % HG
                        hh = H * b + h
                        pe.wait_ge(plo_done, hh + 3)
                        if i == 0:
                            pe.wait_ge(v_lo_done, G * b + h // HG + 1)
                        if h > 0:
                            pe.wait_ge(ctx_done, hh)
                        for kt in range(TT):
                            cols = slice(WOFF[kt], WOFF[kt] + S - kt * P)
                            v = (v_hi[:, par, kt * HG + i, :], v_lo[:, par, kt * HG + i, :])
                            last = three_passes(nc, bank[5][:, kt * P:], v, (p_hi[:, h % 2, cols], p_lo[:, h % 2, cols]),
                                                kt == 0, kt == TT - 1)
                        last.then_inc(pv_full, 1)

                    for what in (Q, K, V):
                        proj(0, 0, what, what)
                    with pe.Fori(0, B) as b:
                        scores_qk(b, 0)
                        for h in range(H):
                            if h + 1 < H:
                                scores_qk(b, h + 1)
                            scores_kq(b, h)
                            if h >= 2:
                                context(b, h - 2)
                            n, what = h // HG + 1, h % HG
                            if n < G and what < 3:
                                proj(b, n, what, turn(b, n, what))
                        proj(b + 1, 0, Q, turn(b, G, Q))
                        context(b, H - 2)
                        proj(b + 1, 0, K, turn(b, G, K))
                        proj(b + 1, 0, V, turn(b, G, V))
                        context(b, H - 1)
                        t = PAIR_FIRST + PAIR_USES * b + 12
                        pe.wait_ge(pair_free, t)
                        for o in range(KC):
                            for c in range(CC):
                                if c == CC - 1:
                                    pe.wait_ge(ctx_split, CC * b + CC)
                                elif o == 0:
                                    pe.wait_ge(ctx_split, CC * b + c + 1)
                                cols = slice(o * P, (o + 1) * P)
                                last = three_passes(nc, pair[o][:], (wo_hi[:, c, cols], wo_lo[:, c, cols]),
                                                    (ctx_hi[:, c, :], ctx_lo[:, c, :]), c == 0, c == CC - 1)
                        last.then_inc(pair_full, 1)
                        pe.wait_ge(attn_scaled, b + 1)
                        pe.wait_ge(pair_free, t + 1)
                        for tt in range(TT):
                            for o in range(KC):
                                at = (tt % 2) * C + o * P
                                last = nc.tensor.transpose(pair[tt // 2][:, at:at + P], attn_T[:, o, tt * P:(tt + 1) * P], ident32[:])
                        last.then_inc(pair_full, 1)
                        pe.wait_ge(xhat_done, b + 1)
                        pe.wait_ge(pair_free, t + 2)
                        for k in range(KC):
                            for tt in range(TT):
                                last = nc.tensor.transpose(pair[k][:, tt * P:(tt + 1) * P], xhat[:, tt, k * P:(k + 1) * P], ident32[:])
                        last.then_inc(pair_full, 1)

                @block.vector
                def _(dve):
                    def maxima(b, h):
                        hh = H * b + h
                        for qt in range(TT):
                            w = (qt + 1) * P
                            dve.wait_ge(s_full, TT * hh + qt + 1)
                            nc.vector.tensor_reduce(row_max[:, h % 2, qt:qt + 1], bank[qt % 2][:, 0:w], AX.X,
                                                    ALU.max).then_inc(max_done, 1)
                        for qt in range(TT):
                            dve.wait_ge(max_done, TT * hh + qt + 3)
                            last = nc.vector.tensor_scalar(neg_max[:, h % 2, qt * P:(qt + 1) * P], ident16[:],
                                                           row_max[:, h % 2, qt:qt + 1], -1.0 / MAX_UNIT, ALU.mult, ALU.mult)
                        last.then_inc(diag_done, 1)

                    def rotate(r, t, wait_sum):
                        dve.wait_ge(pair_full, t + 1)
                        if wait_sum:
                            dve.wait_ge(rope_sum, r)
                        nc.vector.tensor_tensor(rot_part[:, 0, :], pair[0][:], cos_t[:], ALU.mult)
                        nc.vector.tensor_tensor(rot_part[:, 3, :], pair[0][:], sin_t[:], ALU.mult)
                        nc.vector.tensor_tensor(rot_part[:, 1, :], pair[1][:], sin_t[:], ALU.mult)
                        nc.vector.tensor_tensor(rot_part[:, 2, :], pair[1][:], cos_t[:], ALU.mult).then_inc(rope_mul, 1)
                        dve.wait_ge(rope_mul, r + 1)
                        nc.vector.tensor_copy(spare[:, 0:2], ident16[:, 0:2]).then_inc(pair_free, 1)

                    def rotated_lo(r, what):
                        dve.wait_ge(rope_hi, r + 1)
                        nc.vector.tensor_tensor(qk_split[:, what, :, 1, :], rot[:], qk_split[:, what, :, 0, :], ALU.subtract).then_inc(rope_lo, 1)

                    def values_lo(n, par, t):
                        dve.wait_ge(v_hi_done, n + 1)
                        for half in range(2):
                            for eo in range(2):
                                to, of = (value_part(v, par, half, eo) for v in (v_lo, v_hi))
                                last = nc.vector.scalar_tensor_tensor(to, value_source(half, eo), V_SHIFT, of, ALU.mult, ALU.subtract)
                        last.then_inc(v_lo_done, 1)
                        dve.wait_ge(v_lo_done, n + 1)
                        nc.vector.tensor_copy(spare[:, 0:2], ident16[:, 0:2]).then_inc(pair_free, 1)

                    def finish_context(b, h):
                        hh = H * b + h
                        mine, sums = (slice(0, D), slice(D, P)) if h % 2 == 0 else (slice(D, P), slice(0, D))
                        dve.wait_ge(pv_full, hh + 1)
                        nc.vector.reciprocal(recip[mine, :], bank[5][sums, :]).then_inc(recip_done, 1)
                        dve.wait_ge(recip_done, hh + 1)
                        nc.vector.tensor_tensor(ctx32[mine, :], bank[5][mine, :], recip[mine, :], ALU.mult).then_inc(ctx_done, 1)
                        if h % 2 == 1:
                            dve.wait_ge(ctx_done, hh + 1)
                            nc.vector.tensor_copy(ctx_hi[:, h // 2, :], ctx32[:]).then_inc(ctx_part, 1)
                            dve.wait_ge(ctx_part, CC * b + h // 2 + 1)
                            nc.vector.tensor_tensor(ctx_lo[:, h // 2, :], ctx32[:], ctx_hi[:, h // 2, :], ALU.subtract).then_inc(ctx_split, 1)

                    nc.vector.memset(spare[:], 0.0).then_inc(max_done, 2)
                    rotate(0, 0, False)
                    rotated_lo(0, Q)
                    rotate(1, 1, True)
                    rotated_lo(1, K)
                    dve.wait_ge(v_ready, 2)
                    values_lo(0, 0, 2)
                    with dve.Fori(0, B) as b:
                        maxima(b, 0)
                        for h in range(H):
                            if h + 1 < H:
                                maxima(b, h + 1)
                            n, what = h // HG + 1, h % HG
                            if n < G and what < 2:
                                rotate(rope_turn(b, n, what), turn(b, n, what), True)
                            if h >= 2:
                                finish_context(b, h - 2)
                            if n < G and what in (1, 2):
                                rotated_lo(rope_turn(b, n, what - 1), what - 1)
                            if n < G and what == 3:
                                values_lo(G * b + n, n % 2, turn(b, n, V))
                        rotate(rope_turn(b, G, Q), turn(b, G, Q), True)
                        finish_context(b, H - 2)
                        rotated_lo(rope_turn(b, G, Q), Q)
                        rotate(rope_turn(b, G, K), turn(b, G, K), True)
                        rotated_lo(rope_turn(b, G, K), K)
                        values_lo(G * b + G, 0, turn(b, G, V))
                        finish_context(b, H - 1)
                        t = PAIR_FIRST + PAIR_USES * b + 12
                        dve.wait_ge(pair_full, t + 1)
                        for o in range(KC):
                            last = nc.vector.tensor_scalar(attn_T[:, o, :], pair[o][:], gate[:, 0, o, bass.ds(b, 1)], None, ALU.mult)
                        last.then_inc(attn_scaled, 1)
                        dve.wait_ge(attn_scaled, b + 1)
                        nc.vector.tensor_copy(spare[:, 0:2], ident16[:, 0:2]).then_inc(pair_free, 1)
                        dve.wait_ge(pair_full, t + 2)
                        dve.wait_ge(x_loaded, 16 * b + 16)
                        for half in range(2):
                            part = slice(2 * half, 2 * half + 2)
                            last = nc.vector.tensor_tensor(flat(x1_t[:, part, :]), pair[half][:], flat(x_t[:, part, :]), ALU.add)
                        last.then_inc(x1_done, 1)
                        dve.wait_ge(x1_done, b + 1)
                        for tt in range(TT):
                            last = nc.vector.bn_stats(stats[:, tt, :], x1_t[:, tt, :])
                            if tt == 0:
                                last.then_inc(pair_free, 1)
                        last.then_inc(bn_done, 1)
                        dve.wait_ge(v_ready, 2)
                        dve.wait_ge(bn_done, b + 1)
                        for tt in range(TT):
                            last = nc.vector.bn_aggr(mean_var[:, tt, :], stats[:, tt, :])
                        last.then_inc(agg_done, 1)
                        dve.wait_ge(agg_done, b + 1)
                        nc.vector.tensor_scalar(var_eps[:, 0:TT], mean_var[:, 0:TT, 1], EPS, None, ALU.add).then_inc(var_done, 1)
                        dve.wait_ge(rstd_done, b + 1)
                        for tt in range(TT):
                            last = nc.vector.tensor_scalar(xhat[:, tt, :], x1_t[:, tt, :], mean_var[:, tt, 0:1], rstd[:, tt:tt + 1],
                                                           ALU.subtract, ALU.mult)
                        last.then_inc(xhat_done, 1)
                        dve.wait_ge(pair_full, t + 3)
                        for k in range(KC):
                            normalise_chunk(nc, dve, norm_tiles, pair[k][:], 1, b, k, b * KC + k, h32_done, hhi_done, hlo_done)
                        dve.wait_ge(hlo_done, KC * b + KC)
                        nc.vector.tensor_copy(spare[:, 0:2], ident16[:, 0:2]).then_inc(pair_free, 1)

                @block.scalar
                def _(act):
                    def exponents(b, h):
                        hh = H * b + h
                        act.wait_ge(plo_done, hh + 1)
                        for j, (bk, w, to) in enumerate(((2, 512, 0), (3, 384, 512), (4, 384, 896))):
                            act.wait_ge(st_full, 3 * hh + j + 1)
                            nc.scalar.activation(p32[:, h % 2, to:to + w], bank[bk][:, 0:w], ACT.Exp,
                                                 scale=logit_scale[:]).then_inc(exp_done, 1)

                    def probs_hi(b, h):
                        hh = H * b + h
                        act.wait_ge(mask_done, TT * hh + TT)
                        if h >= 2:
                            act.wait_ge(pv_full, hh - 1)
                        nc.scalar.activation(p_hi[:, h % 2, :], p32[:, h % 2, :], ACT.Copy).then_inc(phi_done, 1)

                    def rotated_hi(r, what, uses):
                        act.wait_ge(rope_sum, r + 1)
                        if uses is not None:
                            act.wait_ge(q_stacked if what == Q else k_stacked, uses)
                        nc.scalar.activation(qk_split[:, what, :, 0, :], rot[:], ACT.Copy).then_inc(rope_hi, 1)

                    def values_hi(par, t):
                        act.wait_ge(pair_full, t + 1)
                        for half in range(2):
                            for eo in range(2):
                                last = nc.scalar.activation(value_part(v_hi, par, half, eo), value_source(half, eo), ACT.Copy,
                                                            scale=V_SHIFT)
                        last.then_inc(v_hi_done, 1)

                    def stacked(b, n, what):
                        return (Q_DMAS if what == Q else K_DMAS) * 16 * (G * b + n)

                    nc.scalar.preload_act_table(ACT.Exp)
                    act.wait_ge(v_ready, 2)
                    nc.scalar.activation(p32[:, 0, 0:2], neg_half[:, 0:2], ACT.Copy).then_inc(exp_done, 3)
                    rotated_hi(0, Q, None)
                    rotated_hi(1, K, None)
                    values_hi(0, 2)
                    with act.Fori(0, B) as b:
                        for h in range(H):
                            n, what = h // HG + 1, h % HG
                            exponents(b, h)
                            if n < G and what in (1, 2):
                                rotated_hi(rope_turn(b, n, what - 1), what - 1, stacked(b, n, what - 1))
                            if n < G and what == 3:
                                values_hi(n % 2, turn(b, n, V))
                            probs_hi(b, h)
                        rotated_hi(rope_turn(b, G, Q), Q, stacked(b, G, Q))
                        rotated_hi(rope_turn(b, G, K), K, stacked(b, G, K))
                        values_hi(0, turn(b, G, V))

                @block.gpsimd
                def _(pool):
                    def mask(b, h):
                        hh = H * b + h
                        pool.wait_ge(exp_done, 3 * hh + 6)
                        nc.gpsimd.tensor_tensor(spare[:, 2:4], ident16[:, 0:2], ident16[:, 0:2], ALU.add)
                        for kt in range(TT):
                            part = p32[:, h % 2, WOFF[kt]:WOFF[kt] + P]
                            nc.gpsimd.affine_select(out=part, in_=part, pattern=[[1, P]], compare_op=ALU.is_ge, fill=0.0,
                                                    base=0, channel_multiplier=-1).then_inc(mask_done, 1)

                    def probs_lo(b, h):
                        hh = H * b + h
                        pool.wait_ge(phi_done, hh + 1)
                        pool.wait_ge(mask_done, TT * hh + TT)
                        nc.gpsimd.tensor_tensor(p_lo[:, h % 2, :], p32[:, h % 2, :], p_hi[:, h % 2, :], ALU.subtract).then_inc(plo_done, 1)

                    def rotate_sum(r, wait_lo):
                        pool.wait_ge(rope_mul, r + 1)
                        if wait_lo:
                            pool.wait_ge(rope_lo, r)
                        nc.gpsimd.tensor_tensor(rot[:, 0, :], rot_part[:, 0, :], rot_part[:, 1, :], ALU.subtract)
                        nc.gpsimd.tensor_tensor(rot[:, 1, :], rot_part[:, 2, :], rot_part[:, 3, :], ALU.add).then_inc(rope_sum, 1)

                    nc.gpsimd.memset(v_hi[:], 1.0).then_inc(v_ready, 1)
                    nc.gpsimd.memset(v_lo[:], 0.0).then_inc(v_ready, 1)
                    nc.gpsimd.memset(p_lo[:], 0.0).then_inc(plo_done, 2)
                    rotate_sum(0, False)
                    rotate_sum(1, True)
                    with pool.Fori(0, B) as b:
                        for h in range(H):
                            mask(b, h)
                            probs_lo(b, h)
                            n, what = h // HG + 1, h % HG
                            if n < G and what < 2:
                                rotate_sum(rope_turn(b, n, what), True)
                        rotate_sum(rope_turn(b, G, Q), True)
                        rotate_sum(rope_turn(b, G, K), True)
                        pool.wait_ge(var_done, b + 1)
                        nc.gpsimd.tensor_tensor(rstd[:, 0:TT], var_eps[:, 0:TT], neg_half[:, 0:TT], ALU.pow).then_inc(rstd_done, 1)

        attn.close()

        with ExitStack() as st:
            MC = KC * F
            acc = sb(st, "acc", [P, KC, B, S])
            w_f = sb(st, "w_f", [P, 3, MC])
            w_hi = sb(st, "w_hi", [P, 2, 3, MC], F16)
            w_lo = sb(st, "w_lo", [P, 2, 3, MC], F16)
            silu_t = sb(st, "silu_t", [P, 2, S])
            mid32 = sb(st, "mid32", [P, 2, S])
            mid_hi = sb(st, "mid_hi", [P, 2, S], F16)
            mid_lo = sb(st, "mid_lo", [P, 2, S], F16)
            w_amax = sb(st, "w_amax", [P, 4])
            w_amax_all = sb(st, "w_amax_all", [P, 4])
            w_bound = sb(st, "w_bound", [P, 1])
            w_pow2 = sb(st, "w_pow2", [P, 2, 3])
            w_ipow2 = sb(st, "w_ipow2", [P, 2, 3])
            w_step = sb(st, "w_step", [P, 3])
            w_alpha = sb(st, "w_alpha", [P, 1])
            g_unscale = sb(st, "g_unscale", [P, 2])
            mid_scale = sb(st, "mid_scale", [P, 2])
            pgud = sb(st, "pgud", [P, 1])
            down_unscale = sb(st, "down_unscale", [P, 2])
            spare = sb(st, "spare_e", [P, 2])
            yT = sb(st, "yT", [P, 2, KC, S])
            x1_b = sb(st, "x1_b", [P, 2, TT, C])

            names = """w_in acc_zero const_done amax_done amax_reduced bound_done pow_done ipow_done alpha_done w_hi_done
                w_scaled w_split scal_a scal_b scal_done g_full u_full silu_done mid_done mhi_done mlo_done y_full y_free
                yT_done tr_full res_done x1_in0 x1_in1 stored0 stored1""".split()
            (w_in, acc_zero, const_done, amax_done, amax_reduced, bound_done, pow_done, ipow_done, alpha_done, w_hi_done,
             w_scaled, w_split, scal_a, scal_b, scal_done, g_full, u_full, silu_done, mid_done, mhi_done, mlo_done, y_full, y_free,
             yT_done, tr_full, res_done, x1_in0, x1_in1, stored0, stored1) = (sem(st, "e_" + n) for n in names)
            x1_in, stored = (x1_in0, x1_in1), (stored0, stored1)

            g_bank, u_bank, y_bank = bank[0:2], bank[2:4], (bank[4:6], bank[6:8])
            PIECE = MC // 4

            def chunk_no(e, t, j):
                return (e * B + t) * FC + j

            with nc.Block() as block:
                @block.sync
                def _(sp):
                    wg_v = wg.rearrange("e (k p) n -> e p k n", p=P)
                    wu_v = wu.rearrange("e (k p) n -> e p k n", p=P)
                    wd_v = wd.rearrange("e (k p) n -> e p k n", p=P)
                    x1_v = x1_dram.rearrange("(n p) c -> p n c", p=P)
                    out_v = out.rearrange("(n p) c -> p n c", p=P)

                    def load(e):
                        for i, w in enumerate((wg_v, wu_v, wd_v)):
                            src = w[bass.ds(e, 1)].rearrange("e p k n -> (e p) k n")
                            sp.dma_start(w_f[:, i, :].rearrange("p (k n) -> p k n", k=src.shape[1]), src).then_inc(w_in, 16)

                    def load_x1(t, a):
                        sp.dma_start(x1_b[:, a], x1_v[:, bass.ds(t * TT, TT), :]).then_inc(x1_in[a], 16)

                    load(0)
                    sp.wait_ge(w_split, 3)
                    load(1)
                    for a in range(2):
                        load_x1(a, a)
                    with sp.Fori(0, E // 2) as ep:
                        for p in range(2):
                            sp.wait_ge(w_split, (2 * ep + p) * 3 + 6)
                            load((2 * ep + p + 2) % E)
                    sp.wait_ge(w_in, 48 * (E + 2))
                    with sp.Fori(0, B // 2 - 1) as tp:
                        for a in range(2):
                            sp.wait_ge(res_done, 2 * tp + a + 1)
                            sp.dma_start(out_v[:, bass.ds((2 * tp + a) * TT, TT), :], x1_b[:, a]).then_inc(stored[a], 16)
                            sp.wait_ge(stored[a], 16 * tp + 16)
                            load_x1(2 * tp + a + 2, a)
                    for a in range(2):
                        sp.wait_ge(res_done, B - 1 + a)
                        sp.dma_start(out_v[:, (B - 2 + a) * TT:(B - 1 + a) * TT, :], x1_b[:, a]).then_inc(stored[a], 16)
                    for a in range(2):
                        sp.wait_ge(stored[a], 16 * (B // 2))

                @block.tensor
                def _(pe):
                    def tokens(t, k):
                        return flat(hT_hi[:, bass.ds(t, 1), k, :]), flat(hT_lo[:, bass.ds(t, 1), k, :])

                    def up(p, e, t, j):
                        n = chunk_no(e, t, j)
                        for i, (bk, free, full) in enumerate(((g_bank, silu_done, g_full), (u_bank, mid_done, u_full))):
                            pe.wait_ge(free, n + 1)
                            for k in range(KC):
                                cols = slice(k * F + j * P, k * F + (j + 1) * P)
                                last = three_passes(nc, bk[j % 2][:], (w_hi[:, p, i, cols], w_lo[:, p, i, cols]), tokens(t, k),
                                                    k == 0, k == KC - 1)
                            last.then_inc(full, 1)

                    def down(p, e, t, a, j):
                        if j == 0:
                            pe.wait_ge(y_free, e * B + t + 1)
                        pe.wait_ge(mlo_done, chunk_no(e, t, j) + 1)
                        for o in range(KC):
                            cols = slice(j * C + o * P, j * C + (o + 1) * P)
                            last = three_passes(nc, y_bank[a][o][:], (w_hi[:, p, 2, cols], w_lo[:, p, 2, cols]),
                                                (mid_hi[:, j % 2], mid_lo[:, j % 2]), j == 0, j == FC - 1)
                        if j == FC - 1:
                            last.then_inc(y_full, 1)

                    def tile(p, e, t, a, more):
                        for j in range(1, FC):
                            up(p, e, t, j)
                            down(p, e, t, a, j - 1)
                        if more:
                            up(p, e, t + 1, 0)
                        down(p, e, t, a, FC - 1)

                    with pe.Fori(0, E // 2) as ep:
                        for p in range(2):
                            e = 2 * ep + p
                            pe.wait_ge(w_split, 3 * e + 3)
                            up(p, e, 0, 0)
                            with pe.Fori(0, B // 2 - 1) as tp:
                                for a in range(2):
                                    tile(p, e, 2 * tp + a, a, True)
                            tile(p, e, B - 2, 0, True)
                            tile(p, e, B - 1, 1, False)
                    with pe.Fori(0, B // 2) as tp:
                        for a in range(2):
                            pe.wait_ge(yT_done, 2 * tp + a + 1)
                            for tt in range(TT):
                                for o in range(KC):
                                    at = (tt % 2) * C + o * P
                                    last = nc.tensor.transpose(bank[2 * a + tt // 2][:, at:at + P],
                                                               yT[:, a, o, tt * P:(tt + 1) * P], ident32[:])
                            last.then_inc(tr_full, 1)

                @block.scalar
                def _(act):
                    def gates(p, n, j):
                        act.wait_ge(g_full, n + 1)
                        nc.scalar.activation(silu_t[:, j % 2], g_bank[j % 2][:], ACT.Silu, scale=g_unscale[:, p:p + 1]).then_inc(silu_done, 1)

                    nc.scalar.preload_act_table(ACT.Silu)
                    nc.scalar.activation(silu_t[:, 0, 0:2], neg_half[:, 0:2], ACT.Copy).then_inc(silu_done, 2)
                    with act.Fori(0, E // 2) as ep:
                        for p in range(2):
                            e = 2 * ep + p
                            act.wait_ge(scal_done, e + 1)
                            with act.Fori(0, B) as t:
                                for j in range(FC):
                                    gates(p, chunk_no(e, t, j), j)

                @block.vector
                def _(dve):
                    def amax_piece(i, piece, n):
                        ins = nc.vector.tensor_reduce(w_amax[:, piece:piece + 1],
                                                      flat(w_f[:, bass.ds(i, 1), piece * PIECE:(piece + 1) * PIECE]),
                                                      AX.X, ALU.max, apply_absolute_value=True)
                        if piece == 3:
                            ins.then_inc(amax_done, 1)

                    def find_bound(n):
                        dve.wait_ge(amax_reduced, n + 1)
                        nc.vector.tensor_reduce(w_bound[:], w_amax_all[:], AX.X, ALU.max).then_inc(bound_done, 1)

                    def guard_bound(n):
                        dve.wait_ge(bound_done, 2 * n + 1)
                        nc.vector.tensor_scalar(w_bound[:], w_bound[:], TINY, None, ALU.max).then_inc(bound_done, 1)

                    def find_pow2(p, i, n):
                        dve.wait_ge(bound_done, 2 * n + 2)
                        nc.vector.tensor_scalar(w_pow2[:, p, bass.ds(i, 1)].bitcast(I32), w_bound[:].bitcast(I32), EXPONENT, None,
                                                ALU.bitwise_and).then_inc(pow_done, 1)

                    def invert_pow2(p, i, n):
                        dve.wait_ge(pow_done, n + 1)
                        nc.vector.reciprocal(w_ipow2[:, p, bass.ds(i, 1)], w_pow2[:, p, bass.ds(i, 1)]).then_inc(ipow_done, 1)

                    def find_alpha(p, i, n):
                        dve.wait_ge(ipow_done, n + 1)
                        nc.vector.tensor_scalar(w_alpha[:], w_ipow2[:, p, bass.ds(i, 1)], w_step[:, bass.ds(i, 1)], None,
                                                ALU.mult).then_inc(alpha_done, 1)

                    def derive_first(p, n):
                        dve.wait_ge(ipow_done, n)
                        nc.vector.tensor_scalar(g_unscale[:, p:p + 1], w_pow2[:, p, 0:1], pow2[:, 1:2], SILU_UNSCALE, ALU.mult, ALU.mult)
                        nc.vector.tensor_scalar(pgud[:], w_pow2[:, p, 0:1], w_pow2[:, p, 1:2], w_pow2[:, p, 2:3],
                                                ALU.mult, ALU.mult).then_inc(scal_a, 1)

                    def derive_second(p, e):
                        nc.vector.tensor_scalar(mid_scale[:, p:p + 1], w_ipow2[:, p, 0:1], ipow2[:, 1:2], MID_SHIFT, ALU.mult, ALU.mult)
                        dve.wait_ge(scal_a, e + 1)
                        nc.vector.tensor_scalar(down_unscale[:, p:p + 1], pgud[:], ph2sq[:], DOWN_UNSCALE,
                                                ALU.mult, ALU.mult).then_inc(scal_done, 1)

                    def middle(p, n, j):
                        dve.wait_ge(u_full, n + 1)
                        dve.wait_ge(silu_done, n + 3)
                        nc.vector.scalar_tensor_tensor(mid32[:, j % 2], u_bank[j % 2][:], mid_scale[:, p:p + 1], silu_t[:, j % 2],
                                                       ALU.mult, ALU.mult).then_inc(mid_done, 1)
                        dve.wait_ge(mid_done, n + 3)
                        nc.vector.tensor_copy(mid_hi[:, j % 2], mid32[:, j % 2]).then_inc(mhi_done, 1)
                        dve.wait_ge(mhi_done, n + 1)
                        nc.vector.tensor_tensor(mid_lo[:, j % 2], mid32[:, j % 2], mid_hi[:, j % 2], ALU.subtract).then_inc(mlo_done, 1)

                    def collect(p, e, t, a):
                        dve.wait_ge(y_full, e * B + t + 1)
                        for o in range(KC):
                            part = flat(acc[:, o, bass.ds(t, 1), :])
                            last = nc.vector.scalar_tensor_tensor(part, y_bank[a][o][:], down_unscale[:, p:p + 1], part, ALU.mult, ALU.add)
                        last.then_inc(y_free, 1)

                    def tile(p, e, t, a, more, between):
                        for j in range(1, FC):
                            middle(p, chunk_no(e, t, j), j)
                            between(j)
                        if more:
                            middle(p, chunk_no(e, t + 1, 0), 0)
                        collect(p, e, t, a)

                    nc.vector.memset(mid32[:], 0.0).then_inc(mid_done, 2)
                    nc.vector.memset(mid_lo[:], 0.0).then_inc(y_free, 2)
                    nc.vector.memset(w_step[:, 0:2], W_SCALE).then_inc(const_done, 1)
                    nc.vector.memset(w_step[:, 2:3], O_SCALE).then_inc(const_done, 1)
                    dve.wait_ge(const_done, 2)
                    dve.wait_ge(w_in, 48)
                    for i in range(3):
                        if i:
                            dve.wait_ge(amax_reduced, i)
                        for piece in range(4):
                            amax_piece(i, piece, i)
                        find_bound(i)
                        guard_bound(i)
                        find_pow2(0, i, i)
                        invert_pow2(0, i, i)
                        if i:
                            dve.wait_ge(w_scaled, i)
                        find_alpha(0, i, i)
                    derive_first(0, 3)
                    derive_second(0, 0)
                    dve.wait_ge(scal_done, 1)
                    dve.wait_ge(acc_zero, 1)
                    with dve.Fori(0, E // 2) as ep:
                        for p in range(2):
                            e = 2 * ep + p
                            middle(p, chunk_no(e, 0, 0), 0)
                            with dve.Fori(0, B // 2 - 1) as tp:
                                n = 3 * e + 3 + tp

                                def even(j):
                                    if j == 1:
                                        dve.wait_ge(w_in, 48 * (e + 2))
                                    if 2 <= j < 6:
                                        amax_piece(tp, j - 2, n)

                                def odd(j):
                                    if j == 1:
                                        find_bound(n)
                                    if j == 2:
                                        guard_bound(n)
                                    if j == 3:
                                        find_pow2(1 - p, tp, n)
                                    if j == 4:
                                        invert_pow2(1 - p, tp, n)
                                    if j == 5:
                                        dve.wait_ge(w_scaled, n)
                                        find_alpha(1 - p, tp, n)

                                tile(p, e, 2 * tp, 0, True, even)
                                tile(p, e, 2 * tp + 1, 1, True, odd)

                            def derive(j):
                                if j == 1:
                                    derive_first(1 - p, 3 * e + 6)
                                if j == 2:
                                    derive_second(1 - p, e + 1)

                            tile(p, e, B - 2, 0, True, derive)
                            tile(p, e, B - 1, 1, False, lambda j: None)
                    with dve.Fori(0, B // 2) as tp:
                        for a in range(2):
                            t = 2 * tp + a
                            for o in range(KC):
                                last = nc.vector.tensor_scalar(yT[:, a, o, :], flat(acc[:, o, bass.ds(t, 1), :]),
                                                               gate[:, 1, o, bass.ds(t, 1)], None, ALU.mult)
                            last.then_inc(yT_done, 1)
                        for a in range(2):
                            dve.wait_ge(tr_full, 2 * tp + a + 1)
                            dve.wait_ge(x1_in[a], 16 * tp + 16)
                            for half in range(2):
                                part = flat(x1_b[:, a, 2 * half:2 * half + 2, :])
                                last = nc.vector.tensor_tensor(part, bank[2 * a + half][:], part, ALU.add)
                            last.then_inc(res_done, 1)

                @block.gpsimd
                def _(pool):
                    def split(p, i, n):
                        pool.wait_ge(amax_done, n + 1)
                        nc.gpsimd.tensor_tensor(spare[:], neg_half[:, 0:2], neg_half[:, 0:2], ALU.add)
                        nc.gpsimd.partition_all_reduce(w_amax_all[:], w_amax[:], P, bass.bass_isa.ReduceOp.max).then_inc(amax_reduced, 1)
                        pool.wait_ge(w_in, 48)
                        pool.wait_ge(alpha_done, n + 1)
                        w, hi = w_f[:, i, :], w_hi[:, p, i, :]
                        nc.gpsimd.tensor_scalar(hi, w, w_alpha[:], 1.0, ALU.mult, ALU.mult).then_inc(w_hi_done, 1)
                        pool.wait_ge(w_in, 48)
                        pool.wait_ge(w_hi_done, n + 1)
                        nc.gpsimd.tensor_scalar(w, w, w_alpha[:], 1.0, ALU.mult, ALU.mult).then_inc(w_scaled, 1)
                        pool.wait_ge(w_scaled, n + 1)
                        nc.gpsimd.tensor_tensor(w_lo[:, p, i, :], w, hi, ALU.subtract).then_inc(w_split, 1)

                    for i in range(3):
                        split(0, i, i)
                    nc.gpsimd.memset(acc[:], 0.0).then_inc(acc_zero, 1)
                    with pool.Fori(0, E // 2) as ep:
                        for p in range(2):
                            for i in range(3):
                                split(1 - p, i, 3 * (2 * ep + p) + 3 + i)


def rotary_tables():
    import numpy as np

    half = D // 2
    fraction = np.float32(2.0) * np.arange(half, dtype=np.float32) / np.float32(D)
    timescale = np.float32(1.0) * np.power(np.float32(10000.0), fraction, dtype=np.float32)
    angle = np.arange(S, dtype=np.float32)[None, :] / timescale[:, None]
    return [np.ascontiguousarray(np.tile(f(angle).astype(np.float32) * np.float32(QK_SHIFT), (HG, 1))) for f in (np.cos, np.sin)]


def kernel(L0_attn_x, L0_attn_wqkv, L0_attn_wo, L0_ffn_Wg, L0_ffn_Wu, L0_ffn_Wd, L0_c, L0_wmod):
    import numpy as np
    import concourse.bacc as bacc
    from concourse.bass_utils import run_bass_kernel_spmd

    w = np.asarray(L0_attn_wqkv).reshape(KC, P, 3, G, HG, 2, D // 2)
    qk = w[:, :, 0:2].transpose(1, 0, 3, 2, 5, 4, 6).reshape(P, KC, G, 4 * P)
    v = w[:, :, 2].transpose(1, 0, 2, 3, 4, 5).reshape(P, KC, G, 2 * P)
    cos_t, sin_t = rotary_tables()
    arrays = {
        "x": np.ascontiguousarray(np.asarray(L0_attn_x).reshape(B * S, C)),
        "wqkv": np.ascontiguousarray(np.concatenate([qk, v], axis=3).reshape(P, KC * G * 6 * P)),
        "wo": np.ascontiguousarray(L0_attn_wo),
        "wg": np.ascontiguousarray(L0_ffn_Wg),
        "wu": np.ascontiguousarray(L0_ffn_Wu),
        "wd": np.ascontiguousarray(L0_ffn_Wd),
        "cT": np.ascontiguousarray(np.asarray(L0_c).T.reshape(KC, P, B).transpose(1, 0, 2)),
        "wmod": np.ascontiguousarray(L0_wmod),
        "cosT": cos_t,
        "sinT": sin_t,
    }
    nc = bacc.Bacc("TRN2", target_bir_lowering=False, num_devices=1)
    args = [nc.dram_tensor(n, a.shape, mybir.dt.from_np(a.dtype), kind="ExternalInput").ap() for n, a in arrays.items()]
    args.append(nc.dram_tensor("out", (B * S, C), F32, kind="ExternalOutput").ap())
    args.append(nc.dram_tensor("x1", (B * S, C), F32, kind="Internal").ap())
    args.append(nc.dram_tensor("rows", (2, 2, P, 2, S), F16, kind="Internal").ap())
    adaln_block_kernel(nc, *args)
    r = run_bass_kernel_spmd(nc, [arrays], core_ids=[0])
    return r.results[0]["out"].reshape(B, S, C)
```

```python
import concourse.bass as bass
from concourse import mybir
from contextlib import ExitStack

F32 = mybir.dt.float32
F16 = mybir.dt.float16
I32 = mybir.dt.int32
ACT = mybir.ActivationFunctionType
ALU = mybir.AluOpType
AX = mybir.AxisListType

P = 128
B = 8
S = 512
C = 256
H = 16
D = 64
E = 8
F = 1024
KC = C // P
TT = S // P
G = 4
HG = H // G
CC = H * D // P
FC = F // P
EPS = 1e-5

TINY = 1e-30
EXPONENT = 0x7F800000
H_SCALE = 2.0 ** 13
W_SCALE = 2.0 ** 9
O_SCALE = 2.0 ** 14
QK_SHIFT = 2.0 ** -17
V_SHIFT = 2.0 ** -13
MAX_UNIT = 2.0 ** 15
LOGIT_SCALE = (1.0 / 8.0) / (H_SCALE * W_SCALE * QK_SHIFT) ** 2
ATTN_UNSCALE = 1.0 / (H_SCALE * W_SCALE * V_SHIFT * O_SCALE)
SILU_UNSCALE = 1.0 / (H_SCALE * W_SCALE)
MID_SHIFT = 2.0 ** -19
DOWN_UNSCALE = 1.0 / (H_SCALE * W_SCALE * MID_SHIFT * O_SCALE)

LOG_EXP_SET = 6
WOFF = [0, 512, 896, 1152]
PW = 1280
MASKED = -2.0 ** 15


def flat(ap):
    return ap.rearrange("p a n -> p (a n)")


def three_passes(nc, out, stationary, moving, first, last):
    s, m = stationary, moving
    nc.tensor.matmul(out, s[0], m[0], start=first, stop=False)
    nc.tensor.matmul(out, s[0], m[1], start=False, stop=False)
    return nc.tensor.matmul(out, s[1], m[0], start=False, stop=last)


def normalise_chunk(nc, dve, tiles, ps, which, b, k, n, h32_done, hhi_done, hlo_done):
    hT_hi, hT_lo, h32, ln_mul, ln_add = tiles
    hi = flat(hT_hi[:, bass.ds(b, 1), k, :])
    lo = flat(hT_lo[:, bass.ds(b, 1), k, :])
    nc.vector.tensor_scalar(h32[:, k], ps, ln_mul[:, which, k, bass.ds(b, 1)], ln_add[:, which, k, bass.ds(b, 1)],
                            ALU.mult, ALU.add).then_inc(h32_done, 1)
    dve.wait_ge(h32_done, n + 1)
    nc.vector.tensor_copy(hi, h32[:, k]).then_inc(hhi_done, 1)
    dve.wait_ge(hhi_done, n + 1)
    nc.vector.tensor_tensor(lo, h32[:, k], hi, ALU.subtract).then_inc(hlo_done, 1)


def adaln_block_kernel(nc, x, wqkv, wo, wg, wu, wd, cT, wmod, cosT, sinT, out, x1_dram, rows_dram):
    ctx = ExitStack()
    with ctx:
        def sb(stack, name, shape, dt=F32):
            return stack.enter_context(nc.sbuf_tensor(name, shape, dt))

        def sem(stack, name):
            return stack.enter_context(nc.semaphore(name))

        bank = [ctx.enter_context(nc.psum_tensor(f"bank{i}", [P, 512], F32)) for i in range(8)]

        hT_hi = sb(ctx, "hT_hi", [P, B, KC, S], F16)
        hT_lo = sb(ctx, "hT_lo", [P, B, KC, S], F16)
        modT = sb(ctx, "modT", [P, 12, B])
        ln_mul = sb(ctx, "ln_mul", [P, 2, KC, B])
        ln_add = sb(ctx, "ln_add", [P, 2, KC, B])
        gate = sb(ctx, "gate", [P, 2, KC, B])
        pow2 = sb(ctx, "pow2", [P, 4])
        ipow2 = sb(ctx, "ipow2", [P, 4])
        logit_scale = sb(ctx, "logit_scale", [P, 1])
        ph2sq = sb(ctx, "ph2sq", [P, 1])
        ident32 = sb(ctx, "ident32", [P, P])
        neg_half = sb(ctx, "neg_half", [P, 4 * B])
        xhat = sb(ctx, "xhat", [P, TT, C])
        mean_var = sb(ctx, "mean_var", [P, TT * B, 2])
        var_eps = sb(ctx, "var_eps", [P, TT * B])
        rstd = sb(ctx, "rstd", [P, TT * B])

        attn = ctx.enter_context(ExitStack())
        wqkv_hi = sb(attn, "wqkv_hi", [P, KC, G, 6 * P], F16)
        wqkv_lo = sb(attn, "wqkv_lo", [P, KC, G, 6 * P], F16)
        wo_hi = sb(attn, "wo_hi", [P, CC, C], F16)
        wo_lo = sb(attn, "wo_lo", [P, CC, C], F16)
        gate_rows = sb(attn, "gate_rows", [P, B, C])
        cos_t = sb(attn, "cos_t", [P, S])
        sin_t = sb(attn, "sin_t", [P, S])
        max_mask = sb(attn, "max_mask", [P, P], F16)
        ident_unit = sb(attn, "ident_unit", [P, P], F16)
        ident16 = sb(attn, "ident16", [P, P], F16)
        ones15 = sb(attn, "ones15", [P, P], F16)

        with ExitStack() as st:
            h32 = sb(st, "h32", [P, KC, S])
            norm_tiles = (hT_hi, hT_lo, h32, ln_mul, ln_add)
            x_all = sb(st, "x_all", [P, B * TT, C])
            wqkv_f = sb(st, "wqkv_f", [P, KC * G * 6 * P])
            wo_f = sb(st, "wo_f", [P, CC * C])
            wmod_f = sb(st, "wmod_f", [P, KC, 6 * C])
            c_f = sb(st, "c_f", [P, KC, B])
            c_silu = sb(st, "c_silu", [P, KC, B])
            stats = sb(st, "stats", [P, B * TT, 6])
            one_c = sb(st, "one_c", [P, 2, KC, B])
            amax = sb(st, "amax", [P, 6])
            amax_all = sb(st, "amax_all", [P, 6])
            bound = sb(st, "bound", [P, 4])
            alpha = sb(st, "alpha", [P, 4])
            tmp = sb(st, "tmp", [P, 2, KC, B])
            tmp1 = sb(st, "tmp1", [P, 1])

            x_in, w_in, wo_in, c_in, table_in = (sem(st, n) for n in ("x_in", "w_in", "wo_in", "c_in", "table_in"))
            gate_done, rows_full = sem(st, "gate_done"), sem(st, "rows_full")
            silu_done, mod_full, amax_done, amax_reduced, chain, bn_done = (
                sem(st, n) for n in ("silu_done", "mod_full", "amax_done", "amax_reduced", "chain", "bn_done"))
            var_done, rstd_done, alpha_done, wq_hi_done, wo_hi_done = (
                sem(st, n) for n in ("var_done", "rstd_done", "alpha_done", "wq_hi_done", "wo_hi_done"))
            const_pool, xhat_done, tr_full, h32_done, hhi_done, hlo_done = (
                sem(st, n) for n in ("const_pool", "xhat_done", "tr_full", "h32_done", "hhi_done", "hlo_done"))

            with nc.Block() as block:
                @block.sync
                def _(sp):
                    sp.dma_start(c_f[:], cT).then_inc(c_in, 16)
                    sp.dma_start(wmod_f[:], wmod.rearrange("(k p) n -> p k n", p=P)).then_inc(c_in, 16)
                    for b in range(B):
                        sp.dma_start(x_all[:, b * TT:(b + 1) * TT, :],
                                     x.rearrange("(n p) c -> p n c", p=P)[:, b * TT:(b + 1) * TT, :]).then_inc(x_in, 16)
                    sp.dma_start(wqkv_f[:], wqkv).then_inc(w_in, 16)
                    sp.dma_start(wo_f[:].rearrange("p (c n) -> p c n", n=C),
                                 wo.rearrange("(c p) n -> p c n", p=P)).then_inc(wo_in, 16)
                    sp.dma_start(cos_t[:], cosT).then_inc(table_in, 16)
                    sp.dma_start(sin_t[:], sinT).then_inc(table_in, 16)
                    sp.wait_ge(table_in, 32)

                @block.gpsimd
                def _(pool):
                    step = [0]

                    def link(ins):
                        step[0] += 1
                        ins.then_inc(const_pool, 1)
                        pool.wait_ge(const_pool, step[0])

                    link(nc.gpsimd.memset(ident32[:], 0.0))
                    link(nc.gpsimd.affine_select(out=ident32[:], in_=ident32[:], pattern=[[-1, P]],
                                                 compare_op=ALU.not_equal, fill=1.0, base=0, channel_multiplier=1))
                    link(nc.gpsimd.memset(ident16[:], 0.0))
                    link(nc.gpsimd.affine_select(out=ident16[:], in_=ident16[:], pattern=[[-1, P]],
                                                 compare_op=ALU.not_equal, fill=1.0, base=0, channel_multiplier=1))
                    link(nc.gpsimd.memset(ident_unit[:], 0.0))
                    link(nc.gpsimd.affine_select(out=ident_unit[:], in_=ident_unit[:], pattern=[[-1, P]],
                                                 compare_op=ALU.not_equal, fill=MAX_UNIT, base=0, channel_multiplier=1))
                    link(nc.gpsimd.memset(max_mask[:], 0.0))
                    link(nc.gpsimd.affine_select(out=max_mask[:], in_=max_mask[:],
                                                 pattern=[[-1, P]], compare_op=ALU.is_ge, fill=MASKED,
                                                 base=0, channel_multiplier=1))
                    link(nc.gpsimd.memset(ones15[:], MAX_UNIT))
                    link(nc.gpsimd.memset(neg_half[:], -0.5))
                    pool.wait_ge(var_done, 1)
                    nc.gpsimd.tensor_tensor(rstd[:], var_eps[:], neg_half[:], ALU.pow).then_inc(rstd_done, 1)
                    pool.wait_ge(amax_done, 6)
                    nc.gpsimd.partition_all_reduce(amax_all[:], amax[:], P, bass.bass_isa.ReduceOp.max).then_inc(amax_reduced, 1)

                @block.scalar
                def _(act):
                    act.wait_ge(c_in, 32)
                    nc.scalar.activation(c_silu[:], c_f[:], ACT.Silu).then_inc(silu_done, 1)
                    act.wait_ge(alpha_done, 1)
                    act.wait_ge(w_in, 16)
                    nc.scalar.activation(flat(wqkv_hi[:].rearrange("p k g n -> p k (g n)")), wqkv_f[:], ACT.Copy,
                                         scale=alpha[:, 2:3]).then_inc(wq_hi_done, 1)
                    act.wait_ge(wo_in, 16)
                    nc.scalar.activation(flat(wo_hi[:]), wo_f[:], ACT.Copy, scale=alpha[:, 3:4]).then_inc(wo_hi_done, 1)
                    act.wait_ge(rows_full, 1)
                    for i in range(B // 2):
                        nc.scalar.activation(flat(gate_rows[:, 2 * i:2 * i + 2, :]), bank[1 + i][:], ACT.Copy)

                @block.tensor
                def _(pe):
                    pe.wait_ge(silu_done, 1)
                    for m in range(12):
                        for k in range(KC):
                            last = nc.tensor.matmul(bank[0][:, m * B:(m + 1) * B], wmod_f[:, k, m * P:(m + 1) * P],
                                                    c_silu[:, k, :], start=(k == 0), stop=(k == KC - 1))
                    last.then_inc(mod_full, 1)
                    pe.wait_ge(const_pool, 2)
                    pe.wait_ge(gate_done, 1)
                    for b in range(B):
                        for k in range(KC):
                            col = gate[:, 0, k, b:b + 1].to_broadcast([P, P])
                            at = (b % 2) * C + k * P
                            last = nc.tensor.matmul(bank[1 + b // 2][:, at:at + P], col, ident32[:], start=True, stop=True)
                    last.then_inc(rows_full, 1)
                    with pe.Fori(0, B) as b:
                        pe.wait_ge(xhat_done, b + 1)
                        for k in range(KC):
                            for t in range(TT):
                                last = nc.tensor.transpose(bank[6 + k][:, t * P:(t + 1) * P],
                                                           xhat[:, t, k * P:(k + 1) * P], ident32[:])
                            last.then_inc(tr_full, 1)

                @block.vector
                def _(dve):
                    step = [0]

                    def link(ins):
                        step[0] += 1
                        ins.then_inc(chain, 1)
                        dve.wait_ge(chain, step[0])

                    dve.wait_ge(mod_full, 1)
                    link(nc.vector.tensor_copy(modT[:].rearrange("p m b -> p (m b)"), bank[0][:, 0:12 * B]))
                    m = modT[:].rearrange("p (l r k) b -> p l r k b", l=2, r=3)
                    link(nc.vector.tensor_scalar(one_c[:], m[:, :, 1], 1.0, None, ALU.add))
                    for i in range(2):
                        nc.vector.tensor_reduce(amax[:, 2 + 2 * i:3 + 2 * i], one_c[:, i], AX.XY, ALU.max,
                                                apply_absolute_value=True).then_inc(amax_done, 1)
                        nc.vector.tensor_reduce(amax[:, 3 + 2 * i:4 + 2 * i], m[:, i, 0], AX.XY, ALU.max,
                                                apply_absolute_value=True).then_inc(amax_done, 1)
                    dve.wait_ge(x_in, 16 * B)
                    with dve.Fori(0, B * TT) as t:
                        nc.vector.bn_stats(flat(stats[:, bass.ds(t, 1), :]), flat(x_all[:, bass.ds(t, 1), :])).then_inc(bn_done, 1)
                    dve.wait_ge(bn_done, B * TT)
                    for t in range(B * TT):
                        nc.vector.bn_aggr(mean_var[:, t, :], stats[:, t, :]).then_inc(bn_done, 1)
                    dve.wait_ge(bn_done, 2 * B * TT)
                    nc.vector.tensor_scalar(var_eps[:], mean_var[:, :, 1], EPS, None, ALU.add).then_inc(var_done, 1)
                    dve.wait_ge(w_in, 16)
                    nc.vector.tensor_reduce(amax[:, 0:1], wqkv_f[:], AX.X, ALU.max,
                                            apply_absolute_value=True).then_inc(amax_done, 1)
                    dve.wait_ge(wo_in, 16)
                    nc.vector.tensor_reduce(amax[:, 1:2], wo_f[:], AX.X, ALU.max,
                                            apply_absolute_value=True).then_inc(amax_done, 1)
                    dve.wait_ge(amax_reduced, 1)
                    for i in range(2):
                        link(nc.vector.tensor_scalar(bound[:, i:i + 1], amax_all[:, 2 + 2 * i:3 + 2 * i],
                                                     amax_all[:, 3 + 2 * i:4 + 2 * i], 16.0, ALU.add, ALU.mult))
                    link(nc.vector.tensor_copy(bound[:, 2:4], amax_all[:, 0:2]))
                    link(nc.vector.tensor_scalar(bound[:], bound[:], TINY, None, ALU.max))
                    link(nc.vector.tensor_scalar(pow2[:].bitcast(I32), bound[:].bitcast(I32), EXPONENT, None, ALU.bitwise_and))
                    link(nc.vector.reciprocal(ipow2[:], pow2[:]))
                    for i, s in enumerate((H_SCALE, H_SCALE, W_SCALE, O_SCALE)):
                        ins = nc.vector.tensor_scalar(alpha[:, i:i + 1], ipow2[:, i:i + 1], s, None, ALU.mult)
                        link(ins)
                    nc.vector.tensor_scalar(tmp1[:], pow2[:, 0:1], pow2[:, 2:3], None, ALU.mult).then_inc(alpha_done, 1)
                    dve.wait_ge(alpha_done, 1)
                    link(nc.vector.tensor_scalar(logit_scale[:], tmp1[:], tmp1[:], LOGIT_SCALE, ALU.mult, ALU.mult))
                    link(nc.vector.tensor_scalar(ph2sq[:], pow2[:, 1:2], pow2[:, 1:2], None, ALU.mult))
                    for i in range(2):
                        link(nc.vector.tensor_scalar(ln_mul[:, i], one_c[:, i], alpha[:, i:i + 1], None, ALU.mult))
                        link(nc.vector.tensor_scalar(ln_add[:, i], m[:, i, 0], alpha[:, i:i + 1], None, ALU.mult))
                    g = m[:, :, 2]
                    link(nc.vector.tensor_scalar(tmp[:], g, 0.0, 2.0, ALU.is_ge, ALU.mult))
                    link(nc.vector.tensor_scalar(tmp[:], tmp[:], -1.0, None, ALU.add))
                    link(nc.vector.scalar_tensor_tensor(gate[:].rearrange("p l k b -> p l (k b)"),
                                                        g.rearrange("p l k b -> p l (k b)"), -1.0,
                                                        g.rearrange("p l k b -> p l (k b)"), ALU.mult, ALU.max))
                    link(nc.vector.tensor_scalar(gate[:], gate[:], 0.25, None, ALU.max))
                    link(nc.vector.tensor_tensor(gate[:], gate[:], tmp[:], ALU.mult))
                    link(nc.vector.tensor_scalar(tmp1[:], tmp1[:], pow2[:, 3:4], ATTN_UNSCALE, ALU.mult, ALU.mult))
                    link(nc.vector.tensor_scalar(gate[:, 0], gate[:, 0], tmp1[:], None, ALU.mult))
                    nc.vector.tensor_copy(tmp[:, 0, 0, 0:2], gate[:, 0, 0, 0:2]).then_inc(gate_done, 1)
                    dve.wait_ge(wq_hi_done, 1)
                    nc.vector.scalar_tensor_tensor(flat(wqkv_lo[:].rearrange("p k g n -> p k (g n)")), wqkv_f[:],
                                                   alpha[:, 2:3], flat(wqkv_hi[:].rearrange("p k g n -> p k (g n)")),
                                                   ALU.mult, ALU.subtract)
                    dve.wait_ge(wo_hi_done, 1)
                    nc.vector.scalar_tensor_tensor(flat(wo_lo[:]), wo_f[:], alpha[:, 3:4], flat(wo_hi[:]),
                                                   ALU.mult, ALU.subtract)
                    dve.wait_ge(rstd_done, 1)
                    with dve.Fori(0, B) as b:
                        for t in range(TT):
                            n = b * TT + t
                            last = nc.vector.tensor_scalar(
                                xhat[:, t, :], flat(x_all[:, bass.ds(n, 1), :]), flat(mean_var[:, bass.ds(n, 1), 0:1]),
                                rstd[:, bass.ds(n, 1)], ALU.subtract, ALU.mult)
                        last.then_inc(xhat_done, 1)
                        for k in range(KC):
                            dve.wait_ge(tr_full, b * KC + k + 1)
                            normalise_chunk(nc, dve, norm_tiles, bank[6 + k][:], 0, b, k, b * KC + k, h32_done, hhi_done, hlo_done)

        with ExitStack() as st:
            k_stack = sb(st, "k_stack", [P, 2, HG, S], F16)
            q_stack = sb(st, "q_stack", [P, 2, HG, 2, S], F16)
            rot_part = sb(st, "rot_part", [P, 4, S])
            norm_tiles = (hT_hi, hT_lo, rot_part[:, 0:KC], ln_mul, ln_add)
            rot = sb(st, "rot", [P, 2, S])
            qk_split = sb(st, "qk_split", [P, 2, 2, 2, S], F16)
            v_hi = sb(st, "v_hi", [P, 2, TT * HG, P], F16)
            v_lo = sb(st, "v_lo", [P, 2, TT * HG, P], F16)
            spare = sb(st, "spare", [P, 4], F16)
            row_max = sb(st, "row_max", [P, 2, TT])
            neg_max = sb(st, "neg_max", [P, 2, S], F16)
            p32 = sb(st, "p32", [P, 2, PW])
            p_hi = sb(st, "p_hi", [P, 2, PW], F16)
            p_lo = sb(st, "p_lo", [P, 2, PW], F16)
            recip = sb(st, "recip", [P, S])
            ctx32 = sb(st, "ctx32", [P, S])
            ctx_hi = sb(st, "ctx_hi", [P, 2, CC, S], F16)
            ctx_lo = sb(st, "ctx_lo", [P, 2, CC, S], F16)
            x1_t = sb(st, "x1_t", [P, TT, C])
            stats = sb(st, "stats_b", [P, TT, 6])

            names = """pair_full pair_free rope_mul rope_sum rope_hi rope_lo q_stacked k_stacked v_ready v_hi_done v_lo_done
                s_full max_done diag_done st_full exp_done mask_done phi_done plo_done pv_full recip_done ctx_done
                ctx_part ctx_split x_loaded gated x1_done x1_stored bn_done2 agg_done var_done2 rstd_done2 xhat_done2
                h32_done2 hhi_done2 hlo_done2 log_done""".split()
            (pair_full, pair_free, rope_mul, rope_sum, rope_hi, rope_lo, q_stacked, k_stacked, v_ready, v_hi_done, v_lo_done,
             s_full, max_done, diag_done, st_full, exp_done, mask_done, phi_done, plo_done, pv_full, recip_done, ctx_done,
             ctx_part, ctx_split, x_loaded, gated, x1_done, x1_stored, bn_done, agg_done, var_done, rstd_done, xhat_done,
             h32_done, hhi_done, hlo_done, log_done) = (sem(st, n) for n in names)
            rows_out = (sem(st, "q_rows_out"), sem(st, "k_rows_out"))

            Q, K, V = 0, 1, 2
            AHEAD = 5
            STACK = 4 * 16
            pair = (bank[6], bank[7])

            def ready(eng, s, n):
                if not isinstance(n, int) or n > 0:
                    eng.wait_ge(s, n)

            def turn(b, h):
                if isinstance(b, int) and b == 0:
                    return AHEAD + h - h // HG
                return AHEAD + 12 + 15 * (b - 1) + h

            def rope_no(b, n, what):
                return 2 * (G * b + n) + what

            def value_part(v, par, half, eo):
                tiles = v[:, par, 2 * HG * half:2 * HG * (half + 1), :].rearrange("p (j two) n -> p j two n", two=2)
                return tiles[:, :, eo, eo * D:(eo + 1) * D]

            def value_source(half, eo):
                return pair[half][:].rearrange("p (j two n) -> p j two n", two=2, n=D)[:, :, eo, :]

            with nc.Block() as block:
                @block.sync
                def _(sp):
                    x_v = x.rearrange("(n p) c -> p n c", p=P)
                    x1_v = x1_dram.rearrange("(n p) c -> p n c", p=P)

                    def stack(b, n, what):
                        there = rows_dram[what].rearrange("h p l t -> p h l t")
                        sp.wait_ge(rope_lo, rope_no(b, n, what) + 1)
                        sp.dma_start(there, qk_split[:, what]).then_inc(rows_out[what], 16)
                        sp.wait_ge(rows_out[what], 16 * (G * b + n) + 16)
                        ready(sp, st_full, 3 * (H * b + HG * (n - 1)))
                        for quad in range(4):
                            half = rows_dram[what, quad % 2].rearrange("(i d) l t -> d i l t", i=HG)
                            to = slice(32 * quad, 32 * quad + 32)
                            if what == Q:
                                sp.dma_start(q_stack[to, n % 2], half).then_inc(q_stacked, 16)
                            else:
                                sp.dma_start(k_stack[to, n % 2], half[:, :, quad // 2]).then_inc(k_stacked, 16)

                    def batch(b, first):
                        stack(b, 1, K)
                        stack(b, 2, Q)
                        stack(b, 2, K)
                        stack(b, 3, Q)
                        stack(b, 3, K)
                        if not first:
                            sp.wait_ge(x1_done, 2 * b)
                            sp.dma_start(x1_v[:, bass.ds((b - 1) * TT, TT), :], x1_t[:]).then_inc(x1_stored, 16)
                        stack(b, 4, Q)
                        if not first:
                            sp.wait_ge(x1_stored, 16 * b)
                            sp.wait_ge(xhat_done, b)
                        sp.dma_start(x1_t[:], x_v[:, bass.ds(b * TT, TT), :]).then_inc(x_loaded, 16)
                        stack(b, 4, K)
                        stack(b, 5, Q)

                    stack(0, 0, Q)
                    stack(0, 0, K)
                    stack(0, 1, Q)
                    batch(0, True)
                    with sp.Fori(1, B) as b:
                        batch(b, False)
                    sp.wait_ge(x1_done, 2 * B)
                    sp.dma_start(x1_v[:, (B - 1) * TT:B * TT, :], x1_t[:]).then_inc(x1_stored, 16)
                    sp.wait_ge(x1_stored, 16 * B)
                    sp.wait_ge(q_stacked, STACK * (G * B + 2))

                @block.tensor
                def _(pe):
                    def proj(b, n, what, t):
                        ready(pe, pair_free, t)
                        b, g = ((b + 1) % B, n - G) if n >= G else (b, n)
                        if what in (Q, K):
                            for half in range(2):
                                for k in range(KC):
                                    h = (flat(hT_hi[:, bass.ds(b, 1), k, :]), flat(hT_lo[:, bass.ds(b, 1), k, :]))
                                    cols = slice((2 * what + half) * P, (2 * what + half + 1) * P)
                                    w = (wqkv_hi[:, k, g, cols], wqkv_lo[:, k, g, cols])
                                    last = three_passes(nc, pair[half][:], w, h, k == 0, k == KC - 1)
                        else:
                            for tt in range(TT):
                                for k in range(KC):
                                    rows = slice(tt * P, (tt + 1) * P)
                                    h = (flat(hT_hi[:, bass.ds(b, 1), k, rows]), flat(hT_lo[:, bass.ds(b, 1), k, rows]))
                                    w = (wqkv_hi[:, k, g, 4 * P:], wqkv_lo[:, k, g, 4 * P:])
                                    last = three_passes(nc, pair[tt // 2][:, (tt % 2) * C:(tt % 2 + 1) * C], h, w,
                                                        k == 0, k == KC - 1)
                        last.then_inc(pair_full, 1)

                    def scores_qk(b, h, qt):
                        par, i = (h // HG) % 2, h % HG
                        if i == 0 and qt == 0:
                            pe.wait_ge(q_stacked, STACK * (G * b + h // HG + 1))
                            pe.wait_ge(k_stacked, STACK * (G * b + h // HG + 1))
                        ready(pe, max_done, TT * (H * b + h) + qt - 1)
                        nc.tensor.matmul(bank[qt % 2][:, 0:(qt + 1) * P], q_stack[:, par, i, 0, qt * P:(qt + 1) * P],
                                         k_stack[:, par, i, 0:(qt + 1) * P], start=True, stop=False)
                        nc.tensor.matmul(bank[qt % 2][:, qt * P:(qt + 1) * P], ident_unit[:], max_mask[:],
                                         start=False, stop=True).then_inc(s_full, 1)

                    def scores_kq(b, h, kt):
                        par, i = (h // HG) % 2, h % HG
                        hh = H * b + h
                        at = 2 * P if kt == 3 else 0
                        to = bank[2 + min(kt, 2)][:, at:at + S - kt * P]
                        rows = slice(kt * P, (kt + 1) * P)
                        if kt < 3:
                            ready(pe, exp_done, 3 * (hh - 1) + kt + 1)
                        if kt == 0:
                            pe.wait_ge(diag_done, hh + 1)
                        nc.tensor.matmul(to, k_stack[:, par, i, rows], q_stack[:, par, i, 0, kt * P:], start=True, stop=False)
                        nc.tensor.matmul(to, k_stack[:, par, i, rows], q_stack[:, par, i, 1, kt * P:], start=False, stop=False)
                        last = nc.tensor.matmul(to, ones15[:], neg_max[:, h % 2, kt * P:], start=False, stop=True)
                        if kt != 2:
                            last.then_inc(st_full, 1)

                    def context(b, h):
                        par, i = (h // HG) % 2, h % HG
                        hh = H * b + h
                        pe.wait_ge(plo_done, hh + 1)
                        if i == 0:
                            pe.wait_ge(v_lo_done, G * b + h // HG + 1)
                        ready(pe, ctx_done, hh)
                        for kt in range(TT):
                            cols = slice(WOFF[kt], WOFF[kt] + S - kt * P)
                            v = (v_hi[:, par, kt * HG + i, :], v_lo[:, par, kt * HG + i, :])
                            last = three_passes(nc, bank[5][:, kt * P:], v, (p_hi[:, h % 2, cols], p_lo[:, h % 2, cols]),
                                                kt == 0, kt == TT - 1)
                        last.then_inc(pv_full, 1)

                    def output(b, half, t):
                        pe.wait_ge(pair_free, t)
                        if half == 0:
                            pe.wait_ge(ctx_split, CC * b + CC)
                        for tt in (2 * half, 2 * half + 1):
                            for c in range(CC):
                                rows = slice(tt * P, (tt + 1) * P)
                                c_part = (flat(ctx_hi[:, bass.ds(b % 2, 1), c, rows]), flat(ctx_lo[:, bass.ds(b % 2, 1), c, rows]))
                                last = three_passes(nc, pair[half][:, (tt % 2) * C:(tt % 2 + 1) * C], c_part,
                                                    (wo_hi[:, c, :], wo_lo[:, c, :]), c == 0, c == CC - 1)
                        last.then_inc(pair_full, 1)

                    def transposes(b, t):
                        pe.wait_ge(xhat_done, b + 1)
                        pe.wait_ge(pair_free, t)
                        for k in range(KC):
                            for tt in range(TT):
                                last = nc.tensor.transpose(pair[k][:, tt * P:(tt + 1) * P], xhat[:, tt, k * P:(k + 1) * P], ident32[:])
                        last.then_inc(pair_full, 1)

                    def batch(b, first):
                        for h in range(H):
                            g = h // HG
                            if not first or h >= 2:
                                context(b, h - 2)
                            scores_qk(b, h + 1, 0)
                            scores_qk(b, h + 1, 1)
                            for kt in range(TT):
                                scores_kq(b, h, kt)
                            scores_qk(b, h + 1, 2)
                            scores_qk(b, h + 1, 3)
                            if h % HG < 3:
                                n, what = ((g + 1, V), (g + 2, Q), (g + 2, K))[h % HG]
                                proj(b, n, what, turn(b, h))
                            elif not first and g < 2:
                                output(b - 1, g, turn(b, h))
                            elif not first and g == 2:
                                transposes(b - 1, turn(b, h))

                    for t, (n, what) in enumerate(((0, Q), (0, K), (1, Q), (1, K), (0, V))):
                        proj(0, n, what, t)
                    for qt in range(TT):
                        scores_qk(0, 0, qt)
                    batch(0, True)
                    with pe.Fori(1, B) as b:
                        batch(b, False)
                    context(B, -2)
                    context(B, -1)
                    for half in range(2):
                        output(B - 1, half, turn(B, half))
                    transposes(B - 1, turn(B, 2))

                @block.vector
                def _(dve):
                    def maxima(b, h):
                        hh = H * b + h
                        for qt in range(TT):
                            dve.wait_ge(s_full, TT * hh + qt + 1)
                            nc.vector.tensor_reduce(row_max[:, h % 2, qt:qt + 1], bank[qt % 2][:, 0:(qt + 1) * P], AX.X,
                                                    ALU.max).then_inc(max_done, 1)
                        dve.wait_ge(max_done, TT * hh + TT)
                        for qt in range(TT):
                            last = nc.vector.tensor_scalar(neg_max[:, h % 2, qt * P:(qt + 1) * P], ident16[:],
                                                           row_max[:, h % 2, qt:qt + 1], -1.0 / MAX_UNIT, ALU.mult, ALU.mult)
                        last.then_inc(diag_done, 1)

                    def release_pair():
                        nc.vector.tensor_copy(spare[:, 0:2], ident16[:, 0:2]).then_inc(pair_free, 1)

                    def rotate(b, n, what, t):
                        r = rope_no(b, n, what)
                        dve.wait_ge(pair_full, t + 1)
                        ready(dve, rope_sum, r)
                        nc.vector.tensor_tensor(rot_part[:, 0, :], pair[0][:], cos_t[:], ALU.mult)
                        nc.vector.tensor_tensor(rot_part[:, 3, :], pair[0][:], sin_t[:], ALU.mult)
                        nc.vector.tensor_tensor(rot_part[:, 1, :], pair[1][:], sin_t[:], ALU.mult)
                        nc.vector.tensor_tensor(rot_part[:, 2, :], pair[1][:], cos_t[:], ALU.mult).then_inc(rope_mul, 1)
                        dve.wait_ge(rope_mul, r + 1)
                        release_pair()

                    def rotated_lo(b, n, what):
                        dve.wait_ge(rope_hi, rope_no(b, n, what) + 1)
                        nc.vector.tensor_tensor(qk_split[:, what, :, 1, :], rot[:], qk_split[:, what, :, 0, :],
                                                ALU.subtract).then_inc(rope_lo, 1)

                    def values_lo(b, n):
                        dve.wait_ge(v_hi_done, G * b + n + 1)
                        for half in range(2):
                            for eo in range(2):
                                to, of = (value_part(v, n % 2, half, eo) for v in (v_lo, v_hi))
                                last = nc.vector.scalar_tensor_tensor(to, value_source(half, eo), V_SHIFT, of, ALU.mult, ALU.subtract)
                        last.then_inc(v_lo_done, 1)
                        dve.wait_ge(v_lo_done, G * b + n + 1)
                        release_pair()

                    def finish_context(b, h):
                        hh = H * b + h
                        mine = slice(0, D) if h % 2 == 0 else slice(D, P)
                        if h % 2 == 0:
                            ready(dve, ctx_split, CC * b + h // 2)
                        dve.wait_ge(recip_done, hh + 1)
                        nc.vector.tensor_tensor(ctx32[mine, :], bank[5][mine, :], recip[mine, :], ALU.mult).then_inc(ctx_done, 1)
                        if h % 2 == 1:
                            of, c = (b, h // 2) if h >= 0 else (b - 1, h // 2 + CC)
                            hi, lo = (flat(z[:, bass.ds(of % 2, 1), c, :]) for z in (ctx_hi, ctx_lo))
                            n = CC * b + h // 2 + 1
                            dve.wait_ge(ctx_done, hh + 1)
                            nc.vector.tensor_copy(hi, ctx32[:]).then_inc(ctx_part, 1)
                            dve.wait_ge(ctx_part, n)
                            nc.vector.tensor_tensor(lo, ctx32[:], hi, ALU.subtract).then_inc(ctx_split, 1)

                    def residual(b, half, t):
                        tiles = slice(2 * half, 2 * half + 2)
                        scaled = flat(xhat[:, tiles, :])
                        dve.wait_ge(pair_full, t + 1)
                        if half == 0:
                            dve.wait_ge(x_loaded, 16 * b + 16)
                        for j in range(2):
                            last = nc.vector.tensor_tensor(xhat[:, 2 * half + j, :], pair[half][:, j * C:(j + 1) * C],
                                                           flat(gate_rows[:, bass.ds(b, 1), :]), ALU.mult)
                        last.then_inc(gated, 1)
                        dve.wait_ge(gated, 2 * b + half + 1)
                        nc.vector.tensor_tensor(flat(x1_t[:, tiles, :]), scaled, flat(x1_t[:, tiles, :]), ALU.add).then_inc(x1_done, 1)
                        release_pair()
                        dve.wait_ge(x1_done, 2 * b + half + 1)
                        for tt in (2 * half, 2 * half + 1):
                            last = nc.vector.bn_stats(stats[:, tt, :], x1_t[:, tt, :])
                        last.then_inc(bn_done, 1)

                    def statistics(b):
                        dve.wait_ge(v_ready, 2)
                        dve.wait_ge(bn_done, 2 * b + 2)
                        for tt in range(TT):
                            last = nc.vector.bn_aggr(mean_var[:, tt, :], stats[:, tt, :])
                        last.then_inc(agg_done, 1)
                        dve.wait_ge(agg_done, b + 1)
                        nc.vector.tensor_scalar(var_eps[:, 0:TT], mean_var[:, 0:TT, 1], EPS, None, ALU.add).then_inc(var_done, 1)

                    def normalise(b):
                        dve.wait_ge(rstd_done, b + 1)
                        for tt in range(TT):
                            last = nc.vector.tensor_scalar(xhat[:, tt, :], x1_t[:, tt, :], mean_var[:, tt, 0:1], rstd[:, tt:tt + 1],
                                                           ALU.subtract, ALU.mult)
                        last.then_inc(xhat_done, 1)

                    def modulate(b, t, rotations):
                        dve.wait_ge(pair_full, t + 1)
                        dve.wait_ge(rope_sum, rotations)
                        for k in range(KC):
                            normalise_chunk(nc, dve, norm_tiles, pair[k][:], 1, b, k, b * KC + k, h32_done, hhi_done, hlo_done)
                        release_pair()

                    def batch(b, first):
                        for h in range(H):
                            g = h // HG
                            if h % HG == 0:
                                if not first and g in (1, 2):
                                    residual(b - 1, g - 1, turn(b, h - 1))
                                if not first and g == 3:
                                    modulate(b - 1, turn(b, h - 1), rope_no(b, g + 1, K) + 1)
                            elif h % HG == 1:
                                values_lo(b, g + 1)
                            elif h % HG == 2:
                                rotate(b, g + 2, Q, turn(b, h - 1))
                            else:
                                rotate(b, g + 2, K, turn(b, h - 1))
                                rotated_lo(b, g + 2, Q)
                            maxima(b, h + 1)
                            if not first or h >= 2:
                                finish_context(b, h - 2)
                            if h % HG == 0:
                                rotated_lo(b, g + 1, K)
                            if not first and h == 9:
                                statistics(b - 1)
                            if not first and h == 10:
                                normalise(b - 1)

                    for t, (n, what) in enumerate(((0, Q), (0, K), (1, Q))):
                        rotate(0, n, what, t)
                        rotated_lo(0, n, what)
                    rotate(0, 1, K, 3)
                    dve.wait_ge(v_ready, 2)
                    values_lo(0, 0)
                    maxima(0, 0)
                    batch(0, True)
                    with dve.Fori(1, B) as b:
                        batch(b, False)
                    finish_context(B, -2)
                    finish_context(B, -1)
                    for half in range(2):
                        residual(B - 1, half, turn(B, half))
                    statistics(B - 1)
                    normalise(B - 1)
                    modulate(B - 1, turn(B, 2), rope_no(B, 1, K) + 1)

                @block.scalar
                def _(act):
                    def exponents(b, h):
                        hh = H * b + h
                        ready(act, plo_done, hh - 1)
                        for j, (bk, w, to) in enumerate(((2, 512, 0), (3, 384, 512), (4, 384, 896))):
                            act.wait_ge(st_full, 3 * hh + j + 1)
                            nc.scalar.activation(p32[:, h % 2, to:to + w], bank[bk][:, 0:w], ACT.Exp,
                                                 scale=logit_scale[:]).then_inc(exp_done, 1)

                    def probs_hi(b, h):
                        hh = H * b + h
                        act.wait_ge(mask_done, hh + 1)
                        ready(act, pv_full, hh - 1)
                        nc.scalar.activation(p_hi[:, h % 2, :], p32[:, h % 2, :], ACT.Copy).then_inc(phi_done, 1)

                    def reciprocals(b, h):
                        hh = H * b + h
                        mine, sums = (slice(0, D), slice(D, P)) if h % 2 == 0 else (slice(D, P), slice(0, D))
                        act.wait_ge(pv_full, hh + 1)
                        ready(act, ctx_done, hh - 1)
                        nc.scalar.activation(recip[mine, :], bank[5][sums, :], ACT.Ln).then_inc(log_done, 1)
                        act.wait_ge(log_done, hh + 1)
                        nc.scalar.activation(recip[mine, :], recip[mine, :], ACT.Exp, scale=-1.0).then_inc(recip_done, 1)

                    def rotated_hi(b, n, what):
                        act.wait_ge(rope_sum, rope_no(b, n, what) + 1)
                        ready(act, q_stacked if what == Q else k_stacked, STACK * (G * b + n))
                        nc.scalar.activation(qk_split[:, what, :, 0, :], rot[:], ACT.Copy).then_inc(rope_hi, 1)

                    def values_hi(b, n, t):
                        act.wait_ge(pair_full, t + 1)
                        ready(act, pv_full, H * b + HG * (n - 1))
                        for half in range(2):
                            for eo in range(2):
                                last = nc.scalar.activation(value_part(v_hi, n % 2, half, eo), value_source(half, eo), ACT.Copy,
                                                            scale=V_SHIFT)
                        last.then_inc(v_hi_done, 1)

                    def batch(b, first):
                        for h in range(H):
                            g = h // HG
                            if h % HG == 1:
                                values_hi(b, g + 1, turn(b, h - 1))
                            if not first or h >= 1:
                                probs_hi(b, h - 1)
                            if not first or h >= 2:
                                reciprocals(b, h - 2)
                            exponents(b, h)
                            if h % HG == 2:
                                rotated_hi(b, g + 2, Q)
                            elif h % HG == 3:
                                rotated_hi(b, g + 2, K)

                    nc.scalar.add_instruction(mybir.InstLoadActFuncSet(name=nc.get_next_instruction_name(), act_func_set_id=LOG_EXP_SET,
                                                                       engine=mybir.EngineType.Activation))
                    for n, what in ((0, Q), (0, K), (1, Q), (1, K)):
                        rotated_hi(0, n, what)
                    act.wait_ge(v_ready, 2)
                    values_hi(0, 0, 4)
                    batch(0, True)
                    with act.Fori(1, B) as b:
                        batch(b, False)
                    probs_hi(B, -1)
                    reciprocals(B, -2)
                    reciprocals(B, -1)

                @block.gpsimd
                def _(pool):
                    def mask(b, h):
                        hh = H * b + h
                        pool.wait_ge(exp_done, 3 * hh + 3)
                        nc.gpsimd.tensor_tensor(spare[:, 2:4], ident16[:, 0:2], ident16[:, 0:2], ALU.add)
                        for kt in range(TT):
                            part = p32[:, h % 2, WOFF[kt]:WOFF[kt] + P]
                            last = nc.gpsimd.affine_select(out=part, in_=part, pattern=[[1, P]], compare_op=ALU.is_ge, fill=0.0,
                                                           base=0, channel_multiplier=-1)
                        last.then_inc(mask_done, 1)

                    def probs_lo(b, h):
                        hh = H * b + h
                        pool.wait_ge(phi_done, hh + 1)
                        nc.gpsimd.tensor_tensor(p_lo[:, h % 2, :], p32[:, h % 2, :], p_hi[:, h % 2, :], ALU.subtract).then_inc(plo_done, 1)

                    def rotate_sum(b, n, what):
                        r = rope_no(b, n, what)
                        pool.wait_ge(rope_mul, r + 1)
                        ready(pool, rope_lo, r)
                        nc.gpsimd.tensor_tensor(rot[:, 0, :], rot_part[:, 0, :], rot_part[:, 1, :], ALU.subtract)
                        nc.gpsimd.tensor_tensor(rot[:, 1, :], rot_part[:, 2, :], rot_part[:, 3, :], ALU.add).then_inc(rope_sum, 1)

                    def batch(b, first):
                        for h in range(H):
                            g = h // HG
                            if not first or h >= 1:
                                probs_lo(b, h - 1)
                            if h % HG == 2:
                                rotate_sum(b, g + 2, Q)
                            elif h % HG == 3:
                                rotate_sum(b, g + 2, K)
                            mask(b, h)
                            if not first and h == 9:
                                pool.wait_ge(var_done, b)
                                nc.gpsimd.tensor_tensor(rstd[:, 0:TT], var_eps[:, 0:TT], neg_half[:, 0:TT], ALU.pow).then_inc(rstd_done, 1)

                    nc.gpsimd.memset(v_hi[:], 1.0).then_inc(v_ready, 1)
                    nc.gpsimd.memset(v_lo[:], 0.0).then_inc(v_ready, 1)
                    for n, what in ((0, Q), (0, K), (1, Q), (1, K)):
                        rotate_sum(0, n, what)
                    batch(0, True)
                    with pool.Fori(1, B) as b:
                        batch(b, False)
                    probs_lo(B, -1)
                    pool.wait_ge(var_done, B)
                    nc.gpsimd.tensor_tensor(rstd[:, 0:TT], var_eps[:, 0:TT], neg_half[:, 0:TT], ALU.pow).then_inc(rstd_done, 1)

        attn.close()

        with ExitStack() as st:
            MC = KC * F
            acc = sb(st, "acc", [P, KC, B, S])
            w_f = sb(st, "w_f", [P, 3, MC])
            w_hi = sb(st, "w_hi", [P, 2, 3, MC], F16)
            w_lo = sb(st, "w_lo", [P, 2, 3, MC], F16)
            silu_t = sb(st, "silu_t", [P, 2, S])
            mid32 = sb(st, "mid32", [P, 2, S])
            mid_hi = sb(st, "mid_hi", [P, 2, S], F16)
            mid_lo = sb(st, "mid_lo", [P, 2, S], F16)
            w_amax = sb(st, "w_amax", [P, 4])
            w_amax_all = sb(st, "w_amax_all", [P, 4])
            w_bound = sb(st, "w_bound", [P, 1])
            w_pow2 = sb(st, "w_pow2", [P, 2, 3])
            w_ipow2 = sb(st, "w_ipow2", [P, 2, 3])
            w_step = sb(st, "w_step", [P, 3])
            w_alpha = sb(st, "w_alpha", [P, 1])
            g_unscale = sb(st, "g_unscale", [P, 2])
            mid_scale = sb(st, "mid_scale", [P, 2])
            pgud = sb(st, "pgud", [P, 1])
            down_unscale = sb(st, "down_unscale", [P, 2])
            spare = sb(st, "spare_e", [P, 2])
            yT = sb(st, "yT", [P, 2, KC, S])
            x1_b = sb(st, "x1_b", [P, 2, TT, C])

            names = """w_in acc_zero const_done amax_done amax_reduced bound_done pow_done ipow_done alpha_done w_hi_done
                w_scaled w_split scal_a scal_b scal_done g_full u_full silu_done mid_done mhi_done mlo_done y_full y_free
                yT_done tr_full res_done x1_in0 x1_in1 stored0 stored1""".split()
            (w_in, acc_zero, const_done, amax_done, amax_reduced, bound_done, pow_done, ipow_done, alpha_done, w_hi_done,
             w_scaled, w_split, scal_a, scal_b, scal_done, g_full, u_full, silu_done, mid_done, mhi_done, mlo_done, y_full, y_free,
             yT_done, tr_full, res_done, x1_in0, x1_in1, stored0, stored1) = (sem(st, "e_" + n) for n in names)
            x1_in, stored = (x1_in0, x1_in1), (stored0, stored1)

            g_bank, u_bank, y_bank = bank[0:2], bank[2:4], (bank[4:6], bank[6:8])
            PIECE = MC // 4

            def chunk_no(e, t, j):
                return (e * B + t) * FC + j

            with nc.Block() as block:
                @block.sync
                def _(sp):
                    wg_v = wg.rearrange("e (k p) n -> e p k n", p=P)
                    wu_v = wu.rearrange("e (k p) n -> e p k n", p=P)
                    wd_v = wd.rearrange("e (k p) n -> e p k n", p=P)
                    x1_v = x1_dram.rearrange("(n p) c -> p n c", p=P)
                    out_v = out.rearrange("(n p) c -> p n c", p=P)

                    def load(e):
                        for i, w in enumerate((wg_v, wu_v, wd_v)):
                            src = w[bass.ds(e, 1)].rearrange("e p k n -> (e p) k n")
                            sp.dma_start(w_f[:, i, :].rearrange("p (k n) -> p k n", k=src.shape[1]), src).then_inc(w_in, 16)

                    def load_x1(t, a):
                        sp.dma_start(x1_b[:, a], x1_v[:, bass.ds(t * TT, TT), :]).then_inc(x1_in[a], 16)

                    load(0)
                    sp.wait_ge(w_split, 3)
                    load(1)
                    for a in range(2):
                        load_x1(a, a)
                    with sp.Fori(0, E // 2) as ep:
                        for p in range(2):
                            sp.wait_ge(w_split, (2 * ep + p) * 3 + 6)
                            load((2 * ep + p + 2) % E)
                    sp.wait_ge(w_in, 48 * (E + 2))
                    with sp.Fori(0, B // 2 - 1) as tp:
                        for a in range(2):
                            sp.wait_ge(res_done, 2 * tp + a + 1)
                            sp.dma_start(out_v[:, bass.ds((2 * tp + a) * TT, TT), :], x1_b[:, a]).then_inc(stored[a], 16)
                            sp.wait_ge(stored[a], 16 * tp + 16)
                            load_x1(2 * tp + a + 2, a)
                    for a in range(2):
                        sp.wait_ge(res_done, B - 1 + a)
                        sp.dma_start(out_v[:, (B - 2 + a) * TT:(B - 1 + a) * TT, :], x1_b[:, a]).then_inc(stored[a], 16)
                    for a in range(2):
                        sp.wait_ge(stored[a], 16 * (B // 2))

                @block.tensor
                def _(pe):
                    def tokens(t, k):
                        return flat(hT_hi[:, bass.ds(t, 1), k, :]), flat(hT_lo[:, bass.ds(t, 1), k, :])

                    def up(p, e, t, j):
                        n = chunk_no(e, t, j)
                        for i, (bk, free, full) in enumerate(((g_bank, silu_done, g_full), (u_bank, mid_done, u_full))):
                            pe.wait_ge(free, n + 1)
                            for k in range(KC):
                                cols = slice(k * F + j * P, k * F + (j + 1) * P)
                                last = three_passes(nc, bk[j % 2][:], (w_hi[:, p, i, cols], w_lo[:, p, i, cols]), tokens(t, k),
                                                    k == 0, k == KC - 1)
                            last.then_inc(full, 1)

                    def down(p, e, t, a, j):
                        if j == 0:
                            pe.wait_ge(y_free, e * B + t + 1)
                        pe.wait_ge(mlo_done, chunk_no(e, t, j) + 1)
                        for o in range(KC):
                            cols = slice(j * C + o * P, j * C + (o + 1) * P)
                            last = three_passes(nc, y_bank[a][o][:], (w_hi[:, p, 2, cols], w_lo[:, p, 2, cols]),
                                                (mid_hi[:, j % 2], mid_lo[:, j % 2]), j == 0, j == FC - 1)
                        if j == FC - 1:
                            last.then_inc(y_full, 1)

                    def tile(p, e, t, a, more):
                        for j in range(1, FC):
                            up(p, e, t, j)
                            down(p, e, t, a, j - 1)
                        if more:
                            up(p, e, t + 1, 0)
                        down(p, e, t, a, FC - 1)

                    with pe.Fori(0, E // 2) as ep:
                        for p in range(2):
                            e = 2 * ep + p
                            pe.wait_ge(w_split, 3 * e + 3)
                            up(p, e, 0, 0)
                            with pe.Fori(0, B // 2 - 1) as tp:
                                for a in range(2):
                                    tile(p, e, 2 * tp + a, a, True)
                            tile(p, e, B - 2, 0, True)
                            tile(p, e, B - 1, 1, False)
                    with pe.Fori(0, B // 2) as tp:
                        for a in range(2):
                            pe.wait_ge(yT_done, 2 * tp + a + 1)
                            for tt in range(TT):
                                for o in range(KC):
                                    at = (tt % 2) * C + o * P
                                    last = nc.tensor.transpose(bank[2 * a + tt // 2][:, at:at + P],
                                                               yT[:, a, o, tt * P:(tt + 1) * P], ident32[:])
                            last.then_inc(tr_full, 1)

                @block.scalar
                def _(act):
                    def gates(p, n, j):
                        act.wait_ge(g_full, n + 1)
                        nc.scalar.activation(silu_t[:, j % 2], g_bank[j % 2][:], ACT.Silu, scale=g_unscale[:, p:p + 1]).then_inc(silu_done, 1)

                    nc.scalar.preload_act_table(ACT.Silu)
                    nc.scalar.activation(silu_t[:, 0, 0:2], neg_half[:, 0:2], ACT.Copy).then_inc(silu_done, 2)
                    with act.Fori(0, E // 2) as ep:
                        for p in range(2):
                            e = 2 * ep + p
                            act.wait_ge(scal_done, e + 1)
                            with act.Fori(0, B) as t:
                                for j in range(FC):
                                    gates(p, chunk_no(e, t, j), j)

                @block.vector
                def _(dve):
                    def amax_piece(i, piece, n):
                        ins = nc.vector.tensor_reduce(w_amax[:, piece:piece + 1],
                                                      flat(w_f[:, bass.ds(i, 1), piece * PIECE:(piece + 1) * PIECE]),
                                                      AX.X, ALU.max, apply_absolute_value=True)
                        if piece == 3:
                            ins.then_inc(amax_done, 1)

                    def find_bound(n):
                        dve.wait_ge(amax_reduced, n + 1)
                        nc.vector.tensor_reduce(w_bound[:], w_amax_all[:], AX.X, ALU.max).then_inc(bound_done, 1)

                    def guard_bound(n):
                        dve.wait_ge(bound_done, 2 * n + 1)
                        nc.vector.tensor_scalar(w_bound[:], w_bound[:], TINY, None, ALU.max).then_inc(bound_done, 1)

                    def find_pow2(p, i, n):
                        dve.wait_ge(bound_done, 2 * n + 2)
                        nc.vector.tensor_scalar(w_pow2[:, p, bass.ds(i, 1)].bitcast(I32), w_bound[:].bitcast(I32), EXPONENT, None,
                                                ALU.bitwise_and).then_inc(pow_done, 1)

                    def invert_pow2(p, i, n):
                        dve.wait_ge(pow_done, n + 1)
                        nc.vector.reciprocal(w_ipow2[:, p, bass.ds(i, 1)], w_pow2[:, p, bass.ds(i, 1)]).then_inc(ipow_done, 1)

                    def find_alpha(p, i, n):
                        dve.wait_ge(ipow_done, n + 1)
                        nc.vector.tensor_scalar(w_alpha[:], w_ipow2[:, p, bass.ds(i, 1)], w_step[:, bass.ds(i, 1)], None,
                                                ALU.mult).then_inc(alpha_done, 1)

                    def derive_first(p, n):
                        dve.wait_ge(ipow_done, n)
                        nc.vector.tensor_scalar(g_unscale[:, p:p + 1], w_pow2[:, p, 0:1], pow2[:, 1:2], SILU_UNSCALE, ALU.mult, ALU.mult)
                        nc.vector.tensor_scalar(pgud[:], w_pow2[:, p, 0:1], w_pow2[:, p, 1:2], w_pow2[:, p, 2:3],
                                                ALU.mult, ALU.mult).then_inc(scal_a, 1)

                    def derive_second(p, e):
                        nc.vector.tensor_scalar(mid_scale[:, p:p + 1], w_ipow2[:, p, 0:1], ipow2[:, 1:2], MID_SHIFT, ALU.mult, ALU.mult)
                        dve.wait_ge(scal_a, e + 1)
                        nc.vector.tensor_scalar(down_unscale[:, p:p + 1], pgud[:], ph2sq[:], DOWN_UNSCALE,
                                                ALU.mult, ALU.mult).then_inc(scal_done, 1)

                    def middle(p, n, j):
                        dve.wait_ge(u_full, n + 1)
                        dve.wait_ge(silu_done, n + 3)
                        nc.vector.scalar_tensor_tensor(mid32[:, j % 2], u_bank[j % 2][:], mid_scale[:, p:p + 1], silu_t[:, j % 2],
                                                       ALU.mult, ALU.mult).then_inc(mid_done, 1)
                        dve.wait_ge(mid_done, n + 3)
                        nc.vector.tensor_copy(mid_hi[:, j % 2], mid32[:, j % 2]).then_inc(mhi_done, 1)
                        dve.wait_ge(mhi_done, n + 1)
                        nc.vector.tensor_tensor(mid_lo[:, j % 2], mid32[:, j % 2], mid_hi[:, j % 2], ALU.subtract).then_inc(mlo_done, 1)

                    def collect(p, e, t, a):
                        dve.wait_ge(y_full, e * B + t + 1)
                        for o in range(KC):
                            part = flat(acc[:, o, bass.ds(t, 1), :])
                            last = nc.vector.scalar_tensor_tensor(part, y_bank[a][o][:], down_unscale[:, p:p + 1], part, ALU.mult, ALU.add)
                        last.then_inc(y_free, 1)

                    def tile(p, e, t, a, more, between):
                        for j in range(1, FC):
                            middle(p, chunk_no(e, t, j), j)
                            between(j)
                        if more:
                            middle(p, chunk_no(e, t + 1, 0), 0)
                        collect(p, e, t, a)

                    nc.vector.memset(mid32[:], 0.0).then_inc(mid_done, 2)
                    nc.vector.memset(mid_lo[:], 0.0).then_inc(y_free, 2)
                    nc.vector.memset(w_step[:, 0:2], W_SCALE).then_inc(const_done, 1)
                    nc.vector.memset(w_step[:, 2:3], O_SCALE).then_inc(const_done, 1)
                    dve.wait_ge(const_done, 2)
                    dve.wait_ge(w_in, 48)
                    for i in range(3):
                        if i:
                            dve.wait_ge(amax_reduced, i)
                        for piece in range(4):
                            amax_piece(i, piece, i)
                        find_bound(i)
                        guard_bound(i)
                        find_pow2(0, i, i)
                        invert_pow2(0, i, i)
                        if i:
                            dve.wait_ge(w_scaled, i)
                        find_alpha(0, i, i)
                    derive_first(0, 3)
                    derive_second(0, 0)
                    dve.wait_ge(scal_done, 1)
                    dve.wait_ge(acc_zero, 1)
                    with dve.Fori(0, E // 2) as ep:
                        for p in range(2):
                            e = 2 * ep + p
                            middle(p, chunk_no(e, 0, 0), 0)
                            with dve.Fori(0, B // 2 - 1) as tp:
                                n = 3 * e + 3 + tp

                                def even(j):
                                    if j == 1:
                                        dve.wait_ge(w_in, 48 * (e + 2))
                                    if 2 <= j < 6:
                                        amax_piece(tp, j - 2, n)

                                def odd(j):
                                    if j == 1:
                                        find_bound(n)
                                    if j == 2:
                                        guard_bound(n)
                                    if j == 3:
                                        find_pow2(1 - p, tp, n)
                                    if j == 4:
                                        invert_pow2(1 - p, tp, n)
                                    if j == 5:
                                        dve.wait_ge(w_scaled, n)
                                        find_alpha(1 - p, tp, n)

                                tile(p, e, 2 * tp, 0, True, even)
                                tile(p, e, 2 * tp + 1, 1, True, odd)

                            def derive(j):
                                if j == 1:
                                    derive_first(1 - p, 3 * e + 6)
                                if j == 2:
                                    derive_second(1 - p, e + 1)

                            tile(p, e, B - 2, 0, True, derive)
                            tile(p, e, B - 1, 1, False, lambda j: None)
                    with dve.Fori(0, B // 2) as tp:
                        for a in range(2):
                            t = 2 * tp + a
                            for o in range(KC):
                                last = nc.vector.tensor_scalar(yT[:, a, o, :], flat(acc[:, o, bass.ds(t, 1), :]),
                                                               gate[:, 1, o, bass.ds(t, 1)], None, ALU.mult)
                            last.then_inc(yT_done, 1)
                        for a in range(2):
                            dve.wait_ge(tr_full, 2 * tp + a + 1)
                            dve.wait_ge(x1_in[a], 16 * tp + 16)
                            for half in range(2):
                                part = flat(x1_b[:, a, 2 * half:2 * half + 2, :])
                                last = nc.vector.tensor_tensor(part, bank[2 * a + half][:], part, ALU.add)
                            last.then_inc(res_done, 1)

                @block.gpsimd
                def _(pool):
                    def split(p, i, n):
                        pool.wait_ge(amax_done, n + 1)
                        nc.gpsimd.tensor_tensor(spare[:], neg_half[:, 0:2], neg_half[:, 0:2], ALU.add)
                        nc.gpsimd.partition_all_reduce(w_amax_all[:], w_amax[:], P, bass.bass_isa.ReduceOp.max).then_inc(amax_reduced, 1)
                        pool.wait_ge(w_in, 48)
                        pool.wait_ge(alpha_done, n + 1)
                        w, hi = w_f[:, i, :], w_hi[:, p, i, :]
                        nc.gpsimd.tensor_scalar(hi, w, w_alpha[:], 1.0, ALU.mult, ALU.mult).then_inc(w_hi_done, 1)
                        pool.wait_ge(w_in, 48)
                        pool.wait_ge(w_hi_done, n + 1)
                        nc.gpsimd.tensor_scalar(w, w, w_alpha[:], 1.0, ALU.mult, ALU.mult).then_inc(w_scaled, 1)
                        pool.wait_ge(w_scaled, n + 1)
                        nc.gpsimd.tensor_tensor(w_lo[:, p, i, :], w, hi, ALU.subtract).then_inc(w_split, 1)

                    for i in range(3):
                        split(0, i, i)
                    nc.gpsimd.memset(acc[:], 0.0).then_inc(acc_zero, 1)
                    with pool.Fori(0, E // 2) as ep:
                        for p in range(2):
                            for i in range(3):
                                split(1 - p, i, 3 * (2 * ep + p) + 3 + i)


def rotary_tables():
    import numpy as np

    half = D // 2
    fraction = np.float32(2.0) * np.arange(half, dtype=np.float32) / np.float32(D)
    timescale = np.float32(1.0) * np.power(np.float32(10000.0), fraction, dtype=np.float32)
    angle = np.arange(S, dtype=np.float32)[None, :] / timescale[:, None]
    return [np.ascontiguousarray(np.tile(f(angle).astype(np.float32) * np.float32(QK_SHIFT), (HG, 1))) for f in (np.cos, np.sin)]


def kernel(L0_attn_x, L0_attn_wqkv, L0_attn_wo, L0_ffn_Wg, L0_ffn_Wu, L0_ffn_Wd, L0_c, L0_wmod):
    import numpy as np
    import concourse.bacc as bacc
    from concourse.bass_utils import run_bass_kernel_spmd

    w = np.asarray(L0_attn_wqkv).reshape(KC, P, 3, G, HG, 2, D // 2)
    qk = w[:, :, 0:2].transpose(1, 0, 3, 2, 5, 4, 6).reshape(P, KC, G, 4 * P)
    v = w[:, :, 2].transpose(1, 0, 2, 3, 4, 5).reshape(P, KC, G, 2 * P)
    cos_t, sin_t = rotary_tables()
    arrays = {
        "x": np.ascontiguousarray(np.asarray(L0_attn_x).reshape(B * S, C)),
        "wqkv": np.ascontiguousarray(np.concatenate([qk, v], axis=3).reshape(P, KC * G * 6 * P)),
        "wo": np.ascontiguousarray(L0_attn_wo),
        "wg": np.ascontiguousarray(L0_ffn_Wg),
        "wu": np.ascontiguousarray(L0_ffn_Wu),
        "wd": np.ascontiguousarray(L0_ffn_Wd),
        "cT": np.ascontiguousarray(np.asarray(L0_c).T.reshape(KC, P, B).transpose(1, 0, 2)),
        "wmod": np.ascontiguousarray(L0_wmod),
        "cosT": cos_t,
        "sinT": sin_t,
    }
    nc = bacc.Bacc("TRN2", target_bir_lowering=False, num_devices=1)
    args = [nc.dram_tensor(n, a.shape, mybir.dt.from_np(a.dtype), kind="ExternalInput").ap() for n, a in arrays.items()]
    args.append(nc.dram_tensor("out", (B * S, C), F32, kind="ExternalOutput").ap())
    args.append(nc.dram_tensor("x1", (B * S, C), F32, kind="Internal").ap())
    args.append(nc.dram_tensor("rows", (2, 2, P, 2, S), F16, kind="Internal").ap())
    adaln_block_kernel(nc, *args)
    r = run_bass_kernel_spmd(nc, [arrays], core_ids=[0])
    return r.results[0]["out"].reshape(B, S, C)
```

```python
import concourse.bass as bass
from concourse import mybir
from contextlib import ExitStack

F32 = mybir.dt.float32
F16 = mybir.dt.float16
I32 = mybir.dt.int32
ACT = mybir.ActivationFunctionType
ALU = mybir.AluOpType
AX = mybir.AxisListType

P = 128
B = 8
S = 512
C = 256
H = 16
D = 64
E = 8
F = 1024
KC = C // P
TT = S // P
G = 4
HG = H // G
CC = H * D // P
FC = F // P
EPS = 1e-5
MC = KC * F
PIECE = MC // 4

TINY = 1e-30
EXPONENT = 0x7F800000
H_SCALE = 2.0 ** 13
W_SCALE = 2.0 ** 9
O_SCALE = 2.0 ** 14
QK_SHIFT = 2.0 ** -17
V_SHIFT = 2.0 ** -13
MAX_UNIT = 2.0 ** 15
LOGIT_SCALE = (1.0 / 8.0) / (H_SCALE * W_SCALE * QK_SHIFT) ** 2
ATTN_UNSCALE = 1.0 / (H_SCALE * W_SCALE * V_SHIFT * O_SCALE)
SILU_UNSCALE = 1.0 / (H_SCALE * W_SCALE)
MID_SHIFT = 2.0 ** -19
DOWN_UNSCALE = 1.0 / (H_SCALE * W_SCALE * MID_SHIFT * O_SCALE)

LOG_EXP_SET = 6
WOFF = [0, 512, 896, 1152]
PW = 1280
MASKED = -2.0 ** 15


def flat(ap):
    return ap.rearrange("p a n -> p (a n)")


def three_passes(nc, out, stationary, moving, first, last):
    s, m = stationary, moving
    nc.tensor.matmul(out, s[0], m[0], start=first, stop=False)
    nc.tensor.matmul(out, s[0], m[1], start=False, stop=False)
    return nc.tensor.matmul(out, s[1], m[0], start=False, stop=last)


def normalise_chunk(nc, dve, tiles, ps, which, b, k, n, h32_done, hhi_done, hlo_done):
    hT_hi, hT_lo, h32, ln_mul, ln_add = tiles
    hi = flat(hT_hi[:, bass.ds(b, 1), k, :])
    lo = flat(hT_lo[:, bass.ds(b, 1), k, :])
    nc.vector.tensor_scalar(h32[:, k], ps, ln_mul[:, which, k, bass.ds(b, 1)], ln_add[:, which, k, bass.ds(b, 1)],
                            ALU.mult, ALU.add).then_inc(h32_done, 1)
    dve.wait_ge(h32_done, n + 1)
    nc.vector.tensor_copy(hi, h32[:, k]).then_inc(hhi_done, 1)
    dve.wait_ge(hhi_done, n + 1)
    nc.vector.tensor_tensor(lo, h32[:, k], hi, ALU.subtract).then_inc(hlo_done, 1)


def adaln_block_kernel(nc, x, wqkv, wo, wg, wu, wd, cT, wmod, cosT, sinT, out, x1_dram, rows_dram):
    ctx = ExitStack()
    with ctx:
        def sb(stack, name, shape, dt=F32):
            return stack.enter_context(nc.sbuf_tensor(name, shape, dt))

        def sem(stack, name):
            return stack.enter_context(nc.semaphore(name))

        bank = [ctx.enter_context(nc.psum_tensor(f"bank{i}", [P, 512], F32)) for i in range(8)]

        hT_hi = sb(ctx, "hT_hi", [P, B, KC, S], F16)
        hT_lo = sb(ctx, "hT_lo", [P, B, KC, S], F16)
        modT = sb(ctx, "modT", [P, 12, B])
        ln_mul = sb(ctx, "ln_mul", [P, 2, KC, B])
        ln_add = sb(ctx, "ln_add", [P, 2, KC, B])
        gate = sb(ctx, "gate", [P, 2, KC, B])
        pow2 = sb(ctx, "pow2", [P, 4])
        ipow2 = sb(ctx, "ipow2", [P, 4])
        logit_scale = sb(ctx, "logit_scale", [P, 1])
        ph2sq = sb(ctx, "ph2sq", [P, 1])
        ident32 = sb(ctx, "ident32", [P, P])
        neg_half = sb(ctx, "neg_half", [P, 4 * B])
        xhat = sb(ctx, "xhat", [P, TT, C])
        mean_var = sb(ctx, "mean_var", [P, TT * B, 2])
        var_eps = sb(ctx, "var_eps", [P, TT * B])
        rstd = sb(ctx, "rstd", [P, TT * B])

        w_f = sb(ctx, "w_f", [P, 3, MC])
        wqkv_split = flat(w_f[:]).bitcast(F16).rearrange("p (s k g n) -> p s k g n", s=2, k=KC, g=G)
        wqkv_hi, wqkv_lo = wqkv_split[:, 0], wqkv_split[:, 1]
        w_even = sb(ctx, "w_even", [P, 2, 3, MC], F16)
        stacks = w_even[:].rearrange("p s w n -> p (s w n)")
        q_stack = stacks[:, 0:4 * HG * S].rearrange("p (g i s t) -> p g i s t", g=2, i=HG, s=2)
        k_stack = stacks[:, 4 * HG * S:].rearrange("p (g i t) -> p g i t", g=2, i=HG)
        w_amax = sb(ctx, "w_amax", [P, 4])
        w_amax_all = sb(ctx, "w_amax_all", [P, 4])
        w_bound = sb(ctx, "w_bound", [P, 1])
        w_pow2 = sb(ctx, "w_pow2", [P, 2, 3])
        w_ipow2 = sb(ctx, "w_ipow2", [P, 2, 3])
        w_step = sb(ctx, "w_step", [P, 3])
        w_alpha = sb(ctx, "w_alpha", [P, 3])
        g_unscale = sb(ctx, "g_unscale", [P, 2])
        mid_scale = sb(ctx, "mid_scale", [P, 2])
        pgud = sb(ctx, "pgud", [P, 1])
        down_unscale = sb(ctx, "down_unscale", [P, 2])
        w_in, const_done, amax_done, amax_reduced, bound_done, pow_done, ipow_done, alpha_done, w_hi_done = (
            sem(ctx, "e_" + n) for n in ("w_in", "const_done", "amax_done", "amax_reduced", "bound_done", "pow_done",
                                         "ipow_done", "alpha_done", "w_hi_done"))
        w_scaled, w_split, scal_a, scal_done = (sem(ctx, "e_" + n) for n in ("w_scaled", "w_split", "scal_a", "scal_done"))

        def load_expert(sp, e):
            for i, w in enumerate((wg, wu, wd)):
                src = w.rearrange("e (k p) n -> e p k n", p=P)[bass.ds(e, 1)].rearrange("e p k n -> (e p) k n")
                sp.dma_start(w_f[:, i, :].rearrange("p (k n) -> p k n", k=src.shape[1]), src).then_inc(w_in, 16)

        def amax_piece(i, piece):
            ins = nc.vector.tensor_reduce(w_amax[:, piece:piece + 1],
                                          flat(w_f[:, bass.ds(i, 1), piece * PIECE:(piece + 1) * PIECE]),
                                          AX.X, ALU.max, apply_absolute_value=True)
            if piece == 3:
                ins.then_inc(amax_done, 1)

        def find_bound(dve, n):
            dve.wait_ge(amax_reduced, n + 1)
            nc.vector.tensor_reduce(w_bound[:], w_amax_all[:], AX.X, ALU.max).then_inc(bound_done, 1)

        def guard_bound(dve, n):
            dve.wait_ge(bound_done, 2 * n + 1)
            nc.vector.tensor_scalar(w_bound[:], w_bound[:], TINY, None, ALU.max).then_inc(bound_done, 1)

        def find_pow2(dve, p, i, n):
            dve.wait_ge(bound_done, 2 * n + 2)
            nc.vector.tensor_scalar(w_pow2[:, p, bass.ds(i, 1)].bitcast(I32), w_bound[:].bitcast(I32), EXPONENT, None,
                                    ALU.bitwise_and).then_inc(pow_done, 1)

        def invert_pow2(dve, p, i, n):
            dve.wait_ge(pow_done, n + 1)
            nc.vector.reciprocal(w_ipow2[:, p, bass.ds(i, 1)], w_pow2[:, p, bass.ds(i, 1)]).then_inc(ipow_done, 1)

        def find_alpha(dve, p, i, n):
            dve.wait_ge(ipow_done, n + 1)
            nc.vector.tensor_scalar(w_alpha[:, bass.ds(i, 1)], w_ipow2[:, p, bass.ds(i, 1)], w_step[:, bass.ds(i, 1)], None,
                                    ALU.mult).then_inc(alpha_done, 1)

        def derive_first(dve, p, n):
            dve.wait_ge(ipow_done, n)
            nc.vector.tensor_scalar(g_unscale[:, p:p + 1], w_pow2[:, p, 0:1], pow2[:, 1:2], SILU_UNSCALE, ALU.mult, ALU.mult)
            nc.vector.tensor_scalar(pgud[:], w_pow2[:, p, 0:1], w_pow2[:, p, 1:2], w_pow2[:, p, 2:3],
                                    ALU.mult, ALU.mult).then_inc(scal_a, 1)

        def derive_second(dve, p, e):
            nc.vector.tensor_scalar(mid_scale[:, p:p + 1], w_ipow2[:, p, 0:1], ipow2[:, 1:2], MID_SHIFT, ALU.mult, ALU.mult)
            dve.wait_ge(scal_a, e + 1)
            nc.vector.tensor_scalar(down_unscale[:, p:p + 1], pgud[:], ph2sq[:], DOWN_UNSCALE,
                                    ALU.mult, ALU.mult).then_inc(scal_done, 1)

        def reduce_amax(pool, n, spare):
            pool.wait_ge(amax_done, n + 1)
            nc.gpsimd.tensor_tensor(spare, neg_half[:, 0:2], neg_half[:, 0:2], ALU.add)
            nc.gpsimd.partition_all_reduce(w_amax_all[:], w_amax[:], P, bass.bass_isa.ReduceOp.max).then_inc(amax_reduced, 1)

        attn = ctx.enter_context(ExitStack())
        wo_hi = sb(attn, "wo_hi", [P, CC, C], F16)
        wo_lo = sb(attn, "wo_lo", [P, CC, C], F16)
        gate_rows = sb(attn, "gate_rows", [P, B, C])
        cos_t = sb(attn, "cos_t", [P, S])
        sin_t = sb(attn, "sin_t", [P, S])
        max_mask = sb(attn, "max_mask", [P, P], F16)
        neg_ident = sb(attn, "neg_ident", [P, P])
        ident_unit = sb(attn, "ident_unit", [P, P], F16)
        ident16 = sb(attn, "ident16", [P, P], F16)
        ones15 = sb(attn, "ones15", [P, P], F16)

        with ExitStack() as st:
            h32 = sb(st, "h32", [P, 2, KC, S])
            ln_bank = ((bank[6], bank[7]), (bank[5], bank[0]))
            xhat_two = sb(st, "xhat_two", [P, 2, TT, C])
            x_all = sb(st, "x_all", [P, B * TT, C])
            wqkv_f = sb(st, "wqkv_f", [P, KC * G * 6 * P])
            wo_f = sb(st, "wo_f", [P, CC * C])
            wmod_f = sb(st, "wmod_f", [P, KC, 6 * C])
            c_f = sb(st, "c_f", [P, KC, B])
            c_silu = sb(st, "c_silu", [P, KC, B])
            stats = sb(st, "stats", [P, B * TT, 6])
            one_c = sb(st, "one_c", [P, 2, KC, B])
            amax = sb(st, "amax", [P, 6])
            amax_all = sb(st, "amax_all", [P, 6])
            bound = sb(st, "bound", [P, 4])
            alpha = sb(st, "alpha", [P, 4])
            tmp = sb(st, "tmp", [P, 2, KC, B])
            tmp1 = sb(st, "tmp1", [P, 1])

            x_in = (sem(st, "x_in_first"), sem(st, "x_in_second"))
            p_w_in, wo_in, c_in, table_in = (sem(st, n) for n in ("w_in", "wo_in", "c_in", "table_in"))
            gate_done, rows_full, wq_scaled = (sem(st, n) for n in ("gate_done", "rows_full", "wq_scaled"))
            silu_done, mod_full, p_amax_done, p_amax_reduced, chain, bn_done = (
                sem(st, n) for n in ("silu_done", "mod_full", "amax_done", "amax_reduced", "chain", "bn_done"))
            var_done, rstd_done, p_alpha_done, wq_hi_done, wo_hi_done = (
                sem(st, n) for n in ("var_done", "rstd_done", "alpha_done", "wq_hi_done", "wo_hi_done"))
            const_pool, xhat_done, tr_full, h32_done, hhi_done, hlo_done = (
                sem(st, n) for n in ("const_pool", "xhat_done", "tr_full", "h32_done", "hhi_done", "hlo_done"))

            with nc.Block() as block:
                @block.sync
                def _(sp):
                    sp.dma_start(c_f[:], cT).then_inc(c_in, 16)
                    sp.dma_start(wmod_f[:], wmod.rearrange("(k p) n -> p k n", p=P)).then_inc(c_in, 16)
                    for b in range(B):
                        sp.dma_start(x_all[:, b * TT:(b + 1) * TT, :],
                                     x.rearrange("(n p) c -> p n c", p=P)[:, b * TT:(b + 1) * TT, :]).then_inc(x_in[b // 4], 16)
                    sp.dma_start(wqkv_f[:], wqkv).then_inc(p_w_in, 16)
                    sp.dma_start(wo_f[:].rearrange("p (c n) -> p c n", n=C),
                                 wo.rearrange("(c p) n -> p c n", p=P)).then_inc(wo_in, 16)
                    sp.dma_start(cos_t[:], cosT).then_inc(table_in, 16)
                    sp.dma_start(sin_t[:], sinT).then_inc(table_in, 16)
                    sp.wait_ge(table_in, 32)

                @block.gpsimd
                def _(pool):
                    step = [0]

                    def link(ins):
                        step[0] += 1
                        ins.then_inc(const_pool, 1)
                        pool.wait_ge(const_pool, step[0])

                    link(nc.gpsimd.memset(ident32[:], 0.0))
                    link(nc.gpsimd.affine_select(out=ident32[:], in_=ident32[:], pattern=[[-1, P]],
                                                 compare_op=ALU.not_equal, fill=1.0, base=0, channel_multiplier=1))
                    link(nc.gpsimd.memset(ident16[:], 0.0))
                    link(nc.gpsimd.affine_select(out=ident16[:], in_=ident16[:], pattern=[[-1, P]],
                                                 compare_op=ALU.not_equal, fill=1.0, base=0, channel_multiplier=1))
                    link(nc.gpsimd.memset(neg_ident[:], 0.0))
                    link(nc.gpsimd.affine_select(out=neg_ident[:], in_=neg_ident[:], pattern=[[-1, P]],
                                                 compare_op=ALU.not_equal, fill=-1.0 / MAX_UNIT, base=0, channel_multiplier=1))
                    link(nc.gpsimd.memset(ident_unit[:], 0.0))
                    link(nc.gpsimd.affine_select(out=ident_unit[:], in_=ident_unit[:], pattern=[[-1, P]],
                                                 compare_op=ALU.not_equal, fill=MAX_UNIT, base=0, channel_multiplier=1))
                    link(nc.gpsimd.memset(max_mask[:], 0.0))
                    link(nc.gpsimd.affine_select(out=max_mask[:], in_=max_mask[:],
                                                 pattern=[[-1, P]], compare_op=ALU.is_ge, fill=MASKED,
                                                 base=0, channel_multiplier=1))
                    link(nc.gpsimd.memset(ones15[:], MAX_UNIT))
                    link(nc.gpsimd.memset(neg_half[:], -0.5))
                    pool.wait_ge(var_done, 1)
                    nc.gpsimd.tensor_tensor(rstd[:], var_eps[:], neg_half[:], ALU.pow).then_inc(rstd_done, 1)
                    pool.wait_ge(p_amax_done, 6)
                    nc.gpsimd.partition_all_reduce(amax_all[:], amax[:], P, bass.bass_isa.ReduceOp.max).then_inc(p_amax_reduced, 1)
                    pool.wait_ge(p_alpha_done, 1)
                    pool.wait_ge(wq_hi_done, 1)
                    nc.gpsimd.tensor_scalar(wqkv_f[:], wqkv_f[:], alpha[:, 2:3], 1.0, ALU.mult, ALU.mult).then_inc(wq_scaled, 1)
                    pool.wait_ge(wq_scaled, 1)
                    nc.gpsimd.tensor_tensor(wqkv_lo.rearrange("p k g n -> p (k g n)"), wqkv_f[:],
                                            wqkv_hi.rearrange("p k g n -> p (k g n)"), ALU.subtract)

                @block.scalar
                def _(act):
                    act.wait_ge(c_in, 32)
                    nc.scalar.activation(c_silu[:], c_f[:], ACT.Silu).then_inc(silu_done, 1)
                    act.wait_ge(p_alpha_done, 1)
                    act.wait_ge(p_w_in, 16)
                    nc.scalar.activation(wqkv_hi.rearrange("p k g n -> p (k g n)"), wqkv_f[:], ACT.Copy,
                                         scale=alpha[:, 2:3]).then_inc(wq_hi_done, 1)
                    act.wait_ge(wo_in, 16)
                    nc.scalar.activation(flat(wo_hi[:]), wo_f[:], ACT.Copy, scale=alpha[:, 3:4]).then_inc(wo_hi_done, 1)
                    act.wait_ge(rows_full, 1)
                    for i in range(B // 2):
                        nc.scalar.activation(flat(gate_rows[:, 2 * i:2 * i + 2, :]), bank[1 + i][:], ACT.Copy)
                    with act.Fori(0, B // 2) as bb:
                        for p in range(2):
                            b = 2 * bb + p
                            act.wait_ge(tr_full, b + 3)
                            act.wait_ge(hlo_done, KC * b + 2)
                            for k in range(KC):
                                nc.scalar.activation(h32[:, p, k], ln_bank[p][k][:], ACT.Identity,
                                                     scale=ln_mul[:, 0, k, bass.ds(b, 1)],
                                                     bias=ln_add[:, 0, k, bass.ds(b, 1)]).then_inc(h32_done, 1)
                            act.wait_ge(h32_done, KC * b + 6)
                            nc.scalar.activation(flat(hT_hi[:, bass.ds(b, 1), :, :].rearrange("p b k s -> p b (k s)")),
                                                 flat(h32[:, p]), ACT.Copy).then_inc(hhi_done, 1)

                @block.tensor
                def _(pe):
                    pe.wait_ge(silu_done, 1)
                    for m in range(12):
                        for k in range(KC):
                            last = nc.tensor.matmul(bank[0][:, m * B:(m + 1) * B], wmod_f[:, k, m * P:(m + 1) * P],
                                                    c_silu[:, k, :], start=(k == 0), stop=(k == KC - 1))
                    last.then_inc(mod_full, 1)
                    pe.wait_ge(const_pool, 2)
                    pe.wait_ge(gate_done, 1)
                    for b in range(B):
                        for k in range(KC):
                            col = gate[:, 0, k, b:b + 1].to_broadcast([P, P])
                            at = (b % 2) * C + k * P
                            last = nc.tensor.matmul(bank[1 + b // 2][:, at:at + P], col, ident32[:], start=True, stop=True)
                    last.then_inc(rows_full, 1)
                    with pe.Fori(0, B // 2) as bb:
                        for p in range(2):
                            b = 2 * bb + p
                            pe.wait_ge(xhat_done, b + 1)
                            pe.wait_ge(h32_done, KC * b + 2)
                            for k in range(KC):
                                for t in range(TT):
                                    last = nc.tensor.transpose(ln_bank[p][k][:, t * P:(t + 1) * P],
                                                               xhat_two[:, p, t, k * P:(k + 1) * P], ident32[:])
                            last.then_inc(tr_full, 1)

                @block.vector
                def _(dve):
                    step = [0]

                    def link(ins):
                        step[0] += 1
                        ins.then_inc(chain, 1)
                        dve.wait_ge(chain, step[0])

                    for b in range(B):
                        if b % 4 == 0:
                            dve.wait_ge(x_in[b // 4], 16 * 4)
                        for t in range(b * TT, (b + 1) * TT):
                            nc.vector.bn_stats(stats[:, t, :], x_all[:, t, :]).then_inc(bn_done, 1)
                    dve.wait_ge(bn_done, B * TT)
                    for t in range(B * TT):
                        nc.vector.bn_aggr(mean_var[:, t, :], stats[:, t, :]).then_inc(bn_done, 1)
                    dve.wait_ge(bn_done, 2 * B * TT)
                    nc.vector.tensor_scalar(var_eps[:], mean_var[:, :, 1], EPS, None, ALU.add).then_inc(var_done, 1)
                    dve.wait_ge(mod_full, 1)
                    link(nc.vector.tensor_copy(modT[:].rearrange("p m b -> p (m b)"), bank[0][:, 0:12 * B]))
                    m = modT[:].rearrange("p (l r k) b -> p l r k b", l=2, r=3)
                    link(nc.vector.tensor_scalar(one_c[:], m[:, :, 1], 1.0, None, ALU.add))
                    for i in range(2):
                        nc.vector.tensor_reduce(amax[:, 2 + 2 * i:3 + 2 * i], one_c[:, i], AX.XY, ALU.max,
                                                apply_absolute_value=True).then_inc(p_amax_done, 1)
                        nc.vector.tensor_reduce(amax[:, 3 + 2 * i:4 + 2 * i], m[:, i, 0], AX.XY, ALU.max,
                                                apply_absolute_value=True).then_inc(p_amax_done, 1)
                    dve.wait_ge(p_w_in, 16)
                    nc.vector.tensor_reduce(amax[:, 0:1], wqkv_f[:], AX.X, ALU.max,
                                            apply_absolute_value=True).then_inc(p_amax_done, 1)
                    dve.wait_ge(wo_in, 16)
                    nc.vector.tensor_reduce(amax[:, 1:2], wo_f[:], AX.X, ALU.max,
                                            apply_absolute_value=True).then_inc(p_amax_done, 1)
                    dve.wait_ge(p_amax_reduced, 1)
                    for i in range(2):
                        link(nc.vector.tensor_scalar(bound[:, i:i + 1], amax_all[:, 2 + 2 * i:3 + 2 * i],
                                                     amax_all[:, 3 + 2 * i:4 + 2 * i], 16.0, ALU.add, ALU.mult))
                    link(nc.vector.tensor_copy(bound[:, 2:4], amax_all[:, 0:2]))
                    link(nc.vector.tensor_scalar(bound[:], bound[:], TINY, None, ALU.max))
                    link(nc.vector.tensor_scalar(pow2[:].bitcast(I32), bound[:].bitcast(I32), EXPONENT, None, ALU.bitwise_and))
                    link(nc.vector.reciprocal(ipow2[:], pow2[:]))
                    for i, s in enumerate((H_SCALE, H_SCALE, W_SCALE, O_SCALE)):
                        ins = nc.vector.tensor_scalar(alpha[:, i:i + 1], ipow2[:, i:i + 1], s, None, ALU.mult)
                        link(ins)
                    nc.vector.tensor_scalar(tmp1[:], pow2[:, 0:1], pow2[:, 2:3], None, ALU.mult).then_inc(p_alpha_done, 1)
                    dve.wait_ge(p_alpha_done, 1)
                    link(nc.vector.tensor_scalar(logit_scale[:], tmp1[:], tmp1[:], LOGIT_SCALE, ALU.mult, ALU.mult))
                    link(nc.vector.tensor_scalar(ph2sq[:], pow2[:, 1:2], pow2[:, 1:2], None, ALU.mult))
                    for i in range(2):
                        link(nc.vector.tensor_scalar(ln_mul[:, i], one_c[:, i], alpha[:, i:i + 1], None, ALU.mult))
                        link(nc.vector.tensor_scalar(ln_add[:, i], m[:, i, 0], alpha[:, i:i + 1], None, ALU.mult))
                    g = m[:, :, 2]
                    link(nc.vector.tensor_scalar(tmp[:], g, 0.0, 2.0, ALU.is_ge, ALU.mult))
                    link(nc.vector.tensor_scalar(tmp[:], tmp[:], -1.0, None, ALU.add))
                    link(nc.vector.scalar_tensor_tensor(gate[:].rearrange("p l k b -> p l (k b)"),
                                                        g.rearrange("p l k b -> p l (k b)"), -1.0,
                                                        g.rearrange("p l k b -> p l (k b)"), ALU.mult, ALU.max))
                    link(nc.vector.tensor_scalar(gate[:], gate[:], 0.25, None, ALU.max))
                    link(nc.vector.tensor_tensor(gate[:], gate[:], tmp[:], ALU.mult))
                    link(nc.vector.tensor_scalar(tmp1[:], tmp1[:], pow2[:, 3:4], ATTN_UNSCALE, ALU.mult, ALU.mult))
                    link(nc.vector.tensor_scalar(gate[:, 0], gate[:, 0], tmp1[:], None, ALU.mult))
                    nc.vector.tensor_copy(tmp[:, 0, 0, 0:2], gate[:, 0, 0, 0:2]).then_inc(gate_done, 1)
                    nc.vector.memset(h32[:, 0, 0, 0:2], 0.0).then_inc(hlo_done, 4)
                    nc.vector.memset(h32[:, 1, 0, 0:2], 0.0).then_inc(h32_done, 4)
                    nc.vector.memset(xhat_two[:, 0, 0, 0:2], 0.0).then_inc(tr_full, 2)

                    def normalised(b, p):
                        dve.wait_ge(tr_full, b + 1)
                        for t in range(TT):
                            n = b * TT + t
                            last = nc.vector.tensor_scalar(xhat_two[:, p, t, :], flat(x_all[:, bass.ds(n, 1), :]),
                                                           flat(mean_var[:, bass.ds(n, 1), 0:1]), rstd[:, bass.ds(n, 1)],
                                                           ALU.subtract, ALU.mult)
                        last.then_inc(xhat_done, 1)

                    def halves(b, p):
                        dve.wait_ge(hhi_done, b + 1)
                        hi, lo = (flat(z[:, bass.ds(b, 1), :, :].rearrange("p b k s -> p b (k s)")) for z in (hT_hi, hT_lo))
                        nc.vector.tensor_tensor(lo, flat(h32[:, p]), hi, ALU.subtract).then_inc(hlo_done, KC)

                    dve.wait_ge(rstd_done, 1)
                    normalised(0, 0)
                    normalised(1, 1)
                    dve.wait_ge(wo_hi_done, 1)
                    nc.vector.scalar_tensor_tensor(flat(wo_lo[:]), wo_f[:], alpha[:, 3:4], flat(wo_hi[:]),
                                                   ALU.mult, ALU.subtract)
                    with dve.Fori(0, B // 2 - 1) as bb:
                        for p in range(2):
                            normalised(2 * bb + 2 + p, p)
                            halves(2 * bb + p, p)
                    for p in range(2):
                        halves(B - 2 + p, p)

        with ExitStack() as st:
            rot_part = sb(st, "rot_part", [P, 4, S])
            norm_tiles = (hT_hi, hT_lo, rot_part[:, 0:KC], ln_mul, ln_add)
            rot = sb(st, "rot", [P, 2, S])
            qk_split = sb(st, "qk_split", [P, 2, 2, 2, S], F16)
            v_hi = sb(st, "v_hi", [P, 2, TT * HG, P], F16)
            v_lo = sb(st, "v_lo", [P, 2, TT * HG, P], F16)
            spare = sb(st, "spare", [P, 4], F16)
            spare32 = sb(st, "spare32", [P, 2])
            row_max = sb(st, "row_max", [P, 2, TT])
            neg_max = sb(st, "neg_max", [P, 2, S], F16)
            p32 = sb(st, "p32", [P, 2, PW])
            p_hi = sb(st, "p_hi", [P, 2, PW], F16)
            p_lo = sb(st, "p_lo", [P, 2, PW], F16)
            recip = sb(st, "recip", [P, S])
            ctx32 = sb(st, "ctx32", [P, S])
            ctx_hi = sb(st, "ctx_hi", [P, 2, CC, S], F16)
            ctx_lo = sb(st, "ctx_lo", [P, 2, CC, S], F16)
            x1_t = sb(st, "x1_t", [P, TT, C])
            stats = sb(st, "stats_b", [P, TT, 6])

            names = """pair_full pair_free rope_mul rope_sum rope_hi rope_lo q_stacked k_stacked v_ready v_hi_done v_lo_done
                s_full max_done diag_done st_full exp_done mask_done phi_done plo_done pv_full recip_done ctx_done
                ctx_part ctx_split x_loaded gated x1_done x1_stored bn_done2 agg_done var_done2 rstd_done2 xhat_done2
                h32_done2 hhi_done2 hlo_done2 log_done""".split()
            (pair_full, pair_free, rope_mul, rope_sum, rope_hi, rope_lo, q_stacked, k_stacked, v_ready, v_hi_done, v_lo_done,
             s_full, max_done, diag_done, st_full, exp_done, mask_done, phi_done, plo_done, pv_full, recip_done, ctx_done,
             ctx_part, ctx_split, x_loaded, gated, x1_done, x1_stored, bn_done, agg_done, var_done, rstd_done, xhat_done,
             h32_done, hhi_done, hlo_done, log_done) = (sem(st, n) for n in names)
            rows_out = (sem(st, "q_rows_out"), sem(st, "k_rows_out"))

            Q, K, V = 0, 1, 2
            AHEAD = 5
            STACK = 4 * 16
            pair = (bank[6], bank[7])
            ahead_banks = (pair, bank[0:2], bank[2:4], bank[4:6], pair)
            last_banks = (bank[6], bank[7], bank[2], bank[3])

            def ready(eng, s, n):
                if not isinstance(n, int) or n > 0:
                    eng.wait_ge(s, n)

            def turn(b, h):
                if isinstance(b, int) and b == 0:
                    return AHEAD + h - h // HG
                skipped = 2 if isinstance(b, int) and b == B - 1 and h > 10 else 0
                if isinstance(b, int) and b == B:
                    skipped = 5
                return AHEAD + 12 + 15 * (b - 1) + h - skipped

            def rope_no(b, n, what):
                return 2 * (G * b + n) + what

            def value_part(v, par, half, eo):
                tiles = v[:, par, 2 * HG * half:2 * HG * (half + 1), :].rearrange("p (j two) n -> p j two n", two=2)
                return tiles[:, :, eo, eo * D:(eo + 1) * D]

            def value_source(banks, half, eo):
                return banks[half][:].rearrange("p (j two n) -> p j two n", two=2, n=D)[:, :, eo, :]

            with nc.Block() as block:
                @block.sync
                def _(sp):
                    x_v = x.rearrange("(n p) c -> p n c", p=P)
                    x1_v = x1_dram.rearrange("(n p) c -> p n c", p=P)

                    def stack(b, n, what):
                        there = rows_dram[what].rearrange("h p l t -> p h l t")
                        sp.wait_ge(rope_lo, rope_no(b, n, what) + 1)
                        sp.dma_start(there, qk_split[:, what]).then_inc(rows_out[what], 16)
                        sp.wait_ge(rows_out[what], 16 * (G * b + n) + 16)
                        ready(sp, st_full, 3 * (H * b + HG * (n - 1)))
                        for quad in range(4):
                            half = rows_dram[what, quad % 2].rearrange("(i d) l t -> d i l t", i=HG)
                            to = slice(32 * quad, 32 * quad + 32)
                            if what == Q:
                                sp.dma_start(q_stack[to, n % 2], half).then_inc(q_stacked, 16)
                            else:
                                sp.dma_start(k_stack[to, n % 2], half[:, :, quad // 2]).then_inc(k_stacked, 16)

                    def batch(b, first, last=False):
                        stack(b, 1, K)
                        stack(b, 2, Q)
                        stack(b, 2, K)
                        stack(b, 3, Q)
                        stack(b, 3, K)
                        if last:
                            sp.wait_ge(pair_full, turn(b, 8) + 1)
                            load_expert(sp, 0)
                        if not first:
                            sp.wait_ge(x1_done, 2 * b)
                            sp.dma_start(x1_v[:, bass.ds((b - 1) * TT, TT), :], x1_t[:]).then_inc(x1_stored, 16)
                        if not last:
                            stack(b, 4, Q)
                        if not first:
                            sp.wait_ge(x1_stored, 16 * b)
                            sp.wait_ge(xhat_done, b)
                        sp.dma_start(x1_t[:], x_v[:, bass.ds(b * TT, TT), :]).then_inc(x_loaded, 16)
                        if not last:
                            stack(b, 4, K)
                            stack(b, 5, Q)

                    stack(0, 0, Q)
                    stack(0, 0, K)
                    stack(0, 1, Q)
                    batch(0, True)
                    with sp.Fori(1, B - 1) as b:
                        batch(b, False)
                    batch(B - 1, False, True)
                    sp.wait_ge(x1_done, 2 * B)
                    sp.dma_start(x1_v[:, (B - 1) * TT:B * TT, :], x1_t[:]).then_inc(x1_stored, 16)
                    sp.wait_ge(x1_stored, 16 * B)

                @block.tensor
                def _(pe):
                    def proj(b, n, what, banks, free):
                        ready(pe, pair_free, free)
                        b, g = (b + 1, n - G) if n >= G else (b, n)
                        if what in (Q, K):
                            for half in range(2):
                                for k in range(KC):
                                    h = (flat(hT_hi[:, bass.ds(b, 1), k, :]), flat(hT_lo[:, bass.ds(b, 1), k, :]))
                                    cols = slice((2 * what + half) * P, (2 * what + half + 1) * P)
                                    w = (wqkv_hi[:, k, g, cols], wqkv_lo[:, k, g, cols])
                                    last = three_passes(nc, banks[half][:], w, h, k == 0, k == KC - 1)
                        else:
                            for tt in range(TT):
                                for k in range(KC):
                                    rows = slice(tt * P, (tt + 1) * P)
                                    h = (flat(hT_hi[:, bass.ds(b, 1), k, rows]), flat(hT_lo[:, bass.ds(b, 1), k, rows]))
                                    w = (wqkv_hi[:, k, g, 4 * P:], wqkv_lo[:, k, g, 4 * P:])
                                    last = three_passes(nc, banks[tt // 2][:, (tt % 2) * C:(tt % 2 + 1) * C], h, w,
                                                        k == 0, k == KC - 1)
                        last.then_inc(pair_full, 1)

                    def scores_qk(b, h, qt):
                        par, i = (h // HG) % 2, h % HG
                        if i == 0 and qt == 0:
                            pe.wait_ge(q_stacked, STACK * (G * b + h // HG + 1))
                            pe.wait_ge(k_stacked, STACK * (G * b + h // HG + 1))
                        ready(pe, max_done, TT * (H * b + h) + qt - 1)
                        nc.tensor.matmul(bank[qt % 2][:, 0:(qt + 1) * P], q_stack[:, par, i, 0, qt * P:(qt + 1) * P],
                                         k_stack[:, par, i, 0:(qt + 1) * P], start=True, stop=False)
                        nc.tensor.matmul(bank[qt % 2][:, qt * P:(qt + 1) * P], ident_unit[:], max_mask[:],
                                         start=False, stop=True).then_inc(s_full, 1)

                    def scores_kq(b, h, kt):
                        par, i = (h // HG) % 2, h % HG
                        hh = H * b + h
                        at = 2 * P if kt == 3 else 0
                        to = bank[2 + min(kt, 2)][:, at:at + S - kt * P]
                        rows = slice(kt * P, (kt + 1) * P)
                        if kt < 3:
                            ready(pe, exp_done, 3 * (hh - 1) + kt + 1)
                        if kt == 0:
                            pe.wait_ge(diag_done, hh + 1)
                        nc.tensor.matmul(to, k_stack[:, par, i, rows], q_stack[:, par, i, 0, kt * P:], start=True, stop=False)
                        nc.tensor.matmul(to, k_stack[:, par, i, rows], q_stack[:, par, i, 1, kt * P:], start=False, stop=False)
                        last = nc.tensor.matmul(to, ones15[:], neg_max[:, h % 2, kt * P:], start=False, stop=True)
                        if kt != 2:
                            last.then_inc(st_full, 1)

                    def context(b, h):
                        par, i = (h // HG) % 2, h % HG
                        hh = H * b + h
                        pe.wait_ge(plo_done, hh + 1)
                        if i == 0:
                            pe.wait_ge(v_lo_done, G * b + h // HG + 1)
                        ready(pe, ctx_done, hh)
                        for kt in range(TT):
                            cols = slice(WOFF[kt], WOFF[kt] + S - kt * P)
                            v = (v_hi[:, par, kt * HG + i, :], v_lo[:, par, kt * HG + i, :])
                            last = three_passes(nc, bank[5][:, kt * P:], v, (p_hi[:, h % 2, cols], p_lo[:, h % 2, cols]),
                                                kt == 0, kt == TT - 1)
                        last.then_inc(pv_full, 1)

                    def output(b, half, t):
                        pe.wait_ge(pair_free, t)
                        if half == 0:
                            pe.wait_ge(ctx_split, CC * b + CC)
                        for tt in (2 * half, 2 * half + 1):
                            for c in range(CC):
                                rows = slice(tt * P, (tt + 1) * P)
                                c_part = (flat(ctx_hi[:, bass.ds(b % 2, 1), c, rows]), flat(ctx_lo[:, bass.ds(b % 2, 1), c, rows]))
                                last = three_passes(nc, pair[half][:, (tt % 2) * C:(tt % 2 + 1) * C], c_part,
                                                    (wo_hi[:, c, :], wo_lo[:, c, :]), c == 0, c == CC - 1)
                        last.then_inc(pair_full, 1)

                    def transposes(b, t):
                        pe.wait_ge(xhat_done, b + 1)
                        pe.wait_ge(pair_free, t)
                        for k in range(KC):
                            for tt in range(TT):
                                last = nc.tensor.transpose(pair[k][:, tt * P:(tt + 1) * P], xhat[:, tt, k * P:(k + 1) * P], ident32[:])
                        last.then_inc(pair_full, 1)

                    def batch(b, first, last=False):
                        for h in range(H):
                            g = h // HG
                            more = not last or h + 1 < H
                            if more:
                                scores_qk(b, h + 1, 0)
                                scores_qk(b, h + 1, 1)
                            if not first or h >= 2:
                                context(b, h - 2)
                            for kt in range(TT):
                                scores_kq(b, h, kt)
                            if more:
                                scores_qk(b, h + 1, 2)
                                scores_qk(b, h + 1, 3)
                            if h % HG < 3:
                                n, what = ((g + 1, V), (g + 2, Q), (g + 2, K))[h % HG]
                                if not last or n < G:
                                    proj(b, n, what, pair, turn(b, h))
                            elif not first and g < 2:
                                output(b - 1, g, turn(b, h))
                            elif not first and g == 2:
                                transposes(b - 1, turn(b, h))

                    for t, (n, what) in enumerate(((0, Q), (0, K), (0, V), (1, Q), (1, K))):
                        proj(0, n, what, ahead_banks[t], t - 3)
                    pe.wait_ge(pair_free, AHEAD - 1)
                    for qt in range(TT):
                        scores_qk(0, 0, qt)
                    batch(0, True)
                    with pe.Fori(1, B - 1) as b:
                        batch(b, False)
                    batch(B - 1, False, True)
                    def last_output(half, chunks):
                        for tt in (2 * half, 2 * half + 1):
                            for c in chunks:
                                rows = slice(tt * P, (tt + 1) * P)
                                c_part = (ctx_hi[:, (B - 1) % 2, c, rows], ctx_lo[:, (B - 1) % 2, c, rows])
                                last = three_passes(nc, last_banks[tt][:, 0:C], c_part,
                                                    (wo_hi[:, c, :], wo_lo[:, c, :]), c == 0, c == CC - 1)
                        return last

                    pe.wait_ge(pair_free, turn(B, 0))
                    pe.wait_ge(ctx_split, CC * B - 1)
                    context(B, -2)
                    last_output(0, range(CC - 1))
                    context(B, -1)
                    last_output(1, range(CC - 1))
                    pe.wait_ge(ctx_split, CC * B)
                    for half in range(2):
                        last_output(half, (CC - 1,)).then_inc(pair_full, 1)
                    transposes(B - 1, turn(B, 2))

                @block.vector
                def _(dve):
                    def maxima(b, h, tiles):
                        hh = H * b + h
                        for qt in tiles:
                            dve.wait_ge(s_full, TT * hh + qt + 1)
                            nc.vector.tensor_reduce(row_max[:, h % 2, qt:qt + 1], bank[qt % 2][:, 0:(qt + 1) * P], AX.X,
                                                    ALU.max).then_inc(max_done, 1)

                    def release_pair():
                        nc.vector.tensor_copy(spare[:, 0:2], ident16[:, 0:2]).then_inc(pair_free, 1)

                    def rotate(b, n, what, t, banks=pair):
                        r = rope_no(b, n, what)
                        dve.wait_ge(pair_full, t + 1)
                        ready(dve, rope_sum, r)
                        nc.vector.tensor_tensor(rot_part[:, 0, :], banks[0][:], cos_t[:], ALU.mult)
                        nc.vector.tensor_tensor(rot_part[:, 3, :], banks[0][:], sin_t[:], ALU.mult)
                        nc.vector.tensor_tensor(rot_part[:, 1, :], banks[1][:], sin_t[:], ALU.mult)
                        nc.vector.tensor_tensor(rot_part[:, 2, :], banks[1][:], cos_t[:], ALU.mult).then_inc(rope_mul, 1)
                        dve.wait_ge(rope_mul, r + 1)
                        release_pair()

                    def rotated_lo(b, n, what):
                        dve.wait_ge(rope_hi, rope_no(b, n, what) + 1)
                        nc.vector.tensor_tensor(qk_split[:, what, :, 1, :], rot[:], qk_split[:, what, :, 0, :],
                                                ALU.subtract).then_inc(rope_lo, 1)

                    def values_lo(b, n, banks=pair):
                        dve.wait_ge(v_hi_done, G * b + n + 1)
                        for half in range(2):
                            for eo in range(2):
                                to, of = (value_part(v, n % 2, half, eo) for v in (v_lo, v_hi))
                                last = nc.vector.scalar_tensor_tensor(to, value_source(banks, half, eo), V_SHIFT, of, ALU.mult, ALU.subtract)
                        last.then_inc(v_lo_done, 1)
                        dve.wait_ge(v_lo_done, G * b + n + 1)
                        release_pair()

                    def finish_context(b, h):
                        hh = H * b + h
                        mine = slice(0, D) if h % 2 == 0 else slice(D, P)
                        if h % 2 == 0:
                            ready(dve, ctx_split, CC * b + h // 2)
                        dve.wait_ge(recip_done, hh + 1)
                        nc.vector.tensor_tensor(ctx32[mine, :], bank[5][mine, :], recip[mine, :], ALU.mult).then_inc(ctx_done, 1)

                    def split_context(b, h):
                        hh = H * b + h
                        if h % 2 == 1:
                            of, c = (b, h // 2) if h >= 0 else (b - 1, h // 2 + CC)
                            hi, lo = (flat(z[:, bass.ds(of % 2, 1), c, :]) for z in (ctx_hi, ctx_lo))
                            n = CC * b + h // 2 + 1
                            dve.wait_ge(ctx_done, hh + 1)
                            nc.vector.tensor_copy(hi, ctx32[:]).then_inc(ctx_part, 1)
                            dve.wait_ge(ctx_part, n)
                            nc.vector.tensor_tensor(lo, ctx32[:], hi, ALU.subtract).then_inc(ctx_split, 1)

                    def residual(b, half, t, sources):
                        tiles = slice(2 * half, 2 * half + 2)
                        scaled = flat(xhat[:, tiles, :])
                        dve.wait_ge(pair_full, t + 1)
                        if half == 0:
                            dve.wait_ge(x_loaded, 16 * b + 16)
                        for j in range(2):
                            last = nc.vector.tensor_tensor(xhat[:, 2 * half + j, :], sources[j],
                                                           flat(gate_rows[:, bass.ds(b, 1), :]), ALU.mult)
                        last.then_inc(gated, 1)
                        dve.wait_ge(gated, 2 * b + half + 1)
                        nc.vector.tensor_tensor(flat(x1_t[:, tiles, :]), scaled, flat(x1_t[:, tiles, :]), ALU.add).then_inc(x1_done, 1)
                        release_pair()
                        dve.wait_ge(x1_done, 2 * b + half + 1)
                        for tt in (2 * half, 2 * half + 1):
                            last = nc.vector.bn_stats(stats[:, tt, :], x1_t[:, tt, :])
                        last.then_inc(bn_done, 1)

                    def statistics(b):
                        dve.wait_ge(v_ready, 2)
                        dve.wait_ge(bn_done, 2 * b + 2)
                        for tt in range(TT):
                            last = nc.vector.bn_aggr(mean_var[:, tt, :], stats[:, tt, :])
                        last.then_inc(agg_done, 1)
                        dve.wait_ge(agg_done, b + 1)
                        nc.vector.tensor_scalar(var_eps[:, 0:TT], mean_var[:, 0:TT, 1], EPS, None, ALU.add).then_inc(var_done, 1)

                    def normalise(b):
                        dve.wait_ge(rstd_done, b + 1)
                        for tt in range(TT):
                            last = nc.vector.tensor_scalar(xhat[:, tt, :], x1_t[:, tt, :], mean_var[:, tt, 0:1], rstd[:, tt:tt + 1],
                                                           ALU.subtract, ALU.mult)
                        last.then_inc(xhat_done, 1)

                    def modulate(b, t, rotations):
                        dve.wait_ge(pair_full, t + 1)
                        dve.wait_ge(rope_sum, rotations)
                        for k in range(KC):
                            normalise_chunk(nc, dve, norm_tiles, pair[k][:], 1, b, k, b * KC + k, h32_done, hhi_done, hlo_done)
                        release_pair()

                    def scale_expert(i):
                        if i:
                            dve.wait_ge(amax_reduced, i)
                        for piece in range(4):
                            amax_piece(i, piece)
                        find_bound(dve, i)
                        guard_bound(dve, i)
                        find_pow2(dve, 0, i, i)
                        invert_pow2(dve, 0, i, i)
                        find_alpha(dve, 0, i, i)

                    def weights_lo(i):
                        dve.wait_ge(w_hi_done, i + 1)
                        nc.vector.scalar_tensor_tensor(w_even[:, 1, i, :], w_f[:, i, :], w_alpha[:, i:i + 1], w_even[:, 0, i, :],
                                                       ALU.mult, ALU.subtract).then_inc(w_split, 1)

                    def batch(b, first, last=False):
                        for h in range(H):
                            g = h // HG
                            more = not last or h + 1 < H
                            if more:
                                maxima(b, h + 1, (0, 1))
                            if h % HG == 0:
                                if not first and g in (1, 2):
                                    residual(b - 1, g - 1, turn(b, h - 1), (pair[g - 1][:, 0:C], pair[g - 1][:, C:]))
                                if not first and g == 3:
                                    modulate(b - 1, turn(b, h - 1), rope_no(b, g if last else g + 1, K) + 1)
                            elif h % HG == 1:
                                if not last or g + 1 < G:
                                    values_lo(b, g + 1)
                            elif last and g + 2 >= G:
                                pass
                            elif h % HG == 2:
                                rotate(b, g + 2, Q, turn(b, h - 1))
                            else:
                                rotate(b, g + 2, K, turn(b, h - 1))
                                rotated_lo(b, g + 2, Q)
                            if not first or h >= 2:
                                finish_context(b, h - 2)
                            if more:
                                maxima(b, h + 1, (2, 3))
                            if not first or h >= 2:
                                split_context(b, h - 2)
                            if not first and h == 9:
                                statistics(b - 1)
                            if not first and h == 10:
                                normalise(b - 1)
                            if last and h == H - 4:
                                nc.vector.memset(w_step[:, 0:2], W_SCALE).then_inc(const_done, 1)
                                nc.vector.memset(w_step[:, 2:3], O_SCALE).then_inc(const_done, 1)
                                nc.vector.memset(w_pow2[:, 1, :], 0.0).then_inc(w_scaled, 3)
                                dve.wait_ge(const_done, 2)
                                dve.wait_ge(w_in, 48)
                            if last and h >= H - 3:
                                scale_expert(h - (H - 3))
                            if last and h == H - 1:
                                derive_first(dve, 0, 3)
                                derive_second(dve, 0, 0)

                    def rotate_sum(n, what):
                        ready(dve, rope_lo, rope_no(0, n, what))
                        nc.vector.tensor_tensor(rot[:, 0, :], rot_part[:, 0, :], rot_part[:, 1, :], ALU.subtract)
                        nc.vector.tensor_tensor(rot[:, 1, :], rot_part[:, 2, :], rot_part[:, 3, :], ALU.add).then_inc(rope_sum, 1)

                    rotate(0, 0, Q, 0, ahead_banks[0])
                    rotate_sum(0, Q)
                    rotate(0, 0, K, 1, ahead_banks[1])
                    rotated_lo(0, 0, Q)
                    rotate_sum(0, K)
                    dve.wait_ge(v_ready, 2)
                    values_lo(0, 0, ahead_banks[2])
                    rotated_lo(0, 0, K)
                    rotate(0, 1, Q, 3, ahead_banks[3])
                    rotate_sum(1, Q)
                    rotate(0, 1, K, 4, ahead_banks[4])
                    rotated_lo(0, 1, Q)
                    rotate_sum(1, K)
                    maxima(0, 0, range(TT))
                    batch(0, True)
                    with dve.Fori(1, B - 1) as b:
                        batch(b, False)
                    batch(B - 1, False, True)
                    finish_context(B, -2)
                    finish_context(B, -1)
                    split_context(B, -1)
                    for half in range(2):
                        residual(B - 1, half, turn(B, half), [z[:, 0:C] for z in last_banks[2 * half:2 * half + 2]])
                    statistics(B - 1)
                    weights_lo(0)
                    normalise(B - 1)
                    weights_lo(1)
                    weights_lo(2)
                    modulate(B - 1, turn(B, 2), rope_no(B - 1, G - 1, K) + 1)

                @block.scalar
                def _(act):
                    def exponents(b, h):
                        hh = H * b + h
                        ready(act, plo_done, hh - 1)
                        for j, (bk, w, to) in enumerate(((2, 512, 0), (3, 384, 512), (4, 384, 896))):
                            act.wait_ge(st_full, 3 * hh + j + 1)
                            nc.scalar.activation(p32[:, h % 2, to:to + w], bank[bk][:, 0:w], ACT.Exp,
                                                 scale=logit_scale[:]).then_inc(exp_done, 1)

                    def diagonals(b, h):
                        hh = H * b + h
                        act.wait_ge(max_done, TT * hh + TT)
                        for qt in range(TT):
                            last = nc.scalar.activation(neg_max[:, h % 2, qt * P:(qt + 1) * P], neg_ident[:], ACT.Copy,
                                                        scale=row_max[:, h % 2, qt:qt + 1])
                        last.then_inc(diag_done, 1)

                    def probs_hi(b, h):
                        hh = H * b + h
                        act.wait_ge(mask_done, hh + 1)
                        ready(act, pv_full, hh - 1)
                        nc.scalar.activation(p_hi[:, h % 2, :], p32[:, h % 2, :], ACT.Copy).then_inc(phi_done, 1)

                    def reciprocals(b, h):
                        hh = H * b + h
                        mine, sums = (slice(0, D), slice(D, P)) if h % 2 == 0 else (slice(D, P), slice(0, D))
                        act.wait_ge(pv_full, hh + 1)
                        ready(act, ctx_done, hh - 1)
                        nc.scalar.activation(recip[mine, :], bank[5][sums, :], ACT.Ln).then_inc(log_done, 1)
                        act.wait_ge(log_done, hh + 1)
                        nc.scalar.activation(recip[mine, :], recip[mine, :], ACT.Exp, scale=-1.0).then_inc(recip_done, 1)

                    def rotated_hi(b, n, what):
                        act.wait_ge(rope_sum, rope_no(b, n, what) + 1)
                        ready(act, q_stacked if what == Q else k_stacked, STACK * (G * b + n))
                        nc.scalar.activation(qk_split[:, what, :, 0, :], rot[:], ACT.Copy).then_inc(rope_hi, 1)

                    def values_hi(b, n, t, banks=pair):
                        act.wait_ge(pair_full, t + 1)
                        ready(act, pv_full, H * b + HG * (n - 1))
                        for half in range(2):
                            for eo in range(2):
                                last = nc.scalar.activation(value_part(v_hi, n % 2, half, eo), value_source(banks, half, eo), ACT.Copy,
                                                            scale=V_SHIFT)
                        last.then_inc(v_hi_done, 1)

                    def batch(b, first, last=False):
                        for h in range(H):
                            g = h // HG
                            if h % HG == 1 and (not last or g + 1 < G):
                                values_hi(b, g + 1, turn(b, h - 1))
                            if not first or h >= 1:
                                probs_hi(b, h - 1)
                            if not first or h >= 2:
                                reciprocals(b, h - 2)
                            exponents(b, h)
                            if not last or h + 1 < H:
                                diagonals(b, h + 1)
                            if last and g + 2 >= G:
                                pass
                            elif h % HG == 2:
                                rotated_hi(b, g + 2, Q)
                            elif h % HG == 3:
                                rotated_hi(b, g + 2, K)

                    nc.scalar.add_instruction(mybir.InstLoadActFuncSet(name=nc.get_next_instruction_name(), act_func_set_id=LOG_EXP_SET,
                                                                       engine=mybir.EngineType.Activation))
                    rotated_hi(0, 0, Q)
                    rotated_hi(0, 0, K)
                    act.wait_ge(v_ready, 2)
                    values_hi(0, 0, 2, ahead_banks[2])
                    rotated_hi(0, 1, Q)
                    rotated_hi(0, 1, K)
                    diagonals(0, 0)
                    batch(0, True)
                    with act.Fori(1, B - 1) as b:
                        batch(b, False)
                    batch(B - 1, False, True)
                    probs_hi(B, -1)
                    reciprocals(B, -2)
                    reciprocals(B, -1)
                    act.wait_ge(st_full, 3 * H * B)
                    act.wait_ge(s_full, TT * H * B)
                    act.wait_ge(q_stacked, STACK * G * B)
                    act.wait_ge(k_stacked, STACK * G * B)
                    for i in range(3):
                        act.wait_ge(alpha_done, i + 1)
                        nc.scalar.activation(w_even[:, 0, i, :], w_f[:, i, :], ACT.Copy, scale=w_alpha[:, i:i + 1]).then_inc(w_hi_done, 1)

                @block.gpsimd
                def _(pool):
                    def mask(b, h):
                        hh = H * b + h
                        pool.wait_ge(exp_done, 3 * hh + 3)
                        nc.gpsimd.tensor_tensor(spare[:, 2:4], ident16[:, 0:2], ident16[:, 0:2], ALU.add)
                        for kt in range(TT):
                            part = p32[:, h % 2, WOFF[kt]:WOFF[kt] + P]
                            last = nc.gpsimd.affine_select(out=part, in_=part, pattern=[[1, P]], compare_op=ALU.is_ge, fill=0.0,
                                                           base=0, channel_multiplier=-1)
                        last.then_inc(mask_done, 1)

                    def probs_lo(b, h):
                        hh = H * b + h
                        pool.wait_ge(phi_done, hh + 1)
                        nc.gpsimd.tensor_tensor(p_lo[:, h % 2, :], p32[:, h % 2, :], p_hi[:, h % 2, :], ALU.subtract).then_inc(plo_done, 1)

                    def rotate_sum(b, n, what):
                        r = rope_no(b, n, what)
                        pool.wait_ge(rope_mul, r + 1)
                        ready(pool, rope_lo, r)
                        nc.gpsimd.tensor_tensor(rot[:, 0, :], rot_part[:, 0, :], rot_part[:, 1, :], ALU.subtract)
                        nc.gpsimd.tensor_tensor(rot[:, 1, :], rot_part[:, 2, :], rot_part[:, 3, :], ALU.add).then_inc(rope_sum, 1)

                    def rotated_lo(b, n, what):
                        pool.wait_ge(rope_hi, rope_no(b, n, what) + 1)
                        nc.gpsimd.tensor_tensor(qk_split[:, what, :, 1, :], rot[:], qk_split[:, what, :, 0, :],
                                                ALU.subtract).then_inc(rope_lo, 1)

                    def batch(b, first, last=False):
                        for h in range(H):
                            g = h // HG
                            if not first or h >= 1:
                                probs_lo(b, h - 1)
                            if h % HG == 0 and (not last or g + 1 < G):
                                rotated_lo(b, g + 1, K)
                            if last and g + 2 >= G:
                                pass
                            elif h % HG == 2:
                                rotate_sum(b, g + 2, Q)
                            elif h % HG == 3:
                                rotate_sum(b, g + 2, K)
                            mask(b, h)
                            if last and h >= H - 3:
                                reduce_amax(pool, h - (H - 3), spare32[:])
                            if not first and h == 9:
                                pool.wait_ge(var_done, b)
                                nc.gpsimd.tensor_tensor(rstd[:, 0:TT], var_eps[:, 0:TT], neg_half[:, 0:TT], ALU.pow).then_inc(rstd_done, 1)

                    nc.gpsimd.memset(v_hi[:], 1.0).then_inc(v_ready, 1)
                    nc.gpsimd.memset(v_lo[:], 0.0).then_inc(v_ready, 1)
                    batch(0, True)
                    with pool.Fori(1, B - 1) as b:
                        batch(b, False)
                    batch(B - 1, False, True)
                    probs_lo(B, -1)
                    pool.wait_ge(var_done, B)
                    nc.gpsimd.tensor_tensor(rstd[:, 0:TT], var_eps[:, 0:TT], neg_half[:, 0:TT], ALU.pow).then_inc(rstd_done, 1)

        attn.close()

        with ExitStack() as st:
            acc = sb(st, "acc", [P, KC, B, S])
            w_odd = sb(st, "w_odd", [P, 2, 3, MC], F16)
            w_hi = (w_even[:, 0], w_odd[:, 0])
            w_lo = (w_even[:, 1], w_odd[:, 1])
            silu_t = sb(st, "silu_t", [P, 2, S])
            mid32 = sb(st, "mid32", [P, 2, S])
            mid_hi = sb(st, "mid_hi", [P, 2, S], F16)
            mid_lo = sb(st, "mid_lo", [P, 2, S], F16)
            spare = sb(st, "spare_e", [P, 2])
            yT = sb(st, "yT", [P, 2, KC, S])
            x1_all = sb(st, "x1_all", [P, B * TT, C])

            names = """acc_zero g_full u_full silu_done mid_done mhi_done mlo_done y_full y_free yT_done tr_full res_done
                x1_in stored""".split()
            (acc_zero, g_full, u_full, silu_done, mid_done, mhi_done, mlo_done, y_full, y_free, yT_done, tr_full, res_done,
             x1_in, stored) = (sem(st, "e_" + n) for n in names)

            g_bank, u_bank, y_bank = bank[0:2], bank[2:4], (bank[4:6], bank[6:8])

            def chunk_no(e, t, j):
                return (e * B + t) * FC + j

            with nc.Block() as block:
                @block.sync
                def _(sp):
                    x1_v = x1_dram.rearrange("(n p) c -> p n c", p=P)
                    out_v = out.rearrange("(n p) c -> p n c", p=P)

                    load_expert(sp, 1)
                    sp.dma_start(x1_all[:], x1_v).then_inc(x1_in, 16)
                    with sp.Fori(0, E // 2) as ep:
                        for p in range(2):
                            sp.wait_ge(w_split, (2 * ep + p) * 3 + 6)
                            load_expert(sp, (2 * ep + p + 2) % E)
                    sp.wait_ge(w_in, 48 * (E + 2))
                    with sp.Fori(0, B) as t:
                        sp.wait_ge(res_done, t + 3)
                        sp.dma_start(out_v[:, bass.ds(t * TT, TT), :], x1_all[:, bass.ds(t * TT, TT), :]).then_inc(stored, 16)
                    sp.wait_ge(stored, 16 * B)

                @block.tensor
                def _(pe):
                    def tokens(t, k):
                        return flat(hT_hi[:, bass.ds(t, 1), k, :]), flat(hT_lo[:, bass.ds(t, 1), k, :])

                    def up(p, e, t, j):
                        n = chunk_no(e, t, j)
                        for i, (bk, free, full) in enumerate(((g_bank, silu_done, g_full), (u_bank, mid_done, u_full))):
                            pe.wait_ge(free, n + 1)
                            for k in range(KC):
                                cols = slice(k * F + j * P, k * F + (j + 1) * P)
                                last = three_passes(nc, bk[j % 2][:], (w_hi[p][:, i, cols], w_lo[p][:, i, cols]), tokens(t, k),
                                                    k == 0, k == KC - 1)
                            last.then_inc(full, 1)

                    def down(p, e, t, a, j):
                        if j == 0:
                            pe.wait_ge(y_free, e * B + t + 1)
                        pe.wait_ge(mlo_done, chunk_no(e, t, j) + 1)
                        for o in range(KC):
                            cols = slice(j * C + o * P, j * C + (o + 1) * P)
                            last = three_passes(nc, y_bank[a][o][:], (w_hi[p][:, 2, cols], w_lo[p][:, 2, cols]),
                                                (mid_hi[:, j % 2], mid_lo[:, j % 2]), j == 0, j == FC - 1)
                        if j == FC - 1:
                            last.then_inc(y_full, 1)

                    def tile(p, e, t, a, more):
                        for j in range(1, FC):
                            up(p, e, t, j)
                            down(p, e, t, a, j - 1)
                        if more:
                            up(p, e, t + 1, 0)
                        down(p, e, t, a, FC - 1)

                    with pe.Fori(0, E // 2) as ep:
                        for p in range(2):
                            e = 2 * ep + p
                            pe.wait_ge(w_split, 3 * e + 3)
                            up(p, e, 0, 0)
                            with pe.Fori(0, B // 2 - 1) as tp:
                                for a in range(2):
                                    tile(p, e, 2 * tp + a, a, True)
                            tile(p, e, B - 2, 0, True)
                            tile(p, e, B - 1, 1, False)
                    with pe.Fori(0, B // 2) as tp:
                        for a in range(2):
                            pe.wait_ge(yT_done, 2 * tp + a + 1)
                            pe.wait_ge(res_done, 2 * tp + a + 1)
                            for tt in range(TT):
                                for o in range(KC):
                                    at = (tt % 2) * C + o * P
                                    last = nc.tensor.transpose(bank[2 * a + tt // 2][:, at:at + P],
                                                               yT[:, a, o, tt * P:(tt + 1) * P], ident32[:])
                            last.then_inc(tr_full, 1)

                @block.scalar
                def _(act):
                    def gates(p, n, j):
                        act.wait_ge(g_full, n + 1)
                        nc.scalar.activation(silu_t[:, j % 2], g_bank[j % 2][:], ACT.Silu, scale=g_unscale[:, p:p + 1]).then_inc(silu_done, 1)

                    nc.scalar.preload_act_table(ACT.Silu)
                    nc.scalar.activation(silu_t[:, 0, 0:2], neg_half[:, 0:2], ACT.Copy).then_inc(silu_done, 2)
                    with act.Fori(0, E // 2) as ep:
                        for p in range(2):
                            e = 2 * ep + p
                            act.wait_ge(scal_done, e + 1)
                            with act.Fori(0, B) as t:
                                for j in range(FC):
                                    gates(p, chunk_no(e, t, j), j)
                    with act.Fori(0, B // 2) as tp:
                        for a in range(2):
                            t = 2 * tp + a
                            act.wait_ge(y_free, (E - 1) * B + t + 3)
                            act.wait_ge(tr_full, t + 1)
                            for o in range(KC):
                                last = nc.scalar.activation(yT[:, a, o, :], flat(acc[:, o, bass.ds(t, 1), :]), ACT.Copy,
                                                            scale=gate[:, 1, o, bass.ds(t, 1)])
                            last.then_inc(yT_done, 1)

                @block.vector
                def _(dve):
                    def middle(p, n, j):
                        dve.wait_ge(u_full, n + 1)
                        dve.wait_ge(silu_done, n + 3)
                        nc.vector.scalar_tensor_tensor(mid32[:, j % 2], u_bank[j % 2][:], mid_scale[:, p:p + 1], silu_t[:, j % 2],
                                                       ALU.mult, ALU.mult).then_inc(mid_done, 1)
                        dve.wait_ge(mid_done, n + 3)
                        nc.vector.tensor_copy(mid_hi[:, j % 2], mid32[:, j % 2]).then_inc(mhi_done, 1)
                        dve.wait_ge(mhi_done, n + 1)
                        nc.vector.tensor_tensor(mid_lo[:, j % 2], mid32[:, j % 2], mid_hi[:, j % 2], ALU.subtract).then_inc(mlo_done, 1)

                    def collect(p, e, t, a):
                        dve.wait_ge(acc_zero, 1)
                        dve.wait_ge(y_full, e * B + t + 1)
                        for o in range(KC):
                            part = flat(acc[:, o, bass.ds(t, 1), :])
                            last = nc.vector.scalar_tensor_tensor(part, y_bank[a][o][:], down_unscale[:, p:p + 1], part, ALU.mult, ALU.add)
                        last.then_inc(y_free, 1)

                    def tile(p, e, t, a, more, between):
                        for j in range(1, FC):
                            middle(p, chunk_no(e, t, j), j)
                            between(j)
                        if more:
                            middle(p, chunk_no(e, t + 1, 0), 0)
                        collect(p, e, t, a)

                    nc.vector.memset(mid32[:], 0.0).then_inc(mid_done, 2)
                    nc.vector.memset(yT[:, 0, 0, 0:2], 0.0).then_inc(tr_full, 2)
                    nc.vector.memset(yT[:, 1, 0, 0:2], 0.0).then_inc(res_done, 2)
                    nc.vector.memset(mid_lo[:], 0.0).then_inc(y_free, 2)
                    with dve.Fori(0, E // 2) as ep:
                        for p in range(2):
                            e = 2 * ep + p
                            middle(p, chunk_no(e, 0, 0), 0)
                            with dve.Fori(0, B // 2 - 1) as tp:
                                n = 3 * e + 3 + tp

                                def even(j):
                                    if j == 1:
                                        dve.wait_ge(w_in, 48 * (e + 2))
                                    if 2 <= j < 6:
                                        amax_piece(tp, j - 2)

                                def odd(j):
                                    if j == 1:
                                        find_bound(dve, n)
                                    if j == 2:
                                        guard_bound(dve, n)
                                    if j == 3:
                                        find_pow2(dve, 1 - p, tp, n)
                                    if j == 4:
                                        invert_pow2(dve, 1 - p, tp, n)
                                    if j == 5:
                                        dve.wait_ge(w_scaled, n)
                                        find_alpha(dve, 1 - p, tp, n)

                                tile(p, e, 2 * tp, 0, True, even)
                                tile(p, e, 2 * tp + 1, 1, True, odd)

                            def derive(j):
                                if j == 1:
                                    derive_first(dve, 1 - p, 3 * e + 6)
                                if j == 2:
                                    derive_second(dve, 1 - p, e + 1)

                            tile(p, e, B - 2, 0, True, derive)
                            tile(p, e, B - 1, 1, False, lambda j: None)
                    dve.wait_ge(x1_in, 16)
                    with dve.Fori(0, B // 2) as tp:
                        for a in range(2):
                            dve.wait_ge(tr_full, 2 * tp + a + 3)
                            for half in range(2):
                                part = flat(x1_all[:, bass.ds((2 * tp + a) * TT + 2 * half, 2), :])
                                last = nc.vector.tensor_tensor(part, bank[2 * a + half][:], part, ALU.add)
                            last.then_inc(res_done, 1)

                @block.gpsimd
                def _(pool):
                    def split(p, i, n):
                        reduce_amax(pool, n, spare[:])
                        pool.wait_ge(w_in, 48)
                        pool.wait_ge(alpha_done, n + 1)
                        w, hi = w_f[:, i, :], w_hi[p][:, i, :]
                        nc.gpsimd.tensor_scalar(hi, w, w_alpha[:, i:i + 1], 1.0, ALU.mult, ALU.mult).then_inc(w_hi_done, 1)
                        pool.wait_ge(w_in, 48)
                        pool.wait_ge(w_hi_done, n + 1)
                        nc.gpsimd.tensor_scalar(w, w, w_alpha[:, i:i + 1], 1.0, ALU.mult, ALU.mult).then_inc(w_scaled, 1)
                        pool.wait_ge(w_scaled, n + 1)
                        nc.gpsimd.tensor_tensor(w_lo[p][:, i, :], w, hi, ALU.subtract).then_inc(w_split, 1)

                    nc.gpsimd.memset(acc[:], 0.0).then_inc(acc_zero, 1)
                    with pool.Fori(0, E // 2) as ep:
                        for p in range(2):
                            for i in range(3):
                                split(1 - p, i, 3 * (2 * ep + p) + 3 + i)


def rotary_tables():
    import numpy as np

    half = D // 2
    fraction = np.float32(2.0) * np.arange(half, dtype=np.float32) / np.float32(D)
    timescale = np.float32(1.0) * np.power(np.float32(10000.0), fraction, dtype=np.float32)
    angle = np.arange(S, dtype=np.float32)[None, :] / timescale[:, None]
    return [np.ascontiguousarray(np.tile(f(angle).astype(np.float32) * np.float32(QK_SHIFT), (HG, 1))) for f in (np.cos, np.sin)]


def kernel(L0_attn_x, L0_attn_wqkv, L0_attn_wo, L0_ffn_Wg, L0_ffn_Wu, L0_ffn_Wd, L0_c, L0_wmod):
    import numpy as np
    import concourse.bacc as bacc
    from concourse.bass_utils import run_bass_kernel_spmd

    w = np.asarray(L0_attn_wqkv).reshape(KC, P, 3, G, HG, 2, D // 2)
    qk = w[:, :, 0:2].transpose(1, 0, 3, 2, 5, 4, 6).reshape(P, KC, G, 4 * P)
    v = w[:, :, 2].transpose(1, 0, 2, 3, 4, 5).reshape(P, KC, G, 2 * P)
    cos_t, sin_t = rotary_tables()
    arrays = {
        "x": np.ascontiguousarray(np.asarray(L0_attn_x).reshape(B * S, C)),
        "wqkv": np.ascontiguousarray(np.concatenate([qk, v], axis=3).reshape(P, KC * G * 6 * P)),
        "wo": np.ascontiguousarray(L0_attn_wo),
        "wg": np.ascontiguousarray(L0_ffn_Wg),
        "wu": np.ascontiguousarray(L0_ffn_Wu),
        "wd": np.ascontiguousarray(L0_ffn_Wd),
        "cT": np.ascontiguousarray(np.asarray(L0_c).T.reshape(KC, P, B).transpose(1, 0, 2)),
        "wmod": np.ascontiguousarray(L0_wmod),
        "cosT": cos_t,
        "sinT": sin_t,
    }
    nc = bacc.Bacc("TRN2", target_bir_lowering=False, num_devices=1)
    args = [nc.dram_tensor(n, a.shape, mybir.dt.from_np(a.dtype), kind="ExternalInput").ap() for n, a in arrays.items()]
    args.append(nc.dram_tensor("out", (B * S, C), F32, kind="ExternalOutput").ap())
    args.append(nc.dram_tensor("x1", (B * S, C), F32, kind="Internal").ap())
    args.append(nc.dram_tensor("rows", (2, 2, P, 2, S), F16, kind="Internal").ap())
    adaln_block_kernel(nc, *args)
    r = run_bass_kernel_spmd(nc, [arrays], core_ids=[0])
    return r.results[0]["out"].reshape(B, S, C)
```
